# Optimizing a Trainium2 kernel written in Bass

```python
import numpy as np
import jax
import jax.numpy as jnp

def _softmax(x, axis=-1):
    return jax.nn.softmax(x, axis=axis)

def _gelu(x):
    return jax.nn.gelu(x, approximate=True)

def _silu(x):
    return jax.nn.silu(x)

def _sigmoid(x):
    return jax.nn.sigmoid(x)

def _layernorm(x, axis=-1, eps=1e-05):
    m = jnp.mean(x, axis=axis, keepdims=True)
    v = jnp.var(x, axis=axis, keepdims=True)
    return (x - m) / jnp.sqrt(v + eps)

def _scatter_add(tgt, idx, src, axis=0):
    return tgt.at[idx].add(src)

def _segment_sum(src, seg, n):
    return jax.ops.segment_sum(src, seg, n)
kernel_name = 'mk_perceiver_d2_seqx_r8_cfc1a9'

def setup_inputs(seed: int=0):
    np.random.seed(seed)
    _w = jnp.asarray

    def _rec_inputs():
        import jax
        import jax.numpy as jnp
        _rk = jax.random.key(seed)
        x = -0.0002928 + 1 * jax.random.normal(jax.random.fold_in(_rk, 1), (2, 128, 256), jnp.float32)
        _lenS = 128 - jax.random.randint(jax.random.fold_in(_rk, 7), (2,), 0, max(1, 128 // 4) + 1, jnp.int32)
        _lenS2 = 2048 - jax.random.randint(jax.random.fold_in(_rk, 8), (2,), 0, max(1, 2048 // 4) + 1, jnp.int32)
        _ctx_2048P = jax.random.normal(jax.random.fold_in(_rk, 11), (2, 16, 256), jnp.float32)
        _ctx_2048c = jax.random.dirichlet(jax.random.fold_in(_rk, 511), 0.3 * jnp.ones((16,), jnp.float32), (2, 2048))
        _ctx_2048t = jnp.einsum('bsk,bkd->bsd', _ctx_2048c, _ctx_2048P)
        _ctx_2048t = _ctx_2048t * jax.lax.rsqrt(jnp.mean(jnp.square(_ctx_2048t)) + 1e-12) * 0.953939
        ctx_2048 = 4.13588e-05 + 0.999923 * (_ctx_2048t + 0.3 * jax.random.normal(jax.random.fold_in(_rk, 611), (2, 2048, 256), jnp.float32))
        _validS = jnp.arange(128)[None, :] < _lenS[:, None]
        _validS2 = jnp.arange(2048)[None, :] < _lenS2[:, None]
        _causal = jnp.tril(jnp.ones((128, 128), dtype=bool))
        mask_1xSxS2_ff0 = jnp.where(jnp.ones((1, 128, 2048), dtype=bool), 0.0, -1000000000.0).astype(jnp.float32)
        return (x, ctx_2048, mask_1xSxS2_ff0)
    x, ctx_2048, mask_1xSxS2_ff0 = _rec_inputs()

    def _L0_xattn_setup():
        import jax, jax.numpy as jnp
        import numpy as np
        H = 256
        NH = 16
        NKV = 4
        HD = 128
        GROUPS = NH // NKV
        EPS = 1e-06
        B, S, SE = (1, 256, 512)

        def _rmsnorm(x, w, eps=EPS):
            xf = x.astype(jnp.float32)
            var = jnp.mean(xf * xf, axis=-1, keepdims=True)
            return (xf * jax.lax.rsqrt(var + eps)).astype(x.dtype) * w
        key = jax.random.key(seed)
        ks = jax.random.split(key, 12)
        sc = 0.02
        return {'hidden_states': jax.random.normal(ks[0], (B, S, H), jnp.float32), 'encoder_hidden_states': jax.random.normal(ks[1], (B, SE, H), jnp.float32), 'attention_mask': jnp.zeros((B, S, SE), jnp.float32), 'Wq': jax.random.normal(ks[2], (H, NH * HD), jnp.float32) * sc, 'bq': jax.random.normal(ks[3], (NH * HD,), jnp.float32) * sc, 'Wk': jax.random.normal(ks[4], (H, NKV * HD), jnp.float32) * sc, 'bk': jax.random.normal(ks[5], (NKV * HD,), jnp.float32) * sc, 'Wv': jax.random.normal(ks[6], (H, NKV * HD), jnp.float32) * sc, 'bv': jax.random.normal(ks[7], (NKV * HD,), jnp.float32) * sc, 'Wo': jax.random.normal(ks[8], (NH * HD, H), jnp.float32) * sc, 'qn_w': jnp.ones((HD,), jnp.float32), 'kn_w': jnp.ones((HD,), jnp.float32)}
    _L0_xattn_all = _L0_xattn_setup()
    _L0_xattn_in = {k: v for k, v in _L0_xattn_all.items() if k in ('Wq', 'bq', 'Wk', 'bk', 'Wv', 'bv', 'Wo', 'qn_w', 'kn_w')}
    del _L0_xattn_all

    def _L0_attn_setup():
        import jax, jax.numpy as jnp
        import numpy as np
        EPS = 1.1920929e-07

        def _rms(x):
            return x * jax.lax.rsqrt(jnp.mean(x * x, axis=-1, keepdims=True) + EPS)
        key = jax.random.key(seed)
        k0, k1, k2, k3 = jax.random.split(key, 4)
        B, S, D, DFF = (4, 256, 256, 1024)
        x = jax.random.normal(k0, (B, S, D), dtype=jnp.float32)
        w_qkv = jax.random.normal(k1, (3 * D, D), dtype=jnp.float32) * 0.02
        w_swiglu = jax.random.normal(k2, (2 * DFF, D), dtype=jnp.float32) * 0.02
        w_out = jax.random.normal(k3, (D, DFF), dtype=jnp.float32) * 0.02
        return {'x': x, 'w_qkv': w_qkv, 'w_swiglu': w_swiglu, 'w_out': w_out}
    _L0_attn_all = _L0_attn_setup()
    _L0_attn_in = {k: v for k, v in _L0_attn_all.items() if k in ('w_qkv', 'w_swiglu', 'w_out')}
    del _L0_attn_all

    def _L0_ffn_setup():
        import jax, jax.numpy as jnp
        import numpy as np
        SEQ, BS, D, F, E = (128, 2, 256, 256, 8)
        key = jax.random.key(seed)
        ks = jax.random.split(key, 8)
        s = 0.02
        return {'hidden_states': jax.random.normal(ks[0], (SEQ, BS, D), jnp.float32), 'router_w': jax.random.normal(ks[1], (D, E), jnp.float32) * s, 'gate_w': jax.random.normal(ks[2], (E, D, F), jnp.float32) * s, 'up_w': jax.random.normal(ks[3], (E, D, F), jnp.float32) * s, 'down_w': jax.random.normal(ks[4], (E, F, D), jnp.float32) * s, 'shared_gate_w': jax.random.normal(ks[5], (D, F), jnp.float32) * s, 'shared_up_w': jax.random.normal(ks[6], (D, F), jnp.float32) * s, 'shared_down_w': jax.random.normal(ks[7], (F, D), jnp.float32) * s}
    _L0_ffn_all = _L0_ffn_setup()
    _L0_ffn_in = {k: v for k, v in _L0_ffn_all.items() if k in ('router_w', 'gate_w', 'up_w', 'down_w', 'shared_gate_w', 'shared_up_w', 'shared_down_w')}
    del _L0_ffn_all

    def _L1_xattn_setup():
        import jax, jax.numpy as jnp
        import numpy as np
        from jax import lax
        LN_EPS = 1e-05
        key = jax.random.key(seed)
        ks = jax.random.split(key, 8)
        B, S, T, D = (4, 128, 256, 256)
        scale = 0.02
        return {'Z': jax.random.normal(ks[0], (B, S, D), dtype=jnp.float32), 'kv': jax.random.normal(ks[1], (B, T, D), dtype=jnp.float32), 'decay': jnp.float32(0.9), 'W_in': jax.random.normal(ks[2], (D, D), dtype=jnp.float32) * scale, 'b_in': jnp.zeros((D,), dtype=jnp.float32), 'W_out': jax.random.normal(ks[3], (D, D), dtype=jnp.float32) * scale, 'b_out': jnp.zeros((D,), dtype=jnp.float32), 'gamma': jnp.ones((D,), dtype=jnp.float32), 'beta': jnp.zeros((D,), dtype=jnp.float32)}
    _L1_xattn_all = _L1_xattn_setup()
    _L1_xattn_in = {k: v for k, v in _L1_xattn_all.items() if k in ('decay', 'W_in', 'b_in', 'W_out', 'b_out', 'gamma', 'beta')}
    del _L1_xattn_all

    def _L1_attn_setup():
        import jax, jax.numpy as jnp
        import numpy as np
        B, T, C = (1, 512, 256)
        H, HK, D = (16, 4, 128)
        W = 128
        THETA = 10000.0

        def sine_table(features, length, max_timescale):
            fraction = jnp.arange(0, features, 2, dtype=jnp.float32) / features
            timescale = max_timescale ** fraction
            ang = jnp.arange(length, dtype=jnp.float32)[:, None] / timescale[None, :]
            ang = jnp.concatenate([ang, ang], axis=-1)
            return (jnp.sin(ang), jnp.cos(ang))

        def rotate_half(x):
            x1, x2 = jnp.split(x, 2, axis=-1)
            return jnp.concatenate([-x2, x1], axis=-1)

        def apply_rope(u, sin, cos):
            return u * cos[None, :, None, :] + rotate_half(u) * sin[None, :, None, :]
        key = jax.random.key(seed)
        ks = jax.random.split(key, 5)
        std = 0.02
        return {'x': jax.random.normal(ks[0], (B, T, C), jnp.float32), 'q_kernel': jax.random.normal(ks[1], (C, H * D), jnp.float32) * std, 'k_kernel': jax.random.normal(ks[2], (C, HK * D), jnp.float32) * std, 'v_kernel': jax.random.normal(ks[3], (C, HK * D), jnp.float32) * std, 'out_kernel': jax.random.normal(ks[4], (H * D, C), jnp.float32) * std}
    _L1_attn_all = _L1_attn_setup()
    _L1_attn_in = {k: v for k, v in _L1_attn_all.items() if k in ('q_kernel', 'k_kernel', 'v_kernel', 'out_kernel')}
    del _L1_attn_all

    def _L1_ffn_setup():
        import jax, jax.numpy as jnp
        import numpy as np
        H = 256
        M = 176
        E = 32
        TOPK = 6
        G = 8
        TOPK_G = 4
        SH = 2
        B, S = (1, 128)
        key = jax.random.key(seed)
        ks = jax.random.split(key, 9)
        sc = 0.02
        return {'x': jax.random.normal(ks[0], (B, S, H), dtype=jnp.float32), 'w_router': jax.random.normal(ks[1], (H, E), dtype=jnp.float32) * sc, 'corr_bias': jax.random.normal(ks[2], (E,), dtype=jnp.float32) * 0.1, 'gate_w': jax.random.normal(ks[3], (E, H, M), dtype=jnp.float32) * sc, 'up_w': jax.random.normal(ks[4], (E, H, M), dtype=jnp.float32) * sc, 'down_w': jax.random.normal(ks[5], (E, M, H), dtype=jnp.float32) * sc, 'sh_gate_w': jax.random.normal(ks[6], (H, M * SH), dtype=jnp.float32) * sc, 'sh_up_w': jax.random.normal(ks[7], (H, M * SH), dtype=jnp.float32) * sc, 'sh_down_w': jax.random.normal(ks[8], (M * SH, H), dtype=jnp.float32) * sc}
    _L1_ffn_all = _L1_ffn_setup()
    _L1_ffn_in = {k: v for k, v in _L1_ffn_all.items() if k in ('w_router', 'corr_bias', 'gate_w', 'up_w', 'down_w', 'sh_gate_w', 'sh_up_w', 'sh_down_w')}
    del _L1_ffn_all
    return {'x': x, 'ctx_2048': ctx_2048, 'mask_1xSxS2_ff0': mask_1xSxS2_ff0, 'L0_xattn_Wq': _L0_xattn_in['Wq'], 'L0_xattn_bq': _L0_xattn_in['bq'], 'L0_xattn_Wk': _L0_xattn_in['Wk'], 'L0_xattn_bk': _L0_xattn_in['bk'], 'L0_xattn_Wv': _L0_xattn_in['Wv'], 'L0_xattn_bv': _L0_xattn_in['bv'], 'L0_xattn_Wo': _L0_xattn_in['Wo'], 'L0_xattn_qn_w': _L0_xattn_in['qn_w'], 'L0_xattn_kn_w': _L0_xattn_in['kn_w'], 'L0_attn_w_qkv': _L0_attn_in['w_qkv'], 'L0_attn_w_swiglu': _L0_attn_in['w_swiglu'], 'L0_attn_w_out': _L0_attn_in['w_out'], 'L0_ffn_router_w': _L0_ffn_in['router_w'], 'L0_ffn_gate_w': _L0_ffn_in['gate_w'], 'L0_ffn_up_w': _L0_ffn_in['up_w'], 'L0_ffn_down_w': _L0_ffn_in['down_w'], 'L0_ffn_shared_gate_w': _L0_ffn_in['shared_gate_w'], 'L0_ffn_shared_up_w': _L0_ffn_in['shared_up_w'], 'L0_ffn_shared_down_w': _L0_ffn_in['shared_down_w'], 'L1_xattn_decay': _L1_xattn_in['decay'], 'L1_xattn_W_in': _L1_xattn_in['W_in'], 'L1_xattn_b_in': _L1_xattn_in['b_in'], 'L1_xattn_W_out': _L1_xattn_in['W_out'], 'L1_xattn_b_out': _L1_xattn_in['b_out'], 'L1_xattn_gamma': _L1_xattn_in['gamma'], 'L1_xattn_beta': _L1_xattn_in['beta'], 'L1_attn_q_kernel': _L1_attn_in['q_kernel'], 'L1_attn_k_kernel': _L1_attn_in['k_kernel'], 'L1_attn_v_kernel': _L1_attn_in['v_kernel'], 'L1_attn_out_kernel': _L1_attn_in['out_kernel'], 'L1_ffn_w_router': _L1_ffn_in['w_router'], 'L1_ffn_corr_bias': _L1_ffn_in['corr_bias'], 'L1_ffn_gate_w': _L1_ffn_in['gate_w'], 'L1_ffn_up_w': _L1_ffn_in['up_w'], 'L1_ffn_down_w': _L1_ffn_in['down_w'], 'L1_ffn_sh_gate_w': _L1_ffn_in['sh_gate_w'], 'L1_ffn_sh_up_w': _L1_ffn_in['sh_up_w'], 'L1_ffn_sh_down_w': _L1_ffn_in['sh_down_w']}

def reference(x, ctx_2048, mask_1xSxS2_ff0, L0_xattn_Wq, L0_xattn_bq, L0_xattn_Wk, L0_xattn_bk, L0_xattn_Wv, L0_xattn_bv, L0_xattn_Wo, L0_xattn_qn_w, L0_xattn_kn_w, L0_attn_w_qkv, L0_attn_w_swiglu, L0_attn_w_out, L0_ffn_router_w, L0_ffn_gate_w, L0_ffn_up_w, L0_ffn_down_w, L0_ffn_shared_gate_w, L0_ffn_shared_up_w, L0_ffn_shared_down_w, L1_xattn_decay, L1_xattn_W_in, L1_xattn_b_in, L1_xattn_W_out, L1_xattn_b_out, L1_xattn_gamma, L1_xattn_beta, L1_attn_q_kernel, L1_attn_k_kernel, L1_attn_v_kernel, L1_attn_out_kernel, L1_ffn_w_router, L1_ffn_corr_bias, L1_ffn_gate_w, L1_ffn_up_w, L1_ffn_down_w, L1_ffn_sh_gate_w, L1_ffn_sh_up_w, L1_ffn_sh_down_w):
    import jax
    import jax.numpy as jnp

    def _L0_xattn_ref(hidden_states, encoder_hidden_states, attention_mask, Wq, bq, Wk, bk, Wv, bv, Wo, qn_w, kn_w):
        import jax, jax.numpy as jnp
        import numpy as np
        H = 256
        NH = 16
        NKV = 4
        HD = 128
        GROUPS = NH // NKV
        EPS = 1e-06
        B, S, SE = (1, 256, 512)

        def _rmsnorm(x, w, eps=EPS):
            xf = x.astype(jnp.float32)
            var = jnp.mean(xf * xf, axis=-1, keepdims=True)
            return (xf * jax.lax.rsqrt(var + eps)).astype(x.dtype) * w
        b, s, _ = hidden_states.shape
        se = encoder_hidden_states.shape[1]
        q = (hidden_states @ Wq + bq).reshape(b, s, NH, HD).transpose(0, 2, 1, 3)
        k = (encoder_hidden_states @ Wk + bk).reshape(b, se, NKV, HD).transpose(0, 2, 1, 3)
        v = (encoder_hidden_states @ Wv + bv).reshape(b, se, NKV, HD).transpose(0, 2, 1, 3)
        k = jnp.repeat(k, GROUPS, axis=1)
        v = jnp.repeat(v, GROUPS, axis=1)
        q = _rmsnorm(q, qn_w)
        k = _rmsnorm(k, kn_w)
        scale = 1.0 / np.sqrt(HD).astype(np.float32)
        scores = jnp.einsum('bhsd,bhed->bhse', q, k) * scale
        scores = scores + attention_mask[:, None, :, :]
        probs = jax.nn.softmax(scores.astype(jnp.float32), axis=-1).astype(q.dtype)
        out = jnp.einsum('bhse,bhed->bhsd', probs, v)
        out = out.transpose(0, 2, 1, 3).reshape(b, s, NH * HD)
        return out @ Wo

    def _L0_attn_ref(x, w_qkv, w_swiglu, w_out):
        import jax, jax.numpy as jnp
        import numpy as np
        EPS = 1.1920929e-07

        def _rms(x):
            return x * jax.lax.rsqrt(jnp.mean(x * x, axis=-1, keepdims=True) + EPS)
        qkv = _rms(x) @ w_qkv.T
        q, k, v = jnp.split(qkv, 3, axis=-1)
        q = _rms(q)
        k = _rms(k)
        w = jnp.exp(k)
        kv_cum = jnp.cumsum(w * v, axis=1)
        w_cum = jnp.cumsum(w, axis=1)
        y = jax.nn.sigmoid(q) * (kv_cum / (w_cum + 1e-06))
        uv = y @ w_swiglu.T
        u, g = jnp.split(uv, 2, axis=-1)
        return x + u * jax.nn.silu(g) @ w_out.T

    def _L0_ffn_ref(hidden_states, router_w, gate_w, up_w, down_w, shared_gate_w, shared_up_w, shared_down_w):
        import jax, jax.numpy as jnp
        import numpy as np
        SEQ, BS, D, F, E = (128, 2, 256, 256, 8)
        S, B, Dm = hidden_states.shape
        x = hidden_states.reshape(-1, Dm)
        logits = x @ router_w
        expert_idx = jnp.argmax(logits, axis=-1)
        score = jax.nn.sigmoid(jnp.max(logits, axis=-1))
        xs = x * score[:, None]
        n_experts = router_w.shape[1]
        out = jnp.zeros_like(x)
        for e in range(n_experts):
            m = (expert_idx == e)[:, None]
            xe = jnp.where(m, xs, 0.0)
            h = jax.nn.silu(xe @ gate_w[e]) * (xe @ up_w[e])
            out = out + jnp.where(m, h @ down_w[e], 0.0)
        shared = jax.nn.silu(x @ shared_gate_w) * (x @ shared_up_w) @ shared_down_w
        return (out + shared).reshape(S, B, Dm)

    def _L1_xattn_ref(Z, kv, decay, W_in, b_in, W_out, b_out, gamma, beta):
        import jax, jax.numpy as jnp
        import numpy as np
        from jax import lax
        LN_EPS = 1e-05
        B, T, D = kv.shape
        K = jax.nn.sigmoid(decay)
        x = jnp.einsum('btd,ed->bte', kv, W_in) + b_in

        def scan_fn(s, xt):
            s = K * s + xt
            return (s, s)
        s0 = jnp.zeros((B, D), dtype=kv.dtype)
        _, states = lax.scan(scan_fn, s0, jnp.swapaxes(x, 0, 1))
        states = jnp.swapaxes(states, 0, 1)
        proj = jnp.einsum('btd,ed->bte', states, W_out) + b_out
        summary = jnp.mean(proj, axis=1, keepdims=True)
        y = Z + summary
        mu = jnp.mean(y, axis=-1, keepdims=True)
        var = jnp.mean((y - mu) ** 2, axis=-1, keepdims=True)
        return (y - mu) / jnp.sqrt(var + LN_EPS) * gamma + beta

    def _L1_attn_ref(x, q_kernel, k_kernel, v_kernel, out_kernel):
        import jax, jax.numpy as jnp
        import numpy as np
        B, T, C = (1, 512, 256)
        H, HK, D = (16, 4, 128)
        W = 128
        THETA = 10000.0

        def sine_table(features, length, max_timescale):
            fraction = jnp.arange(0, features, 2, dtype=jnp.float32) / features
            timescale = max_timescale ** fraction
            ang = jnp.arange(length, dtype=jnp.float32)[:, None] / timescale[None, :]
            ang = jnp.concatenate([ang, ang], axis=-1)
            return (jnp.sin(ang), jnp.cos(ang))

        def rotate_half(x):
            x1, x2 = jnp.split(x, 2, axis=-1)
            return jnp.concatenate([-x2, x1], axis=-1)

        def apply_rope(u, sin, cos):
            return u * cos[None, :, None, :] + rotate_half(u) * sin[None, :, None, :]
        b, t, c = x.shape
        q = jnp.dot(x, q_kernel).reshape(b, t, H, D)
        k = jnp.dot(x, k_kernel).reshape(b, t, HK, D)
        v = jnp.dot(x, v_kernel).reshape(b, t, HK, D)
        sin, cos = sine_table(D, t, THETA)
        q = apply_rope(q, sin, cos)
        k = apply_rope(k, sin, cos)
        rep = H // HK
        k = jnp.repeat(k, rep, axis=2)
        v = jnp.repeat(v, rep, axis=2)
        nb = t // W
        qb = q.reshape(b, nb, W, H, D)
        kb = k.reshape(b, nb, W, H, D)
        vb = v.reshape(b, nb, W, H, D)
        pad = ((0, 0), (1, 0), (0, 0), (0, 0), (0, 0))
        kp = jnp.pad(kb, pad)
        vp = jnp.pad(vb, pad)
        kw = jnp.concatenate([kp[:, :-1], kp[:, 1:]], axis=2)
        vw = jnp.concatenate([vp[:, :-1], vp[:, 1:]], axis=2)
        scale = 1.0 / np.sqrt(D)
        scores = jnp.einsum('bnqhd,bnkhd->bnhqk', qb, kw).astype(jnp.float32) * scale
        p = jnp.arange(W)[:, None]
        j = jnp.arange(2 * W)[None, :]
        base = (j >= p) & (j <= p + W)
        blk = jnp.arange(nb)[:, None, None]
        mask = base[None] & ((blk > 0) | (j[None] >= W))
        scores = jnp.where(mask[None, :, None], scores, jnp.float32(-1e+30))
        probs = jax.nn.softmax(scores, axis=-1).astype(v.dtype)
        ob = jnp.einsum('bnhqk,bnkhd->bnqhd', probs, vw)
        out = ob.reshape(b, t, H * D)
        return jnp.dot(out, out_kernel)

    def _L1_ffn_ref(x, w_router, corr_bias, gate_w, up_w, down_w, sh_gate_w, sh_up_w, sh_down_w):
        import jax, jax.numpy as jnp
        import numpy as np
        H = 256
        M = 176
        E = 32
        TOPK = 6
        G = 8
        TOPK_G = 4
        SH = 2
        B, S = (1, 128)
        b, s, h = x.shape
        xf = x.reshape(-1, h)
        T = xf.shape[0]
        logits = xf @ w_router
        scores = jax.nn.sigmoid(logits)
        sfc = scores + corr_bias
        grp = sfc.reshape(T, G, E // G)
        top2, _ = jax.lax.top_k(grp, 2)
        group_scores = top2.sum(-1)
        _, gidx = jax.lax.top_k(group_scores, TOPK_G)
        group_mask = jax.nn.one_hot(gidx, G, dtype=jnp.float32).sum(axis=1) > 0
        score_mask = jnp.repeat(group_mask, E // G, axis=1)
        masked = jnp.where(score_mask, sfc, -jnp.inf)
        _, topk_idx = jax.lax.top_k(masked, TOPK)
        topk_w = jnp.take_along_axis(scores, topk_idx, axis=1)
        combine = jnp.zeros((T, E), dtype=x.dtype).at[jnp.arange(T)[:, None], topk_idx].add(topk_w)
        g = jnp.einsum('th,ehm->etm', xf, gate_w)
        u = jnp.einsum('th,ehm->etm', xf, up_w)
        eo = jnp.einsum('etm,emh->eth', jax.nn.silu(g) * u, down_w)
        routed = jnp.einsum('te,eth->th', combine, eo)
        shared = jax.nn.silu(xf @ sh_gate_w) * (xf @ sh_up_w) @ sh_down_w
        return (routed + shared).reshape(b, s, h)
    x = x + _L0_xattn_ref(_layernorm(x, axis=-1), ctx_2048, mask_1xSxS2_ff0, L0_xattn_Wq, L0_xattn_bq, L0_xattn_Wk, L0_xattn_bk, L0_xattn_Wv, L0_xattn_bv, L0_xattn_Wo, L0_xattn_qn_w, L0_xattn_kn_w)
    x = x + _L0_attn_ref(_layernorm(x, axis=-1), L0_attn_w_qkv, L0_attn_w_swiglu, L0_attn_w_out)
    x = x + _L0_ffn_ref(_layernorm(x, axis=-1), L0_ffn_router_w, L0_ffn_gate_w, L0_ffn_up_w, L0_ffn_down_w, L0_ffn_shared_gate_w, L0_ffn_shared_up_w, L0_ffn_shared_down_w)
    x = x + _L1_xattn_ref(_layernorm(x, axis=-1), ctx_2048, L1_xattn_decay, L1_xattn_W_in, L1_xattn_b_in, L1_xattn_W_out, L1_xattn_b_out, L1_xattn_gamma, L1_xattn_beta)
    x = x + _L1_attn_ref(_layernorm(x, axis=-1), L1_attn_q_kernel, L1_attn_k_kernel, L1_attn_v_kernel, L1_attn_out_kernel)
    x = x + _L1_ffn_ref(_layernorm(x, axis=-1), L1_ffn_w_router, L1_ffn_corr_bias, L1_ffn_gate_w, L1_ffn_up_w, L1_ffn_down_w, L1_ffn_sh_gate_w, L1_ffn_sh_up_w, L1_ffn_sh_down_w)
    return x

_drawn_inputs = setup_inputs


def setup_inputs(seed=0):
    import zlib

    import numpy as np

    out = dict(_drawn_inputs(seed))
    spreads = {'L0_xattn_qn_w': (1.0, 0.6),
     'L0_xattn_kn_w': (1.0, 0.6),
     'L1_xattn_b_in': (0.0, 0.8),
     'L1_xattn_b_out': (0.0, 0.753),
     'L1_xattn_gamma': (1.0, 0.2),
     'L1_xattn_beta': (0.0, 0.374)}
    factors = {'L0_xattn_bq': 8.0,
     'L0_xattn_bk': 8.0,
     'L0_xattn_bv': 3.302,
     'L0_attn_w_qkv': 8.0,
     'L0_attn_w_swiglu': 8.0,
     'L0_attn_w_out': 8.0,
     'L0_ffn_router_w': 8.0,
     'L0_ffn_gate_w': 8.0,
     'L0_ffn_up_w': 8.0,
     'L0_ffn_down_w': 8.0,
     'L0_ffn_shared_gate_w': 6.813,
     'L0_ffn_shared_up_w': 6.695,
     'L0_ffn_shared_down_w': 6.663,
     'L1_attn_q_kernel': 8.0,
     'L1_attn_k_kernel': 8.0,
     'L1_ffn_w_router': 8.0,
     'L1_ffn_corr_bias': 8.0,
     'L1_ffn_gate_w': 8.0,
     'L1_ffn_up_w': 8.0,
     'L1_ffn_down_w': 8.0,
     'L1_ffn_sh_gate_w': 8.0,
     'L1_ffn_sh_up_w': 8.0,
     'L1_ffn_sh_down_w': 8.0}
    for name, (base, spread) in spreads.items():
        noise = np.random.default_rng([zlib.crc32(name.encode()), seed]).standard_normal(out[name].shape)
        drawn = base * np.exp(spread * noise) if base else spread * noise
        out[name] = jnp.asarray(drawn.astype(out[name].dtype))
    for name, factor in factors.items():
        out[name] = (out[name] * factor).astype(out[name].dtype)
    return out
```

```python
from contextlib import ExitStack

import concourse.bass as bass
from concourse import mybir
from concourse.alu_op_type import AluOpType as ALU

F32 = mybir.dt.float32
ACT = mybir.ActivationFunctionType
AX = mybir.AxisListType

P = 128
B = 2
D = 256
KD = D // P
NH, NKV = 16, 4
GH = NH // NKV
GW = GH * P
SE = 2048
NT = SE // P
NG = NKV * B
NC = SE // GW
FF = 1024
FB = FF // P
E0 = 8
E1, M1 = 32, 176
CH = 2
CW = CH * M1
IT = 8
NCH = IT // CH
BLOCKS = [(0, 2), (2, 5), (5, 8), (8, 11)]
SHW = 384
NB = IT * M1 // P
BIG = 3.0e38
SCALE = float(P) ** -0.5

KB = 1024
AT_CTX = 0
AT_S0 = 32 * KB
AT_S1 = 64 * KB
AT_KV = 96 * KB
AT_K2 = 128 * KB
AT_Q = 136 * KB
AT_MASK = 152 * KB
AT_SPARE = 160 * KB
AT_M = 176 * KB
AT_SMALL = 186 * KB


SW = (0, 1, 3, 4)


def rope_at(u):
    return u + u // NKV + 1


def column(e):
    return bass.ds(e, 1) if not isinstance(e, int) else slice(e, e + 1)


def perceiver(nc, a, out, last_stage=6):
    ctx = ExitStack()
    base = (nc.sbuf_base + 31) // 32 * 32
    small = [AT_SMALL]

    def at(name, shape, offset):
        n = 4
        for s in shape[1:]:
            n *= s
        assert base + offset + n <= nc.sbuf_usable_end, name
        return nc.alloc_sbuf_tensor_at(name, shape, F32, offset=base + offset)

    def sb(name, *shape):
        t = at(name, [P, *shape], small[0])
        n = 4
        for s in shape:
            n *= s
        small[0] += (n + 31) // 32 * 32
        return t

    def sem(name):
        return ctx.enter_context(nc.semaphore(name))

    class Steps:

        def __init__(self, name):
            self.sem, self.n = sem(name), 0

        def __call__(self, ins):
            ins.then_inc(self.sem, 1)
            self.n += 1
            return self.n

    with ctx:
        ctxT = at("ctxT", [P, B, KD, SE], AT_CTX)
        S = [at(f"S{i}", [P, NT, GW], AT_S0 + i * 32 * KB) for i in range(2)]
        wq = at("wq", [P, KD, NH * P], AT_S1)
        q_tok = at("q_tok", [P, B, NH, P], AT_S1 + 16 * KB)
        bq = at("bq", [P, NH * P], AT_S0)
        qsq = at("qsq", [P, 2, GW], AT_S0 + 8 * KB)
        KT = [at(f"KT{i}", [P, SE], AT_KV + i * 8 * KB) for i in range(2)]
        V = [at(f"V{i}", [P, NT, P], AT_KV + (2 + i) * 8 * KB) for i in range(2)]
        K2 = at("K2", [P, SE], AT_K2)
        QT = at("QT", [P, B, NKV, GW], AT_Q)
        maskT = at("maskT", [P, NT, P], AT_MASK)
        cdec = at("cdec", [P, SE], AT_SPARE)
        cprod = at("cprod", [P, SE], AT_SPARE + 8 * KB)
        M = [at(f"M{i}", [P, GW], AT_M + i * 2 * KB) for i in range(2)]
        psums = [at(f"psums{i}", [P, GW], AT_M + (2 + i) * 2 * KB) for i in range(2)]
        rden = at("rden", [P, GW], AT_M + 8 * KB)
        wo = at("wo", [P, NH, D], AT_CTX)
        wqkv = at("wqkv", [P, KD, 3 * D], AT_CTX + 16 * KB)
        wout = at("wout", [P, FB, D], AT_CTX + 22 * KB)
        wsw = at("wsw", [P, KD, 2 * FF], AT_S0)
        hsw = at("hsw", [P, FB, D], AT_S0 + 16 * KB)
        ww = at("ww", [P, B, 2 * D], AT_S0 + 24 * KB)
        w0 = at("w0", [P, E0 + 1, KD, 2 * D], AT_S1)
        d0 = at("d0", [P, E0 + 1, KD, D], AT_S1 + 36 * KB)
        wq5 = at("wq5", [P, KD, NH * P], AT_CTX)
        wo5 = at("wo5", [P, NH, D], AT_CTX + 16 * KB)
        wkv5 = at("wkv5", [P, KD, 2 * NKV * P], AT_K2)

        hx = at("hx", [P, B, D], AT_SPARE)
        yt = at("yt", [P, B, D], AT_SPARE + 2 * KB)
        eq = at("eq", [P, B, D], AT_SPARE + 4 * KB)
        yden = at("yden", [P, B, D], AT_SPARE + 6 * KB)
        sq = at("sq", [P, 4, D], AT_SPARE + 8 * KB)
        win = at("win", [P, KD, D], AT_SPARE + 12 * KB)
        wlin = at("wlin", [P, KD, D], AT_SPARE + 14 * KB)
        ssw = at("ssw", [P, 2, D], AT_MASK)
        sg0 = at("sg0", [P, 2, B, D], AT_MASK + 2 * KB)
        hT0 = at("hT0", [P, KD, B, P], AT_MASK + 6 * KB)
        h0 = at("h0", [P, 2, B, D], AT_M)
        rc = at("rc", [P, 2, GH, P], AT_S0)
        rs = at("rs", [P, 2, GH, P], AT_S0 + 4 * KB)
        rope = at("rope", [P, 2, GH, P], AT_S0 + 8 * KB)
        KT5 = at("KT5", [P, B, NKV, P], AT_S0 + 12 * KB)
        V5 = at("V5", [P, B, NKV, P], AT_S0 + 16 * KB)
        QT5 = [at(f"QT5{i}", [P, GH, P], AT_S0 + (20 + 2 * i) * KB) for i in range(2)]
        P5 = at("P5", [P, 2, GH, P], AT_S0 + 24 * KB)
        PT5 = at("PT5", [P, GH, P], AT_S0 + 28 * KB)
        OT5 = at("OT5", [P, GH, P], AT_S0 + 30 * KB)
        gu1 = [at(f"gu1{c}", [P, KD, 2 * CW], AT_S1 + c * 5632) for c in range(NCH)]
        dn1 = at("dn1", [P, NB, D], AT_S1 + 22 * KB)
        gush = at("gush", [P, KD, 2 * SHW], AT_S1 + 33 * KB)
        dnsh = at("dnsh", [P, SHW // P, D], AT_S1 + 39 * KB)
        h6 = at("h6", [P, B, IT * M1], AT_S1 + 42 * KB)
        sg6 = at("sg6", [P, B, SHW], AT_S1 + 53 * KB)
        hT6 = at("hT6", [P, B, 3, P], AT_S1 + 56 * KB)

        late_at = [AT_M + 4 * KB]

        def late(name, *shape):
            t = at(name, [P, *shape], late_at[0])
            n = 4
            for s in shape:
                n *= s
            late_at[0] += (n + 31) // 32 * 32
            assert late_at[0] <= AT_SMALL
            return t

        nmax5 = late("nmax5", 2, GH * B * NKV)
        sum5 = late("sum5", 2, GH * B * NKV)
        sc1 = late("sc1", 3, B, E1)
        pair1 = late("pair1", 2, B * E1 // 4, 2)
        grp1 = late("grp1", 3, B * E1 // 4)
        gre1 = late("gre1", B, 16)
        top1 = late("top1", 4, 8)
        gsel1 = late("gsel1", B, E1 // 4)
        msk1 = late("msk1", 2, B, E1)
        comb = late("comb", B, E1)
        summ = late("summ", B, D)
        lin = late("lin", 3, KD, B)
        ssq = late("ssq", 4)
        nrstd = late("nrstd", 4)
        r0m = late("r0m", 4, B)
        r0s = late("r0s", B)

        x = sb("xres", B, D)
        xn = sb("xn", B, D)
        xnT = sb("xnT", KD, B * P)
        consts = sb("consts", 5, P)
        ident, tri, causal, cosT, sinT = (consts[:, i, :] for i in range(5))
        ones = sb("ones", P)
        wkv = sb("wkv", KD * 2 * P + 1)
        bv = sb("bv", NKV, P)
        cols = sb("cols", 8)
        stats = sb("stats", B, 6)
        mv = sb("mv", B, 2)
        var = sb("var", 32)
        rstd = sb("rstd", 32)
        kvar = sb("kvar", 2, NT)
        krstd = sb("krstd", 2, NT)
        halfneg = sb("halfneg", 32)
        qkn = sb("qkn", 1)
        qss = sb("qss", B, NH)
        mq = sb("mq", GH)
        sig = sb("sig", 4)
        csum = sb("csum", KD, B)
        rows = sb("rows", 3, D)
        warm = sb("warm", 1)
        router0 = sb("router0", KD, E0)
        router1 = sb("router1", KD, E1)
        r0 = sb("r0", 4, B, E0)
        sel0 = sb("sel0", B, E0 + 1)
        order = sb("order", E0)
        bias1 = sb("bias1", E1)
        gsc1 = sb("gsc1", B, 16)

        ps = [ctx.enter_context(nc.psum_tensor(f"ps{i}", [P, GW], F32)) for i in range(8)]
        SC = ps[0:3]
        PR = ps[3:5]
        MISC, MB, PO = ps[5], ps[6], ps[7]

        in_x, in_consts, in_cols, in_wq, in_bq, in_mask, in_bv = (
            sem(n) for n in ("in_x", "in_consts", "in_cols", "in_wq", "in_bq", "in_mask", "in_bv"))
        in_wkv = sem("in_wkv")
        in_ctx = [[sem(f"in_ctx{b}{c}") for c in range(NC)] for b in range(B)]
        consts_set = sem("consts_set")
        var_ready, rstd_ready = sem("var_ready"), sem("rstd_ready")
        xn_ready, xT_done, xT_ready = sem("xn_ready"), sem("xT_done"), sem("xT_ready")
        q_done, q_biased, q_squared, q_summed = (sem(n) for n in ("q_done", "q_biased", "q_squared", "q_summed"))
        q_var, q_rstd, q_scaled = sem("q_var"), sem("q_rstd"), sem("q_scaled")
        qT_done, qT_ready = sem("qT_done"), sem("qT_ready")
        k_done, k_ready, v_done, v_ready = (sem(n) for n in ("k_done", "k_ready", "v_done", "v_ready"))
        ksum_done, kvar_ready, krstd_ready = sem("ksum_done"), sem("kvar_ready"), sem("krstd_ready")
        s_done, s_ready, max_step = sem("s_done"), sem("s_ready"), sem("max_step")
        maxT_done, max_ready, mb_done = sem("maxT_done"), sem("max_ready"), sem("mb_done")
        sub_done, exp_done, psum_step = sem("sub_done"), sem("exp_done"), sem("psum_step")
        pv_done, den_done, rden_ready, o_ready = (sem(n) for n in ("pv_done", "den_done", "rden_ready", "o_ready"))
        exp_dec = sem("exp_dec")
        dve_step = Steps("dve_step")
        pool_step = Steps("pool_step")
        csum_ready = sem("csum_ready")
        in_w2, in_wsw, in_lin, in_e0, in_w5, in_kv5, in_sh, in_rows = (
            sem(n) for n in ("in_w2", "in_wsw", "in_lin", "in_e0", "in_w5", "in_kv5", "in_sh", "in_rows"))
        in_gu = [sem(f"in_gu{c}") for c in range(NCH)]
        in_dn = [sem(f"in_dn{c}") for c in range(NCH)]
        qkv_done, qk_squared, nrstd_ready, w_ready, eq_ready, wv_ready, cum_done = (
            sem(n) for n in ("qkv_done", "qk_squared", "nrstd_ready", "w_ready", "eq_ready", "wv_ready", "cum_done"))
        sw_done, sw_silu, sw_ready = sem("sw_done"), sem("sw_silu"), sem("sw_ready")
        lin_done, lin_ready = sem("lin_done"), sem("lin_ready")
        max0_ready, tanh0_ready = sem("max0_ready"), sem("tanh0_ready")
        r0_done, sel0_ready, gu0_done, silu0_done, h0_ready, t0_done, hT0_ready = (
            sem(n) for n in ("r0_done", "sel0_ready", "gu0_done", "silu0_done", "h0_ready", "t0_done", "hT0_ready"))
        p5_done, rope_mul, rope_ready, v5_ready, t5_done, t5_ready, s5_done = (
            sem(n) for n in ("p5_done", "rope_mul", "rope_ready", "v5_ready", "t5_done", "t5_ready", "s5_done"))
        soft5, exp5, norm5, pT5_done, pT5_ready, o5_done, o5_ready = (
            sem(n) for n in ("soft5", "exp5", "norm5", "pT5_done", "pT5_ready", "o5_done", "o5_ready"))
        r1_done, exp1_done, comb_ready, gu6_done, silu6_done, h6_ready, t6_done, d6_done = (
            sem(n) for n in ("r1_done", "exp1_done", "comb_ready", "gu6_done", "silu6_done", "h6_ready", "t6_done",
                             "d6_done"))
        hT6_ready = [sem("hT6_ready0"), sem("hT6_ready1")]
        in_wo = sem("in_wo")
        proj_done = sem("proj_done")
        out_stored = sem("out_stored")
        x_ready = sem("x_ready")

        block = ctx.enter_context(nc.Block())

        @block.sync
        def _(sp):
            sp.dma_start(x[:].rearrange("p b d -> p (b d)"), a["x"]).then_inc(in_x, 16)
            sp.dma_start(consts[:].rearrange("p b d -> p (b d)"), a["consts"]).then_inc(in_consts, 16)
            sp.dma_start(wq[:].rearrange("p k n -> p (k n)"), a["wq"]).then_inc(in_wq, 16)
            for c in range(NC):
                sp.dma_start(ctxT[:, 0, :, c * GW:(c + 1) * GW],
                             a["ctxT"][:, 0, :, c * GW:(c + 1) * GW]).then_inc(in_ctx[0][c], 16)
            sp.dma_start(maskT[:].rearrange("p t n -> p (t n)"), a["maskT"]).then_inc(in_mask, 16)
            for c in range(NC):
                sp.dma_start(ctxT[:, 1, :, c * GW:(c + 1) * GW],
                             a["ctxT"][:, 1, :, c * GW:(c + 1) * GW]).then_inc(in_ctx[1][c], 16)
            with sp.Fori(0, NKV - 1) as i:
                sp.wait_ge(ksum_done, 2 * i + 2)
                sp.dma_start(wkv[:], a["wkv"][:, i + 1, :]).then_inc(in_wkv, 16)
            sp.wait_ge(ksum_done, NG)
            sp.wait_ge(csum_ready, B * KD)
            sp.dma_start(wo[:].rearrange("p h d -> p (h d)"), a["wo"]).then_inc(in_wo, 16)
            sp.dma_start(wqkv[:].rearrange("p k n -> p (k n)"), a["wqkv"]).then_inc(in_w2, 16)
            sp.dma_start(wout[:].rearrange("p k n -> p (k n)"), a["wout"]).then_inc(in_w2, 16)
            sp.dma_start(win[:].rearrange("p k n -> p (k n)"), a["win"]).then_inc(in_lin, 16)
            sp.dma_start(wlin[:].rearrange("p k n -> p (k n)"), a["wlin"]).then_inc(in_lin, 16)
            sp.wait_ge(den_done, NG - 1)
            sp.dma_start(wsw[:].rearrange("p k n -> p (k n)"), a["wsw"]).then_inc(in_wsw, 16)
            sp.wait_ge(den_done, NG)
            sp.dma_start(w0[:].rearrange("p e k n -> p (e k n)"), a["w0"]).then_inc(in_e0, 16)
            sp.dma_start(d0[:].rearrange("p e k n -> p (e k n)"), a["d0"]).then_inc(in_e0, 16)
            sp.wait_ge(proj_done, 4)
            sp.dma_start(wkv5[:].rearrange("p k n -> p (k n)"), a["wkv5"]).then_inc(in_kv5, 16)
            sp.dma_start(wq5[:].rearrange("p k n -> p (k n)"), a["wq5"]).then_inc(in_w5, 16)
            sp.dma_start(wo5[:].rearrange("p k n -> p (k n)"), a["wo5"]).then_inc(in_w5, 16)
            sp.wait_ge(proj_done, 6)
            sp.dma_start(gush[:].rearrange("p k n -> p (k n)"), a["gush"]).then_inc(in_sh, 16)
            sp.dma_start(dnsh[:].rearrange("p k n -> p (k n)"), a["downsh"]).then_inc(in_sh, 16)

            def load_chunk(c, turn):
                lo, hi = BLOCKS[c]
                sp.dma_start(gu1[c][:].rearrange("p k n -> p (k n)"),
                             a["gu1"].rearrange("p (i c) n -> p i c n", c=NCH)[:, turn, c, :]).then_inc(in_gu[c], 16)
                return (dn1[:, lo:hi, :], a["down1"].rearrange("p (i k) n -> p i k n", k=NB)[:, turn, lo:hi, :])

            for c in range(NCH):
                sp.dma_start(*load_chunk(c, 0)).then_inc(in_dn[c], 16)
            with sp.Fori(0, E1 // IT - 1) as i:
                for c in range(NCH):
                    sp.wait_ge(gu6_done, B * NCH * i + B * (c + 2))
                    down = load_chunk(c, i + 1)
                    sp.wait_ge(d6_done, NCH * i + c + 2)
                    sp.dma_start(*down).then_inc(in_dn[c], 16)
            for b in range(B):
                sp.wait_ge(x_ready, b + 1)
                sp.dma_start(out[:, b * D:(b + 1) * D], x[:, b, :]).then_inc(out_stored, 16)
            sp.wait_ge(out_stored, 16 * B)

        @block.gpsimd
        def _(pool):
            nc.gpsimd.memset(ones[:], 1.0)
            nc.gpsimd.memset(sel0[:, :, 0:1], 1.0)
            nc.gpsimd.memset(gsc1[:], -BIG)
            for e in range(E0):
                nc.gpsimd.memset(order[:, e:e + 1], float(E0 - e))
            nc.gpsimd.memset(halfneg[:], -0.5).then_inc(consts_set, 1)
            pool.wait_ge(consts_set, 1)

            def rsqrt(dst, src, n):
                return nc.gpsimd.tensor_tensor(dst, src, halfneg[:, 0:n], ALU.pow)

            pool.wait_ge(var_ready, 1)
            rsqrt(rstd[:, 0:B], var[:, 0:B], B).then_inc(rstd_ready, 1)
            pool.wait_ge(q_var, 1)
            rsqrt(rstd[:], var[:], B * NH).then_inc(q_rstd, 1)

            def key_norms(g, b):
                pool.wait_ge(kvar_ready, g + 1)
                rsqrt(krstd[:, b, :], kvar[:, b, :], NT).then_inc(krstd_ready, 1)

            def sum_probs(g, b, tiles):
                for j in tiles:
                    pool.wait_ge(exp_done, g * NT + j + 1)
                    if j > 1:
                        pool.wait_ge(psum_step, g * (NT - 1) + j - 1)
                    nc.gpsimd.tensor_tensor(psums[b][:], S[b][:, 0, :] if j == 1 else psums[b][:],
                                            S[b][:, j, :], ALU.add).then_inc(psum_step, 1)

            def half(n, b, scores=True, keys=True):
                if scores:
                    sum_probs(n + 1, 1 - b, range(1, 11))
                if keys:
                    key_norms(n + 2, b)
                if scores:
                    sum_probs(n + 1, 1 - b, range(11, NT))

            key_norms(0, 0)
            half(-1, 1)
            with pool.Fori(0, NKV - 1) as i:
                half(2 * i, 0)
                half(2 * i + 1, 1)
            half(NG - 2, 0, keys=False)

            for n, width in ((2, 2), (3, 2), (4, 4), (5, 2), (6, 2), (7, 2), (8, 2)):
                pool.wait_ge(var_ready, n)
                rsqrt(rstd[:, 0:width], var[:, 0:width], width).then_inc(rstd_ready, 1)
            for r in range(B * (NKV + 1)):
                pool.wait_ge(rope_mul, r + 1)
                if r >= 2:
                    pool.wait_ge(t5_done, r - 1)
                nc.gpsimd.tensor_tensor(rope[:, r % 2], rc[:, r % 2], rs[:, r % 2], ALU.add).then_inc(rope_ready, 1)
            pool.wait_ge(var_ready, 9)
            rsqrt(rstd[:, 0:B], var[:, 0:B], B).then_inc(rstd_ready, 1)

        @block.scalar
        def _(act):
            act.dma_start(cols[:], a["cols"]).then_inc(in_cols, 16)
            act.dma_start(wkv[:], a["wkv"][:, 0, :]).then_inc(in_wkv, 16)
            act.dma_start(bq[:], a["bq"].broadcast_to([P, NH * P])).then_inc(in_bq, 16)
            act.dma_start(bv[:].rearrange("p g d -> p (g d)"), a["bv"].broadcast_to([P, NKV * P])).then_inc(in_bv, 16)
            act.dma_start(rows[:].rearrange("p g d -> p (g d)"), a["rows"].broadcast_to([P, 3 * D])).then_inc(in_rows, 16)
            act.dma_start(router0[:].rearrange("p k d -> p (k d)"), a["router0"]).then_inc(in_rows, 16)
            act.dma_start(router1[:].rearrange("p k d -> p (k d)"), a["router1"]).then_inc(in_rows, 16)
            act.dma_start(bias1[:], a["bias1"].broadcast_to([P, E1])).then_inc(in_rows, 16)
            act.wait_ge(in_cols, 16)
            nc.scalar.activation(sig[:, 0:1], cols[:, 4:5], ACT.Exp, scale=-1.0).then_inc(exp_dec, 1)
            for u in range(B * NKV):
                act.wait_ge(q_biased, u + 1)
                if u >= 2:
                    act.wait_ge(q_summed, u - 1)
                nc.scalar.activation(qsq[:, u % 2, :], q_tok[:, u // NKV, u % NKV * GH:(u % NKV + 1) * GH, :],
                                     ACT.Square).then_inc(q_squared, 1)

            bk = wkv[:, KD * 2 * P:KD * 2 * P + 1]

            def key_chunk(g, b, t):
                act.wait_ge(k_done, NC * g + t + 1)
                nc.scalar.activation(KT[b][:, t * GW:(t + 1) * GW], PR[t % 2][:], ACT.Identity, bias=bk)
                nc.scalar.activation(K2[:, t * GW:(t + 1) * GW], PR[t % 2][:], ACT.Square,
                                     bias=bk).then_inc(k_ready, 1)

            def exps(g, b, tiles):
                for j in tiles:
                    act.wait_ge(sub_done, g * NT + j + 1)
                    nc.scalar.activation(S[b][:, j, :], S[b][:, j, :], ACT.Exp).then_inc(exp_done, 1)

            def half(n, b, scores=True, keys=True):
                after = [0, 4, 6, 6, NT]
                for t in range(NC):
                    if keys:
                        key_chunk(n + 2, b, t)
                    if scores:
                        exps(n + 1, 1 - b, range(after[t], after[t + 1]))

            for t in range(NC):
                key_chunk(0, 0, t)
            for u in range(B * NKV):
                act.wait_ge(qT_done, u + 1)
                nc.scalar.activation(QT[:, u // NKV, u % NKV, :], PR[u % 2][:], ACT.Identity,
                                     scale=qkn[:, 0:1]).then_inc(qT_ready, 1)
            half(-1, 1)
            with act.Fori(0, NKV - 1) as i:
                half(2 * i, 0)
                half(2 * i + 1, 1)
            half(NG - 2, 0, keys=False)

            def silu_tables():
                nc.scalar.activation(warm[:], ones[:, 0:1], ACT.Silu)

            for b in range(B):
                act.wait_ge(qkv_done, 2 * b + 1)
                for i in range(2):
                    nc.scalar.activation(sq[:, 2 * b + i, :], ps[b][:, i * D:(i + 1) * D], ACT.Square,
                                         accum_out=ssq[:, 2 * b + i:2 * b + i + 1]).then_inc(qk_squared, 1)
            act.wait_ge(rstd_ready, 4)
            for b in range(B):
                nc.scalar.activation(ww[:, b, D:2 * D], ps[b][:, D:2 * D], ACT.Exp,
                                     scale=rstd[:, 2 * b + 1:2 * b + 2]).then_inc(w_ready, 1)
            act.wait_ge(nrstd_ready, 1)
            for b in range(B):
                nc.scalar.activation(eq[:, b, :], ps[b][:, 0:D], ACT.Exp,
                                     scale=nrstd[:, 2 * b:2 * b + 1]).then_inc(eq_ready, 1)
            silu_tables()
            for f in range(FB):
                act.wait_ge(sw_done, f + 1)
                if f >= 2:
                    act.wait_ge(sw_ready, f - 1)
                nc.scalar.activation(ssw[:, f % 2, :], ps[SW[f % 4]][:, D:2 * D], ACT.Silu).then_inc(sw_silu, 1)

            def silu0(e, par):
                for b in range(B):
                    act.wait_ge(gu0_done, B * e + b + 1)
                    nc.scalar.activation(sg0[:, par, b, :], ps[1 + 2 * par + b][:, 0:D], ACT.Silu,
                                         scale=sel0[:, b, column(e)]).then_inc(silu0_done, 1)

            def turned0(e):
                act.wait_ge(t0_done, e + 1)
                nc.scalar.activation(hT0[:].rearrange("p k b t -> p (k b t)"), ps[5][:], ACT.Copy).then_inc(hT0_ready, 1)

            act.wait_ge(max0_ready, 1)
            nc.scalar.activation(r0s[:], r0m[:, 0], ACT.Tanh, scale=0.5).then_inc(tanh0_ready, 1)
            silu0(0, 0)
            act.wait_ge(sel0_ready, 1)
            silu0(1, 1)
            turned0(0)
            with act.Fori(0, 3) as i:
                silu0(2 * i + 2, 0)
                turned0(2 * i + 1)
                silu0(2 * i + 3, 1)
                turned0(2 * i + 2)
            silu0(E0, 0)
            turned0(E0 - 1)
            turned0(E0)
            nc.scalar.activation(warm[:], ones[:, 0:1], ACT.Exp)

            def turned5(r, dst):
                act.wait_ge(t5_done, r + 1)
                nc.scalar.activation(dst, ps[2][:].rearrange("p (h t) -> p h t", h=GH), ACT.Copy).then_inc(t5_ready, 1)

            for s in range(B * NKV + 2):
                b, c = divmod(s, NKV)
                if s < B * NKV and c == 0:
                    act.wait_ge(p5_done, 6 * b + 2)
                    nc.scalar.activation(V5[:, b].rearrange("p g d -> p (g d)"), ps[1][:], ACT.Copy).then_inc(v5_ready, 1)
                u = s - 1
                if 0 <= u < B * NKV:
                    if u % NKV == 0:
                        turned5(rope_at(u) - 1, KT5[:, u // NKV])
                    turned5(rope_at(u), QT5[u % 2][:])
                if 0 <= s - 2:
                    act.wait_ge(pT5_done, s - 1)
                    nc.scalar.activation(PT5[:].rearrange("p h t -> p (h t)"), ps[3][:], ACT.Copy).then_inc(pT5_ready, 1)
                    act.wait_ge(o5_done, s - 1)
                    nc.scalar.activation(OT5[:].rearrange("p h t -> p (h t)"), ps[5][:], ACT.Copy).then_inc(o5_ready, 1)
                if 0 <= u < B * NKV:
                    act.wait_ge(soft5, u + 1)
                    for h in range(GH):
                        last = nc.scalar.activation(P5[:, u % 2, h, :], P5[:, u % 2, h, :], ACT.Exp,
                                                    bias=nmax5[:, 1, u * GH + h:u * GH + h + 1],
                                                    accum_out=sum5[:, 0, u * GH + h:u * GH + h + 1])
                    last.then_inc(exp5, 1)

            act.wait_ge(r1_done, 1)
            nc.scalar.activation(sc1[:, 0].rearrange("p b e -> p (b e)"), ps[4][:, 0:B * E1], ACT.Exp,
                                 scale=-1.0).then_inc(exp1_done, 1)
            silu_tables()

            def silu6(step, width):
                for b in range(B):
                    act.wait_ge(gu6_done, B * step + b + 1)
                    nc.scalar.activation(sg6[:, b, 0:width], ps[2 * b][:, 0:width], ACT.Silu).then_inc(silu6_done, 1)

            def turned6(step, n):
                act.wait_ge(t6_done, B * step + 1)
                nc.scalar.activation(hT6[:, 0, 0:n, :].rearrange("p k t -> p (k t)"), ps[4][:, 0:n * P],
                                     ACT.Copy).then_inc(hT6_ready[0], 1)

            silu6(0, SHW)
            silu6(1, CW)
            turned6(0, SHW // P)
            with act.Fori(0, E1 // IT - 1) as i:
                for c in range(NCH):
                    silu6(NCH * i + c + 2, CW)
                    turned6(NCH * i + c + 1, BLOCKS[c][1] - BLOCKS[c][0])
            for c in range(NCH):
                if c < NCH - 1:
                    silu6(E1 // CH - NCH + c + 2, CW)
                turned6(E1 // CH - NCH + c + 1, BLOCKS[c][1] - BLOCKS[c][0])

        @block.vector
        def _(dve):
            def norm_stats(src, n):
                for b in range(B):
                    c = dve_step(nc.vector.bn_stats(stats[:, b, :], src[:, b, :]))
                dve.wait_ge(dve_step.sem, c)
                for b in range(B):
                    c = dve_step(nc.vector.bn_aggr(mv[:, b, :], stats[:, b, :]))
                dve.wait_ge(dve_step.sem, c)
                nc.vector.tensor_scalar(var[:, 0:B], mv[:, :, 1], 1e-5, None, ALU.add).then_inc(var_ready, 1)
                dve.wait_ge(rstd_ready, n)

            def normalise(dst, src, sem_, n):
                norm_stats(src, n)
                for b in range(B):
                    last = nc.vector.tensor_scalar(dst[:, b, :], src[:, b, :], mv[:, b, 0:1], rstd[:, b:b + 1],
                                                   ALU.subtract, ALU.mult)
                last.then_inc(sem_, 1)

            dve.wait_ge(in_x, 16)
            normalise(xn, x, xn_ready, 1)
            dve.wait_ge(exp_dec, 1)
            dve.wait_ge(consts_set, 1)
            c = dve_step(nc.vector.tensor_scalar(sig[:, 1:2], sig[:, 0:1], 1.0, None, ALU.add))
            dve_step(nc.vector.tensor_tensor(qkn[:], cols[:, 0:1], cols[:, 1:2], ALU.mult))
            dve.wait_ge(dve_step.sem, c)
            c = dve_step(nc.vector.reciprocal(sig[:, 2:3], sig[:, 1:2]))
            dve.wait_ge(dve_step.sem, c)
            dve_step(nc.vector.tensor_scalar(qkn[:], qkn[:], SCALE, None, ALU.mult))
            c = dve_step(nc.vector.tensor_tensor_scan(cdec[:, ::-1], sig[:, 2:3].broadcast_to([P, SE]),
                                                      ones[:, 0:1].broadcast_to([P, SE]), 0.0, ALU.mult, ALU.add))
            dve.wait_ge(xT_done, 1)
            nc.vector.tensor_copy(xnT[:].rearrange("p k n -> p (k n)"), SC[0][:]).then_inc(xT_ready, 1)
            dve.wait_ge(dve_step.sem, c)
            dve_step(nc.vector.reduce_sum(sig[:, 3:4], cdec[:], AX.X))

            dve.wait_ge(in_bq, 16)
            for u in range(B * NKV + 1):
                if u < B * NKV:
                    dve.wait_ge(q_done, u + 1)
                    nc.vector.tensor_tensor(q_tok[:, u // NKV, u % NKV * GH:(u % NKV + 1) * GH, :].rearrange("p h d -> p (h d)"),
                                            SC[1 + u % 2][:], bq[:, u % NKV * GW:(u % NKV + 1) * GW],
                                            ALU.add).then_inc(q_biased, 1)
                if u:
                    dve.wait_ge(q_squared, u)
                    v = u - 1
                    nc.vector.reduce_sum(qss[:, v // NKV, v % NKV * GH:(v % NKV + 1) * GH],
                                         qsq[:, v % 2, :].rearrange("p (h d) -> p h d", h=GH), AX.X).then_inc(q_summed, 1)
            dve.wait_ge(q_summed, B * NKV)
            nc.vector.tensor_scalar(var[:], qss[:].rearrange("p b h -> p (b h)"), 1.0 / P, 1e-6,
                                    ALU.mult, ALU.add).then_inc(q_var, 1)
            dve.wait_ge(q_rstd, 1)
            for b in range(B):
                nc.vector.tensor_tensor(q_tok[:, b, :, :], q_tok[:, b, :, :],
                                        rstd[:, b * NH:(b + 1) * NH].unsqueeze(2).broadcast_to([P, NH, P]),
                                        ALU.mult).then_inc(q_scaled, 1)

            def value_chunk(g, b, t, kvh):
                dve.wait_ge(v_done, NC * g + t + 1)
                nc.vector.tensor_tensor(V[b][:, 4 * t:4 * t + 4, :], PR[t % 2][:].rearrange("p (t d) -> p t d", t=4),
                                        bv[:, kvh, :].unsqueeze(1).broadcast_to([P, 4, P]), ALU.add).then_inc(v_ready, 1)

            def key_vars(g, b):
                dve.wait_ge(ksum_done, g + 1)
                nc.vector.tensor_scalar(kvar[:, b, :], MISC[:, 0:NT], 1.0 / P, 1e-6, ALU.mult, ALU.add).then_inc(kvar_ready, 1)

            def running_max(g, b, j):
                dve.wait_ge(s_ready, g * NT + j + 1)
                if j > 1:
                    dve.wait_ge(max_step, g * (NT - 1) + j - 1)
                nc.vector.tensor_tensor(M[b][:], S[b][:, 0, :] if j == 1 else M[b][:], S[b][:, j, :],
                                        ALU.max).then_inc(max_step, 1)

            def score_tiles(g, b):
                dve.wait_ge(krstd_ready, g + 1)
                for j in range(NT):
                    dve.wait_ge(s_done, g * NT + j + 1)
                    nc.vector.scalar_tensor_tensor(
                        out=S[b][:, j, :].rearrange("p (h q) -> p h q", h=GH),
                        in0=SC[j % 3][:].rearrange("p (h q) -> p h q", h=GH), scalar=krstd[:, b, j:j + 1],
                        in1=maskT[:, j, :].unsqueeze(1).broadcast_to([P, GH, P]),
                        op0=ALU.mult, op1=ALU.add).then_inc(s_ready, 1)
                    if j >= 2:
                        running_max(g, b, j - 1)
                running_max(g, b, NT - 1)

            def reduce_maxima(g):
                dve.wait_ge(maxT_done, g + 1)
                nc.vector.reduce_max(mq[:], MISC[:].rearrange("p (h k) -> p h k", h=GH), AX.X).then_inc(max_ready, 1)

            def outputs(g, b, kvh):
                dve.wait_ge(den_done, g + 1)
                nc.vector.reciprocal(rden[:], MISC[:]).then_inc(rden_ready, 1)
                dve.wait_ge(rden_ready, g + 1)
                nc.vector.tensor_tensor(QT[:, b, kvh, :], PO[:], rden[:], ALU.mult).then_inc(o_ready, 1)

            def subtract_maxima(g, b, tiles):
                dve.wait_ge(mb_done, g + 1)
                for j in tiles:
                    nc.vector.tensor_tensor(S[b][:, j, :], S[b][:, j, :], MB[:], ALU.subtract).then_inc(sub_done, 1)

            def half(n, b, kvh, scores=True, pv=True, keys=True):
                if scores:
                    score_tiles(n + 1, 1 - b)
                    reduce_maxima(n + 1)
                    subtract_maxima(n + 1, 1 - b, range(0, 6))
                if pv:
                    outputs(n, b, kvh)
                for t in range(NC):
                    if keys:
                        value_chunk(n + 2, b, t, kvh + 1)
                    if scores:
                        subtract_maxima(n + 1, 1 - b, range(6 + 3 * t, min(9 + 3 * t, NT)))
                if keys:
                    key_vars(n + 2, b)

            def context_sum(b):
                for t in range(NC):
                    dve.wait_ge(in_ctx[b][t], 16)
                for k in range(KD):
                    if b + k:
                        dve.wait_ge(csum_ready, b * KD + k)
                    nc.vector.tensor_tensor_reduce(cprod[:], ctxT[:, b, k, :], cdec[:], 1.0, 0.0, ALU.mult, ALU.add,
                                                   csum[:, k, b:b + 1]).then_inc(csum_ready, 1)


            dve.wait_ge(in_bv, 16)
            for t in range(NC):
                value_chunk(0, 0, t, 0)
            key_vars(0, 0)
            context_sum(0)
            dve.wait_ge(in_mask, 16)
            half(-1, 1, -1, pv=False)
            context_sum(1)
            with dve.Fori(0, NKV - 1) as i:
                half(2 * i, 0, i)
                half(2 * i + 1, 1, i)
            half(NG - 2, 0, NKV - 1, keys=False)
            half(NG - 1, 1, NKV - 1, scores=False, keys=False)

            def add_to_x(n, bank=6):
                for b in range(B):
                    dve.wait_ge(proj_done, n + b)
                    last = nc.vector.tensor_tensor(x[:, b, :], x[:, b, :], ps[bank + b][:, 0:D], ALU.add)
                    if n == 9:
                        last.then_inc(x_ready, 1)
                if n < 9:
                    dve.wait_ge(dve_step.sem, dve_step(last))

            def copy_turned(n):
                dve.wait_ge(xT_done, n)
                nc.vector.tensor_copy(xnT[:].rearrange("p k n -> p (k n)"), ps[2][:]).then_inc(xT_ready, 1)

            def then(ins):
                dve.wait_ge(dve_step.sem, dve_step(ins))

            add_to_x(1, 0)
            norm_stats(x, 2)
            for b in range(B):
                c = dve_step(nc.vector.tensor_scalar(xn[:, b, :], x[:, b, :], mv[:, b, 0:1], rstd[:, b:b + 1],
                                                     ALU.subtract, ALU.mult))
            for b in range(B):
                dve.wait_ge(dve_step.sem, c - 1 + b)
                last = nc.vector.tensor_tensor_reduce(sq[:, b, :], xn[:, b, :], xn[:, b, :], 1.0 / D, 1.1920929e-07,
                                                      ALU.mult, ALU.add, var[:, b:b + 1])
            last.then_inc(var_ready, 1)
            then(nc.vector.tensor_tensor(x[:], x[:], xn[:], ALU.add))
            dve.wait_ge(rstd_ready, 3)
            for b in range(B):
                last = nc.vector.tensor_scalar(hx[:, b, :], xn[:, b, :], rstd[:, b:b + 1], None, ALU.mult)
            last.then_inc(xn_ready, 1)
            copy_turned(2)
            c = dve_step(nc.vector.tensor_scalar(lin[:, 0, :, 0], cols[:, 2:4], sig[:, 3:4], None, ALU.mult))
            dve.wait_ge(dve_step.sem, c)
            dve.wait_ge(lin_done, 1)
            then(nc.vector.tensor_tensor(lin[:, 1], ps[7][:, 0:KD * B].rearrange("p (k b) -> p k b", b=B),
                                         lin[:, 0, :, 0:1].broadcast_to([P, KD, B]), ALU.add))
            nc.vector.tensor_scalar(lin[:, 2], lin[:, 1], 1.0 / SE, None, ALU.mult).then_inc(lin_ready, 1)
            dve.wait_ge(qk_squared, 2 * B)
            nc.vector.tensor_scalar(var[:, 0:4], ssq[:], 1.0 / D, 1.1920929e-07, ALU.mult, ALU.add).then_inc(var_ready, 1)
            dve.wait_ge(rstd_ready, 4)
            nc.vector.tensor_scalar(nrstd[:], rstd[:, 0:4], -1.0, None, ALU.mult).then_inc(nrstd_ready, 1)
            for b in range(B):
                dve.wait_ge(w_ready, b + 1)
                dve.wait_ge(qkv_done, 2 * b + 2)
                nc.vector.tensor_tensor(ww[:, b, 0:D], ww[:, b, D:2 * D], ps[3 + b][:, 0:D], ALU.mult).then_inc(wv_ready, 1)
            for b in range(B):
                dve.wait_ge(cum_done, b + 1)
                c = dve_step(nc.vector.tensor_scalar(yden[:, b, :], ps[5 + b][:, D:2 * D], 1e-6, None, ALU.add))
            dve.wait_ge(eq_ready, B)
            for b in range(B):
                dve.wait_ge(dve_step.sem, c - 1 + b)
                d = dve_step(nc.vector.scalar_tensor_tensor(out=yden[:, b, :], in0=eq[:, b, :], scalar=1.0,
                                                            in1=yden[:, b, :], op0=ALU.add, op1=ALU.mult))
            for b in range(B):
                dve.wait_ge(dve_step.sem, d - 1 + b)
                c = dve_step(nc.vector.reciprocal(yden[:, b, :], yden[:, b, :]))
            for b in range(B):
                dve.wait_ge(dve_step.sem, c - 1 + b)
                last = nc.vector.tensor_tensor(yt[:, b, :], ps[5 + b][:, 0:D], yden[:, b, :], ALU.mult)
            last.then_inc(xn_ready, 1)
            copy_turned(3)
            for f in range(FB):
                dve.wait_ge(sw_silu, f + 1)
                nc.vector.tensor_tensor(hsw[:, f, :], ps[SW[f % 4]][:, 0:D], ssw[:, f % 2, :], ALU.mult).then_inc(sw_ready, 1)
            dve.wait_ge(in_rows, 64)
            dve.wait_ge(lin_done, 2)
            nc.vector.tensor_tensor(summ[:], ps[7][:].rearrange("p (b d) -> p b d", b=B),
                                    rows[:, 0:1, :].broadcast_to([P, B, D]), ALU.add).then_inc(lin_ready, 1)
            add_to_x(3, 5)

            def normalise_x(n, nx):
                norm_stats(x, n)
                for b in range(B):
                    last = nc.vector.tensor_scalar(xn[:, b, :], x[:, b, :], mv[:, b, 0:1], rstd[:, b:b + 1],
                                                   ALU.subtract, ALU.mult)
                last.then_inc(xn_ready, 1)
                copy_turned(nx)

            normalise_x(5, 4)
            dve.wait_ge(r0_done, 1)
            lg = ps[0][:, 0:B * E0].rearrange("p (b e) -> p b e", b=B)
            nc.vector.reduce_max(r0m[:, 0], lg, AX.X).then_inc(max0_ready, 1)
            dve.wait_ge(max0_ready, 1)
            then(nc.vector.tensor_tensor(r0[:, 0], lg, r0m[:, 0].unsqueeze(2).broadcast_to([P, B, E0]), ALU.is_equal))
            then(nc.vector.tensor_tensor(r0[:, 1], r0[:, 0], order[:].unsqueeze(1).broadcast_to([P, B, E0]), ALU.mult))
            then(nc.vector.reduce_max(r0m[:, 2], r0[:, 1], AX.X))
            then(nc.vector.tensor_tensor(r0[:, 2], r0[:, 1], r0m[:, 2].unsqueeze(2).broadcast_to([P, B, E0]), ALU.is_equal))
            dve.wait_ge(tanh0_ready, 1)
            then(nc.vector.tensor_scalar(r0m[:, 3], r0s[:], 0.5, 0.5, ALU.mult, ALU.add))
            nc.vector.tensor_tensor(sel0[:, :, 1:E0 + 1], r0[:, 2], r0m[:, 3].unsqueeze(2).broadcast_to([P, B, E0]),
                                    ALU.mult).then_inc(sel0_ready, 1)
            dve.wait_ge(sel0_ready, 1)

            def products0(e, par):
                for b in range(B):
                    dve.wait_ge(silu0_done, B * e + b + 1)
                    nc.vector.scalar_tensor_tensor(out=h0[:, par, b, :], in0=ps[1 + 2 * par + b][:, D:2 * D],
                                                   scalar=sel0[:, b, column(e)], in1=sg0[:, par, b, :],
                                                   op0=ALU.mult, op1=ALU.mult).then_inc(h0_ready, 1)

            products0(0, 0)
            with dve.Fori(0, E0 // 2) as i:
                products0(2 * i + 1, 1)
                products0(2 * i + 2, 0)
            add_to_x(5)

            norm_stats(x, 6)
            for b in range(B):
                c = dve_step(nc.vector.tensor_scalar(xn[:, b, :], x[:, b, :], mv[:, b, 0:1], rstd[:, b:b + 1],
                                                     ALU.subtract, ALU.mult))
            dve.wait_ge(dve_step.sem, c)
            then(nc.vector.tensor_tensor(yt[:], xn[:], summ[:], ALU.add))
            norm_stats(yt, 7)
            for b in range(B):
                c = dve_step(nc.vector.tensor_scalar(xn[:, b, :], yt[:, b, :], mv[:, b, 0:1], rstd[:, b:b + 1],
                                                     ALU.subtract, ALU.mult))
            dve.wait_ge(dve_step.sem, c)
            then(nc.vector.tensor_tensor(yt[:], xn[:], rows[:, 1:2, :].broadcast_to([P, B, D]), ALU.mult))
            then(nc.vector.tensor_tensor(xn[:], yt[:], rows[:, 2:3, :].broadcast_to([P, B, D]), ALU.add))
            then(nc.vector.tensor_tensor(x[:], x[:], xn[:], ALU.add))

            normalise_x(8, 5)

            def rotate(r, m):
                dve.wait_ge(p5_done, m + 1)
                if r >= 2:
                    dve.wait_ge(rope_ready, r - 1)
                src = ps[m % 2][:].rearrange("p (h d) -> p h d", h=GH)
                nc.vector.tensor_tensor(rc[:, r % 2], src, cosT.unsqueeze(1).broadcast_to([P, GH, P]), ALU.mult)
                for lo, hi in ((0, P // 2), (P // 2, P)):
                    last = nc.vector.tensor_tensor(rs[:, r % 2, :, lo:hi], src[:, :, P // 2 - lo:P - lo],
                                                   sinT[:, lo:hi].unsqueeze(1).broadcast_to([P, GH, P // 2]), ALU.mult)
                last.then_inc(rope_mul, 1)

            for s in range(B * NKV + 2):
                b, c = divmod(s, NKV)
                if s - 2 >= 0:
                    u = s - 2
                    dve.wait_ge(exp5, u + 1)
                    then(nc.vector.reciprocal(sum5[:, 1, u * GH:(u + 1) * GH], sum5[:, 0, u * GH:(u + 1) * GH]))
                    nc.vector.tensor_tensor(P5[:, u % 2], P5[:, u % 2],
                                            sum5[:, 1, u * GH:(u + 1) * GH].unsqueeze(2).broadcast_to([P, GH, P]),
                                            ALU.mult).then_inc(norm5, 1)
                if s < B * NKV:
                    if c == 0:
                        rotate(rope_at(s) - 1, 6 * b)
                    rotate(rope_at(s), 6 * b + 2 + c)
                if 1 <= s <= B * NKV:
                    u = s - 1
                    dve.wait_ge(s5_done, u + 1)
                    then(nc.vector.scalar_tensor_tensor(
                        out=P5[:, u % 2], in0=ps[4][:].rearrange("p (h k) -> p h k", h=GH), scalar=SCALE,
                        in1=causal.unsqueeze(1).broadcast_to([P, GH, P]), op0=ALU.mult, op1=ALU.add))
                    then(nc.vector.reduce_max(nmax5[:, 0, u * GH:(u + 1) * GH], P5[:, u % 2], AX.X))
                    nc.vector.tensor_scalar(nmax5[:, 1, u * GH:(u + 1) * GH], nmax5[:, 0, u * GH:(u + 1) * GH], -1.0, None,
                                            ALU.mult).then_inc(soft5, 1)
            add_to_x(7)

            normalise_x(9, 6)
            dve.wait_ge(exp1_done, 1)
            then(nc.vector.tensor_scalar(sc1[:, 0], sc1[:, 0], 1.0, None, ALU.add))
            then(nc.vector.reciprocal(sc1[:, 1], sc1[:, 0]))
            then(nc.vector.tensor_tensor(sc1[:, 2], sc1[:, 1], bias1[:].unsqueeze(1).broadcast_to([P, B, E1]), ALU.add))
            four = sc1[:, 2].rearrange("p b (g f) -> p (b g) f", f=4)
            nc.vector.tensor_tensor(pair1[:, 0], four[:, :, 0:2], four[:, :, 2:4], ALU.max)
            then(nc.vector.tensor_tensor(pair1[:, 1], four[:, :, 0:2], four[:, :, 2:4], ALU.min))
            nc.vector.tensor_tensor(grp1[:, 0], pair1[:, 0, :, 0], pair1[:, 0, :, 1], ALU.max)
            nc.vector.tensor_tensor(grp1[:, 1], pair1[:, 0, :, 0], pair1[:, 0, :, 1], ALU.min)
            then(nc.vector.tensor_tensor(grp1[:, 2], pair1[:, 1, :, 0], pair1[:, 1, :, 1], ALU.max))
            then(nc.vector.tensor_tensor(grp1[:, 1], grp1[:, 1], grp1[:, 2], ALU.max))
            then(nc.vector.tensor_tensor(gsc1[:, :, 0:E1 // 4], grp1[:, 0].rearrange("p (b g) -> p b g", b=B),
                                         grp1[:, 1].rearrange("p (b g) -> p b g", b=B), ALU.add))
            for b in range(B):
                then(nc.vector.max(top1[:, b, :], gsc1[:, b, :]))
                then(nc.vector.memset(top1[:, b, 4:8], -BIG))
                c = dve_step(nc.vector.match_replace(gre1[:, b, :], top1[:, b, :], gsc1[:, b, :], -BIG))
            dve.wait_ge(dve_step.sem, c)
            then(nc.vector.tensor_tensor(gsel1[:], gsc1[:, :, 0:E1 // 4], gre1[:, :, 0:E1 // 4], ALU.not_equal))
            then(nc.vector.tensor_scalar(gsel1[:], gsel1[:], BIG, -BIG, ALU.mult, ALU.add))
            then(nc.vector.tensor_tensor(msk1[:, 0].rearrange("p b (g f) -> p (b g) f", f=4), four,
                                         gsel1[:].rearrange("p b g -> p (b g)").unsqueeze(2).broadcast_to([P, B * E1 // 4, 4]),
                                         ALU.add))
            for b in range(B):
                then(nc.vector.max(top1[:, 2 + b, :], msk1[:, 0, b, :]))
                then(nc.vector.memset(top1[:, 2 + b, 6:8], -BIG))
                c = dve_step(nc.vector.match_replace(msk1[:, 1, b, :], top1[:, 2 + b, :], msk1[:, 0, b, :], -BIG))
            dve.wait_ge(dve_step.sem, c)
            then(nc.vector.tensor_tensor(msk1[:, 1], msk1[:, 0], msk1[:, 1], ALU.not_equal))
            nc.vector.tensor_tensor(comb[:], msk1[:, 1], sc1[:, 1], ALU.mult).then_inc(comb_ready, 1)

            def products6(step, e):
                for b in range(B):
                    dve.wait_ge(silu6_done, B * step + b + 1)
                    if e is None:
                        last = nc.vector.tensor_tensor(h6[:, b, IT * M1 - SHW:IT * M1], ps[2 * b + 1][:, 0:SHW],
                                                       sg6[:, b, :], ALU.mult)
                    else:
                        chunk, first = e
                        for j in range(CH):
                            last = nc.vector.scalar_tensor_tensor(
                                out=h6[:, b, chunk * CW + j * M1:chunk * CW + (j + 1) * M1],
                                in0=ps[2 * b + 1][:, j * M1:(j + 1) * M1], scalar=comb[:, b, column(first + j)],
                                in1=sg6[:, b, j * M1:(j + 1) * M1], op0=ALU.mult, op1=ALU.mult)
                    last.then_inc(h6_ready, 1)

            def turned6(step, n):
                dve.wait_ge(t6_done, B * step + 2)
                nc.vector.tensor_copy(hT6[:, 1, 0:n, :].rearrange("p k t -> p (k t)"), ps[5][:, 0:n * P])\
                    .then_inc(hT6_ready[1], 1)

            products6(0, None)
            dve.wait_ge(comb_ready, 1)
            products6(1, (0, 0))
            turned6(0, SHW // P)
            with dve.Fori(0, E1 // IT - 1) as i:
                for c in range(NCH):
                    products6(NCH * i + c + 2, ((c + 1) % NCH, IT * i + CH * (c + 1)))
                    turned6(NCH * i + c + 1, BLOCKS[c][1] - BLOCKS[c][0])
            for c in range(NCH):
                if c < NCH - 1:
                    products6(E1 // CH - NCH + c + 2, (c + 1, E1 - IT + CH * (c + 1)))
                turned6(E1 // CH - NCH + c + 1, BLOCKS[c][1] - BLOCKS[c][0])
            add_to_x(9)

        @block.tensor
        def _(pe):
            mm, tr = nc.tensor.matmul, nc.tensor.transpose

            def transpose_tokens(dst):
                for k in range(KD):
                    for b in range(B):
                        last = tr(dst[:, (k * B + b) * P:(k * B + b + 1) * P], xn[:, b, k * P:(k + 1) * P], ident)
                last.then_inc(xT_done, 1)

            pe.wait_ge(in_consts, 16)
            pe.wait_ge(xn_ready, 1)
            transpose_tokens(SC[0])
            pe.wait_ge(xT_ready, 1)
            pe.wait_ge(in_wq, 16)
            for u in range(B * NKV):
                if u >= 2:
                    pe.wait_ge(q_biased, u - 1)
                for k in range(KD):
                    last = mm(SC[1 + u % 2][:], xnT[:, k, u // NKV * P:(u // NKV + 1) * P],
                              wq[:, k, u % NKV * GW:(u % NKV + 1) * GW], start=(k == 0), stop=(k == KD - 1))
                last.then_inc(q_done, 1)

            def key_chunks(g, b, kvh, chunks, first=False):
                pe.wait_ge(in_wkv, 16 * (kvh + 1))
                for t in chunks:
                    if isinstance(g, int) and g < B:
                        pe.wait_ge(in_ctx[b][t], 16)
                    if t >= 2:
                        pe.wait_ge(k_ready, NC * g + t - 1)
                    elif not first:
                        pe.wait_ge(v_ready, NC * (g - 1) + t + 3)
                    for k in range(KD):
                        last = mm(PR[t % 2][:], wkv[:, k * 2 * P:k * 2 * P + P], ctxT[:, b, k, t * GW:(t + 1) * GW],
                                  start=(k == 0), stop=(k == KD - 1))
                    last.then_inc(k_done, 1)

            def value_chunks(g, b, first=False):
                for t in range(NC):
                    if t < 2:
                        pe.wait_ge(k_ready, NC * g + t + 3)
                    else:
                        pe.wait_ge(v_ready, NC * g + t - 1)
                    for j in range(4):
                        for k in range(KD):
                            last = mm(PR[t % 2][:, j * P:(j + 1) * P], ctxT[:, b, k, (4 * t + j) * P:(4 * t + j + 1) * P],
                                      wkv[:, k * 2 * P + P:(k + 1) * 2 * P], start=(k == 0), stop=(k == KD - 1))
                    last.then_inc(v_done, 1)
                if not first:
                    pe.wait_ge(max_ready, g)
                if not (isinstance(g, int) and g < B):
                    pe.wait_ge(rden_ready, g - 1)
                for j in range(NT):
                    last = mm(MISC[:, j:j + 1], K2[:, j * P:(j + 1) * P], ones[:, 0:1], start=True, stop=True)
                last.then_inc(ksum_done, 1)

            def score_tile(g, b, kvh, j):
                if j == 0:
                    pe.wait_ge(k_ready, NC * (g + 1))
                if j >= 3:
                    pe.wait_ge(s_ready, g * NT + j - 2)
                mm(SC[j % 3][:], KT[b][:, j * P:(j + 1) * P], QT[:, b, kvh, :], start=True, stop=True).then_inc(s_done, 1)

            def value_tile(g, b, j):
                pe.wait_ge(exp_done, g * NT + j + 1)
                mm(PO[:], V[b][:, j, :], S[b][:, j, :], start=(j == 0), stop=(j == NT - 1))

            def transpose_maxima(g, b):
                pe.wait_ge(max_step, (g + 1) * (NT - 1))
                for h in range(GH):
                    last = tr(MISC[:, h * P:(h + 1) * P], M[b][:, h * P:(h + 1) * P], ident)
                last.then_inc(maxT_done, 1)

            def spread_maxima(g):
                pe.wait_ge(max_ready, g + 1)
                for h in range(GH):
                    last = mm(MB[:, h * P:(h + 1) * P], mq[:, h:h + 1].broadcast_to([P, P]), ident, start=True, stop=True)
                last.then_inc(mb_done, 1)

            def denominators(g, b):
                pe.wait_ge(psum_step, (g + 1) * (NT - 1))
                mm(MISC[:], ones[:], psums[b][:], start=True, stop=True).then_inc(den_done, 1)

            def half(n, b, kvh, scores=True, pv=True, keys=True):
                for j in range(NT):
                    if scores:
                        score_tile(n + 1, 1 - b, kvh + b, j)
                    if pv:
                        value_tile(n, b, j)
                if keys:
                    key_chunks(n + 2, b, kvh + 1, range(0, 1))
                if scores:
                    transpose_maxima(n + 1, 1 - b)
                if keys:
                    key_chunks(n + 2, b, kvh + 1, range(1, 2))
                if scores:
                    spread_maxima(n + 1)
                if pv:
                    denominators(n, b)
                if keys:
                    key_chunks(n + 2, b, kvh + 1, range(2, NC))
                    value_chunks(n + 2, b)

            key_chunks(0, 0, 0, range(NC), first=True)
            value_chunks(0, 0, first=True)
            for u in range(B * NKV):
                if u == 0:
                    pe.wait_ge(v_ready, NC)
                if u % NKV == 0:
                    pe.wait_ge(q_scaled, u // NKV + 1)
                if u >= 2:
                    pe.wait_ge(qT_ready, u - 1)
                for h in range(GH):
                    last = tr(PR[u % 2][:, h * P:(h + 1) * P], q_tok[:, u // NKV, u % NKV * GH + h, :], ident)
                last.then_inc(qT_done, 1)
            pe.wait_ge(qT_ready, B * NKV)
            half(-1, 1, -1, pv=False)
            with pe.Fori(0, NKV - 1) as i:
                half(2 * i, 0, i)
                half(2 * i + 1, 1, i)
            half(NG - 2, 0, NKV - 1, keys=False)
            pe.wait_ge(o_ready, NG - 1)
            half(NG - 1, 1, NKV - 1, scores=False, keys=False)

            pe.wait_ge(in_wo, 16)
            pe.wait_ge(o_ready, NG)
            for b in range(B):
                for h in range(NH):
                    last = mm(ps[b][:, 0:D], QT[:, b, h // GH, h % GH * P:(h % GH + 1) * P], wo[:, h, :],
                              start=(h == 0), stop=(h == NH - 1))
                last.then_inc(proj_done, 1)

            def turn(src, n):
                pe.wait_ge(xn_ready, n)
                for k in range(KD):
                    for b in range(B):
                        last = tr(ps[2][:, (k * B + b) * P:(k * B + b + 1) * P], src[:, b, k * P:(k + 1) * P], ident)
                last.then_inc(xT_done, 1)
                pe.wait_ge(xT_ready, n)

            def over_tokens(dst, b, weights):
                for k in range(KD):
                    last = mm(dst, xnT[:, k, b * P:(b + 1) * P], weights[:, k, :], start=(k == 0), stop=(k == KD - 1))
                return last

            turn(hx, 2)
            pe.wait_ge(in_w2, 32)
            for b in range(B):
                over_tokens(ps[b][:], b, wqkv[:, :, 0:2 * D]).then_inc(qkv_done, 1)
                over_tokens(ps[3 + b][:, 0:D], b, wqkv[:, :, 2 * D:3 * D]).then_inc(qkv_done, 1)
            pe.wait_ge(in_lin, 32)
            pe.wait_ge(csum_ready, B * KD)
            for m in range(KD):
                for k in range(KD):
                    last = mm(ps[7][:, m * B:(m + 1) * B], win[:, k, m * P:(m + 1) * P], csum[:, k, :],
                              start=(k == 0), stop=(k == KD - 1))
            last.then_inc(lin_done, 1)
            for b in range(B):
                pe.wait_ge(wv_ready, b + 1)
                mm(ps[5 + b][:], tri, ww[:, b, :], start=True, stop=True).then_inc(cum_done, 1)
            pe.wait_ge(lin_ready, 1)
            for b in range(B):
                for k in range(KD):
                    last = mm(ps[7][:, b * D:(b + 1) * D], lin[:, 2, k, b:b + 1].broadcast_to([P, P]), wlin[:, k, :],
                              start=(k == 0), stop=(k == KD - 1))
            last.then_inc(lin_done, 1)
            turn(yt, 3)
            pe.wait_ge(in_wsw, 16)

            def swiglu_out(f):
                pe.wait_ge(sw_ready, f + 1)
                for b in range(B):
                    last = mm(ps[5 + b][:, 0:D], hsw[:, f, b * P:(b + 1) * P], wout[:, f, :],
                              start=(f == 0), stop=(f == FB - 1))
                    if f == FB - 1:
                        last.then_inc(proj_done, 1)

            for f in range(FB):
                if f >= 4:
                    pe.wait_ge(sw_ready, f - 3)
                for i in range(2):
                    for k in range(KD):
                        last = mm(ps[SW[f % 4]][:, i * D:(i + 1) * D], wsw[:, k, i * FF + f * P:i * FF + (f + 1) * P],
                                  xnT[:, k, :], start=(k == 0), stop=(k == KD - 1))
                last.then_inc(sw_done, 1)
                if f >= 2:
                    swiglu_out(f - 2)
            swiglu_out(FB - 2)
            swiglu_out(FB - 1)

            turn(xn, 4)
            pe.wait_ge(in_rows, 64)
            for b in range(B):
                last = over_tokens(ps[0][:, b * E0:(b + 1) * E0], b, router0)
            last.then_inc(r0_done, 1)
            pe.wait_ge(in_e0, 32)

            def gate_up0(e, par, b):
                over_tokens(ps[1 + 2 * par + b][:], b, w0[:, e]).then_inc(gu0_done, 1)

            def step0(e, par, first=False, more=True):
                if more:
                    if not first:
                        pe.wait_ge(h0_ready, B * e)
                    gate_up0(e + 1, 1 - par, 0)
                pe.wait_ge(h0_ready, B * (e + 1))
                if not first:
                    pe.wait_ge(hT0_ready, e)
                for k in range(KD):
                    for b in range(B):
                        last = tr(ps[5][:, (k * B + b) * P:(k * B + b + 1) * P], h0[:, par, b, k * P:(k + 1) * P], ident)
                last.then_inc(t0_done, 1)
                if more:
                    gate_up0(e + 1, 1 - par, 1)
                pe.wait_ge(hT0_ready, e + 1)
                for b in range(B):
                    for k in range(KD):
                        last = mm(ps[6 + b][:, 0:D], hT0[:, k, b, :], d0[:, e, k, :], start=(first and k == 0),
                                  stop=(not more and k == KD - 1), skip_group_check=True)
                    if not more:
                        last.then_inc(proj_done, 1)

            for b in range(B):
                gate_up0(0, 0, b)
            step0(0, 0, first=True)
            with pe.Fori(0, 3) as i:
                step0(2 * i + 1, 1)
                step0(2 * i + 2, 0)
            step0(E0 - 1, 1)
            step0(E0, 0, more=False)

            turn(xn, 5)
            pe.wait_ge(in_kv5, 16)

            def project5(m, weights):
                if m >= 2:
                    b, c = divmod(m - 2, 6)
                    if c == 1:
                        pe.wait_ge(v5_ready, b + 1)
                    else:
                        pe.wait_ge(rope_mul, b * (NKV + 1) + (c if c == 0 else c - 1) + 1)
                over_tokens(ps[m % 2][:], m // 6, weights).then_inc(p5_done, 1)

            def turn5(r):
                pe.wait_ge(rope_ready, r + 1)
                if r:
                    pe.wait_ge(t5_ready, r)
                for h in range(GH):
                    last = tr(ps[2][:, h * P:(h + 1) * P], rope[:, r % 2, h, :], ident)
                last.then_inc(t5_done, 1)

            for s in range(B * NKV + 3):
                b, c = divmod(s, NKV)
                if s < B * NKV:
                    if c == 0:
                        project5(6 * b, wkv5[:, :, 0:GW])
                        project5(6 * b + 1, wkv5[:, :, GW:2 * GW])
                    if s == 0:
                        pe.wait_ge(in_w5, 32)
                    project5(6 * b + 2 + c, wq5[:, :, c * GW:(c + 1) * GW])
                u = s - 1
                if 0 <= u < B * NKV:
                    if u % NKV == 0:
                        turn5(rope_at(u) - 1)
                    turn5(rope_at(u))
                u = s - 3
                if 0 <= u:
                    pe.wait_ge(o5_ready, u + 1)
                    for h in range(GH):
                        last = mm(ps[6 + u // NKV][:, 0:D], OT5[:, h, :], wo5[:, u % NKV * GH + h, :],
                                  start=(u % NKV == 0 and h == 0), stop=(u % NKV == NKV - 1 and h == GH - 1))
                    if u % NKV == NKV - 1:
                        last.then_inc(proj_done, 1)
                u = s - 2
                if 0 <= u < B * NKV:
                    pe.wait_ge(norm5, u + 1)
                    if u:
                        pe.wait_ge(pT5_ready, u)
                    for h in range(GH):
                        last = tr(ps[3][:, h * P:(h + 1) * P], P5[:, u % 2, h, :], ident)
                    last.then_inc(pT5_done, 1)
                u = s - 1
                if 0 <= u < B * NKV:
                    pe.wait_ge(t5_ready, rope_at(u) + 1)
                    if u:
                        pe.wait_ge(soft5, u)
                    for h in range(GH):
                        last = mm(ps[4][:, h * P:(h + 1) * P], QT5[u % 2][:, h, :], KT5[:, u // NKV, u % NKV, :],
                                  start=True, stop=True)
                    last.then_inc(s5_done, 1)
                u = s - 2
                if 0 <= u < B * NKV:
                    pe.wait_ge(pT5_ready, u + 1)
                    pe.wait_ge(v5_ready, u // NKV + 1)
                    if u:
                        pe.wait_ge(o5_ready, u)
                    mm(ps[5][:], V5[:, u // NKV, u % NKV, :], PT5[:].rearrange("p h t -> p (h t)"), start=True,
                       stop=True).then_inc(o5_done, 1)

            turn(xn, 6)
            for b in range(B):
                last = over_tokens(ps[4][:, b * E1:(b + 1) * E1], b, router1)
            last.then_inc(r1_done, 1)

            def gate_up6(step, b, weights, width, first=False):
                if not first:
                    pe.wait_ge(h6_ready, B * (step - 1) + b + 1)
                for i in range(2):
                    last = over_tokens(ps[2 * b + i][:, 0:width], b, weights[:, :, i * width:(i + 1) * width])
                last.then_inc(gu6_done, 1)

            def step6(step, blocks, down, ready, following=None, first=False, last_=False):
                if following:
                    c, turn_ = following
                    pe.wait_ge(in_gu[c], 16 * (turn_ + 1))
                    gate_up6(step + 1, 0, gu1[c], CW)
                pe.wait_ge(h6_ready, B * (step + 1))
                n = len(blocks)
                for b in range(B):
                    for k, blk in enumerate(blocks):
                        last = tr(ps[4 + b][:, k * P:(k + 1) * P], h6[:, b, blk * P:(blk + 1) * P], ident)
                    last.then_inc(t6_done, 1)
                if following:
                    gate_up6(step + 1, 1, gu1[c], CW)
                ready()
                for b in range(B):
                    pe.wait_ge(hT6_ready[b], step + 1)
                    for k in range(n):
                        last = mm(ps[6 + b][:, 0:D], hT6[:, b, k, :], down[:, k, :], start=(first and k == 0),
                                  stop=(last_ and k == n - 1), skip_group_check=True)
                    if last_:
                        last.then_inc(proj_done, 1)
                if not last_:
                    last.then_inc(d6_done, 1)

            def routed_step(step, c, turn_, following, last_=False):
                lo, hi = BLOCKS[c]
                step6(step, range(lo, hi), dn1[:, lo:hi], lambda: pe.wait_ge(in_dn[c], 16 * (turn_ + 1)), following,
                      last_=last_)

            pe.wait_ge(in_sh, 32)
            for b in range(B):
                gate_up6(0, b, gush, SHW, first=True)
            pe.wait_ge(exp1_done, 1)
            step6(0, range(NB - SHW // P, NB), dnsh, lambda: None, (0, 0), first=True)
            with pe.Fori(0, E1 // IT - 1) as i:
                for c in range(NCH):
                    routed_step(NCH * i + c + 1, c, i, (c + 1, i) if c < NCH - 1 else (0, i + 1))
            for c in range(NCH):
                routed_step(E1 // CH - NCH + c + 1, c, E1 // IT - 1, (c + 1, E1 // IT - 1) if c < NCH - 1 else None,
                            last_=(c == NCH - 1))


def _blocks(w):
    k, n = w.shape
    return w.reshape(k // P, P, n).transpose(1, 0, 2)


def _constants():
    import numpy as np
    i = np.arange(P)
    ident = np.eye(P, dtype=np.float32)
    tri = (i[:, None] <= i[None, :]).astype(np.float32)
    causal = np.where(i[None, :] <= i[:, None], 0.0, -1e30).astype(np.float32)
    fraction = np.arange(0, P, 2, dtype=np.float32) / np.float32(P)
    angle = i[:, None].astype(np.float32) / (np.float32(10000.0) ** fraction)[None, :]
    cos, sin = np.cos(angle), np.sin(angle)
    return np.stack([ident, tri, causal, np.concatenate([cos, cos], 1), np.concatenate([-sin, sin], 1)], 1)


def _layout(i):
    import numpy as np
    c = lambda v, *s: np.ascontiguousarray(v).reshape(*s)
    wk = _blocks(i["L0_xattn_Wk"]).reshape(P, KD, NKV, P)
    wv = _blocks(i["L0_xattn_Wv"]).reshape(P, KD, NKV, P)
    wkv = np.stack([wk, wv], 3).transpose(0, 2, 1, 3, 4).reshape(P, NKV, KD * 2 * P)
    bk = i["L0_xattn_bk"].reshape(NKV, P).T[:, :, None]
    zeros = np.zeros((P, 2), np.float32)
    decay = np.broadcast_to(i["L1_xattn_decay"].reshape(1, 1), (P, 1))
    b_in = i["L1_xattn_b_in"].reshape(KD, P).T
    experts0 = [(i["L0_ffn_shared_gate_w"], i["L0_ffn_shared_up_w"], i["L0_ffn_shared_down_w"])]
    experts0 += [(i["L0_ffn_gate_w"][e], i["L0_ffn_up_w"][e], i["L0_ffn_down_w"][e]) for e in range(E0)]
    gu1 = [np.concatenate([_blocks(np.concatenate(list(i[n][CH * c:CH * c + CH]), 1))
                           for n in ("L1_ffn_gate_w", "L1_ffn_up_w")], 2).reshape(P, -1) for c in range(E1 // CH)]
    pad = lambda w: np.pad(w, ((0, 0), (0, SHW - w.shape[1])))
    return {
        "x": c(i["x"].transpose(1, 0, 2), P, B * D),
        "consts": c(_constants(), P, 5 * P),
        "ctxT": c(i["ctx_2048"].transpose(2, 0, 1).reshape(KD, P, B, SE).transpose(1, 2, 0, 3), P, B, KD, SE),
        "maskT": c(i["mask_1xSxS2_ff0"][0].T.reshape(NT, P, P).transpose(1, 0, 2), P, NT * P),
        "wq": c(_blocks(i["L0_xattn_Wq"]), P, KD * NH * P),
        "bq": c(i["L0_xattn_bq"], 1, NH * P),
        "wkv": c(np.concatenate([wkv, bk], 2), P, NKV, KD * 2 * P + 1),
        "bv": c(i["L0_xattn_bv"], 1, NKV * P),
        "wo": c(_blocks(i["L0_xattn_Wo"]), P, NH * D),
        "cols": c(np.concatenate([i["L0_xattn_qn_w"][:, None], i["L0_xattn_kn_w"][:, None], b_in, decay, zeros,
                                  zeros[:, :1]], 1), P, 8),
        "wqkv": c(_blocks(i["L0_attn_w_qkv"].T), P, KD * 3 * D),
        "wsw": c(_blocks(i["L0_attn_w_swiglu"].T), P, KD * 2 * FF),
        "wout": c(_blocks(i["L0_attn_w_out"].T), P, FB * D),
        "w0": c(np.stack([_blocks(np.concatenate([g, u], 1)) for g, u, _ in experts0], 1), P, (E0 + 1) * KD * 2 * D),
        "d0": c(np.stack([_blocks(d) for _, _, d in experts0], 1), P, (E0 + 1) * KD * D),
        "router0": c(_blocks(i["L0_ffn_router_w"]), P, KD * E0),
        "win": c(_blocks(i["L1_xattn_W_in"].T), P, KD * D),
        "wlin": c(_blocks(i["L1_xattn_W_out"].T), P, KD * D),
        "rows": c(np.concatenate([i["L1_xattn_b_out"], i["L1_xattn_gamma"], i["L1_xattn_beta"]]), 1, 3 * D),
        "wq5": c(_blocks(i["L1_attn_q_kernel"]), P, KD * NH * P),
        "wkv5": c(_blocks(np.concatenate([i["L1_attn_k_kernel"], i["L1_attn_v_kernel"]], 1)), P, KD * 2 * NKV * P),
        "wo5": c(_blocks(i["L1_attn_out_kernel"]), P, NH * D),
        "router1": c(_blocks(i["L1_ffn_w_router"]), P, KD * E1),
        "bias1": c(i["L1_ffn_corr_bias"], 1, E1),
        "gu1": c(np.stack(gu1, 1), P, E1 // CH, KD * 2 * CW),
        "down1": c(_blocks(i["L1_ffn_down_w"].reshape(E1 * M1, D)), P, E1 * M1 // P, D),
        "gush": c(np.concatenate([_blocks(pad(i["L1_ffn_sh_gate_w"])), _blocks(pad(i["L1_ffn_sh_up_w"]))], 2),
                  P, KD * 2 * SHW),
        "downsh": c(_blocks(np.pad(i["L1_ffn_sh_down_w"], ((0, SHW - 352), (0, 0)))), P, SHW // P * D),
    }


def kernel(**inputs):
    import numpy as np
    import concourse.bacc as bacc
    from concourse.bass_utils import run_bass_kernel_spmd

    arrays = {f"in_{n}": v for n, v in _layout({k: np.asarray(v) for k, v in inputs.items()}).items()}
    nc = bacc.Bacc("TRN2", target_bir_lowering=False, num_devices=1)
    aps = {n[3:]: nc.dram_tensor(n, v.shape, mybir.dt.from_np(v.dtype), kind="ExternalInput").ap()
           for n, v in arrays.items()}
    out = nc.dram_tensor("out_x", (P, B * D), F32, kind="ExternalOutput").ap()
    perceiver(nc, aps, out)
    r = run_bass_kernel_spmd(nc, [arrays], core_ids=[0])
    return r.results[0]["out_x"].reshape(P, B, D).transpose(1, 0, 2)
```

```python
from contextlib import ExitStack

import concourse.bass as bass
from concourse import mybir
from concourse.alu_op_type import AluOpType as ALU

F32 = mybir.dt.float32
F32R = mybir.dt.float32r
ACT = mybir.ActivationFunctionType
AX = mybir.AxisListType

P = 128
B = 2
D = 256
KD = D // P
NH, NKV = 16, 4
GH = NH // NKV
GW = GH * P
SE = 2048
NT = SE // P
NG = NKV * B
NC = SE // GW
FF = 1024
FB = FF // P
E0 = 8
E1, M1 = 32, 176
CH = 2
CW = CH * M1
IT = 8
NCH = IT // CH
BLOCKS = [(0, 2), (2, 5), (5, 8), (8, 11)]
SHW = 384
NB = IT * M1 // P
BIG = 3.0e38
SCALE = float(P) ** -0.5

KB = 1024
AT_CTX = 0
AT_S0 = 32 * KB
AT_S1 = 64 * KB
AT_V = 96 * KB
AT_QH = 128 * KB
AT_QL = 144 * KB
AT_MASK = 160 * KB
AT_K2 = 168 * KB
AT_M = 176 * KB
AT_SMALL = 186 * KB



SW = (0, 1, 3, 4)


def rope_at(u):
    return u + u // NKV + 1


def column(e):
    return bass.ds(e, 1) if not isinstance(e, int) else slice(e, e + 1)


def perceiver(nc, a, out, last_stage=6):
    ctx = ExitStack()
    base = (nc.sbuf_base + 31) // 32 * 32
    small = [AT_SMALL]

    def at(name, shape, offset, dtype=F32):
        n = 4
        for s in shape[1:]:
            n *= s
        assert base + offset + n <= nc.sbuf_usable_end, name
        return nc.alloc_sbuf_tensor_at(name, shape, dtype, offset=base + offset)

    def sb(name, *shape):
        t = at(name, [P, *shape], small[0])
        n = 4
        for s in shape:
            n *= s
        small[0] += (n + 31) // 32 * 32
        return t

    def sem(name):
        return ctx.enter_context(nc.semaphore(name))

    class Steps:

        def __init__(self, name):
            self.sem, self.n = sem(name), 0

        def __call__(self, ins):
            ins.then_inc(self.sem, 1)
            self.n += 1
            return self.n

    with ctx:
        ctxT = at("ctxT", [P, B, KD, SE], AT_CTX)
        S = at("S", [P, NT, GW], AT_S0)
        q_tok = at("q_tok", [P, B, NH, P], AT_S0)
        cdec = at("cdec", [P, SE], AT_S0 + 16 * KB)
        cprod = at("cprod", [P, SE], AT_S0 + 24 * KB)
        KH, KL = ([at(f"{n}{i}", [P, SE], AT_S1 + (2 * i + j) * 8 * KB, F32R) for i in range(2)]
                  for j, n in enumerate(("KH", "KL")))
        wq = at("wq", [P, KD, NH * P], AT_S1 + 16 * KB)
        V = [at(f"V{i}", [P, NT, P], AT_V + 2 * i * 8 * KB) for i in range(2)]
        K = at("K", [P, SE], AT_V + 8 * KB)
        bq = at("bq", [P, NH * P], AT_V + 16 * KB)
        qsq = at("qsq", [P, 2, GW], AT_V + 24 * KB)
        K2 = at("K2", [P, SE], AT_K2)
        QH = at("QH", [P, B, NKV, GW], AT_QH, F32R)
        QL = at("QL", [P, B, NKV, GW], AT_QL, F32R)
        OT = at("OT", [P, B, NKV, GW], AT_QH)
        maskT = at("maskT", [P, NT, P], AT_MASK)
        M = [at(f"M{i}", [P, GW], AT_M + i * 2 * KB) for i in range(2)]
        psums = [at(f"psums{i}", [P, GW], AT_M + (2 + i) * 2 * KB) for i in range(2)]
        rden = at("rden", [P, GW], AT_M + 8 * KB)
        wo = at("wo", [P, NH, D], AT_CTX)
        wqkv = at("wqkv", [P, KD, 3 * D], AT_CTX + 16 * KB)
        wout = at("wout", [P, FB, D], AT_CTX + 22 * KB)
        wsw = at("wsw", [P, KD, 2 * FF], AT_S1)
        hsw = at("hsw", [P, FB, D], AT_S1 + 16 * KB)
        ww = at("ww", [P, B, 2 * D], AT_S1 + 24 * KB)
        w0 = at("w0", [P, E0 + 1, KD, 2 * D], AT_V)
        d0 = at("d0", [P, E0 + 1, KD, D], AT_S0)
        wq5 = at("wq5", [P, KD, NH * P], AT_CTX)
        wo5 = at("wo5", [P, NH, D], AT_CTX + 16 * KB)
        wkv5 = at("wkv5", [P, KD, 2 * NKV * P], AT_QL)

        hx = at("hx", [P, B, D], AT_MASK)
        yt = at("yt", [P, B, D], AT_MASK + 2 * KB)
        eq = at("eq", [P, B, D], AT_MASK + 4 * KB)
        yden = at("yden", [P, B, D], AT_MASK + 6 * KB)
        sq = at("sq", [P, 4, D], AT_MASK + 8 * KB)
        win = at("win", [P, KD, D], AT_CTX + 30 * KB)
        wlin = at("wlin", [P, KD, D], AT_S1 + 28 * KB)
        ssw = at("ssw", [P, 2, D], AT_QL + 8 * KB)
        sg0 = at("sg0", [P, 2, B, D], AT_QL + 10 * KB)
        hT0 = at("hT0", [P, KD, B, P], AT_QL + 14 * KB)
        h0 = at("h0", [P, 2, B, D], AT_M)
        rc = at("rc", [P, 2, GH, P], AT_S0)
        rs = at("rs", [P, 2, GH, P], AT_S0 + 4 * KB)
        rope = at("rope", [P, 2, GH, P], AT_S0 + 8 * KB)
        KT5 = at("KT5", [P, B, NKV, P], AT_S0 + 12 * KB)
        V5 = at("V5", [P, B, NKV, P], AT_S0 + 16 * KB)
        QT5 = [at(f"QT5{i}", [P, GH, P], AT_S0 + (20 + 2 * i) * KB) for i in range(2)]
        P5 = at("P5", [P, 2, GH, P], AT_S0 + 24 * KB)
        PT5 = at("PT5", [P, GH, P], AT_S0 + 28 * KB)
        OT5 = at("OT5", [P, GH, P], AT_S0 + 30 * KB)
        gu1 = [at(f"gu1{c}", [P, KD, 2 * CW], AT_S1 + c * 5632) for c in range(NCH)]
        dn1 = at("dn1", [P, NB, D], AT_S1 + 22 * KB)
        gush = at("gush", [P, KD, 2 * SHW], AT_S1 + 33 * KB)
        dnsh = at("dnsh", [P, SHW // P, D], AT_S1 + 39 * KB)
        h6 = at("h6", [P, B, IT * M1], AT_S1 + 42 * KB)
        sg6 = at("sg6", [P, B, SHW], AT_S1 + 53 * KB)
        hT6 = at("hT6", [P, B, 3, P], AT_S1 + 56 * KB)

        late_at = [AT_M + 4 * KB]

        def late(name, *shape):
            t = at(name, [P, *shape], late_at[0])
            n = 4
            for s in shape:
                n *= s
            late_at[0] += (n + 31) // 32 * 32
            assert late_at[0] <= AT_SMALL
            return t

        nmax5 = late("nmax5", 2, GH * B * NKV)
        sum5 = late("sum5", 2, GH * B * NKV)
        sc1 = late("sc1", 3, B, E1)
        pair1 = late("pair1", 2, B * E1 // 4, 2)
        grp1 = late("grp1", 3, B * E1 // 4)
        gre1 = late("gre1", B, 16)
        top1 = late("top1", 4, 8)
        gsel1 = late("gsel1", B, E1 // 4)
        msk1 = late("msk1", 2, B, E1)
        comb = late("comb", B, E1)
        summ = late("summ", B, D)
        lin = late("lin", 3, KD, B)
        ssq = late("ssq", 4)
        nrstd = late("nrstd", 4)
        r0m = late("r0m", 4, B)
        r0s = late("r0s", B)

        x = sb("xres", B, D)
        xn = sb("xn", B, D)
        xnT = sb("xnT", KD, B * P)
        consts = sb("consts", 5, P)
        ident, tri, causal, cosT, sinT = (consts[:, i, :] for i in range(5))
        ones = sb("ones", P)
        wkv = sb("wkv", KD * 2 * P + 1)
        bv = sb("bv", NKV)
        cols = sb("cols", 8)
        stats = sb("stats", B, 6)
        mv = sb("mv", B, 2)
        var = sb("var", 32)
        rstd = sb("rstd", 32)
        kvar = sb("kvar", 2, NT)
        krstd = sb("krstd", 2, NT)
        halfneg = sb("halfneg", 32)
        qkn = sb("qkn", 1)
        qss = sb("qss", B, NH)
        mq = sb("mq", GH)
        sig = sb("sig", 4)
        csum = sb("csum", KD, B)
        rows = sb("rows", 3, D)
        warm = sb("warm", 1)
        router0 = sb("router0", KD, E0)
        router1 = sb("router1", KD, E1)
        r0 = sb("r0", 4, B, E0)
        sel0 = sb("sel0", B, E0 + 1)
        order = sb("order", E0)
        bias1 = sb("bias1", E1)
        gsc1 = sb("gsc1", B, 16)

        ps = [ctx.enter_context(nc.psum_tensor(f"ps{i}", [P, GW], F32)) for i in range(8)]
        SC = ps[0:3]
        PR = ps[3:5]
        QR = ps[0:5]
        MISC, MB, PO = ps[5], ps[6], ps[7]

        in_x, in_consts, in_cols, in_wq, in_bq, in_mask, in_bv = (
            sem(n) for n in ("in_x", "in_consts", "in_cols", "in_wq", "in_bq", "in_mask", "in_bv"))
        in_wkv = sem("in_wkv")
        in_ctx = [[sem(f"in_ctx{b}{c}") for c in range(NC)] for b in range(B)]
        consts_set = sem("consts_set")
        var_ready, rstd_ready = sem("var_ready"), sem("rstd_ready")
        xn_ready, xT_done, xT_ready = sem("xn_ready"), sem("xT_done"), sem("xT_ready")
        q_done, q_biased, q_squared, q_summed = (sem(n) for n in ("q_done", "q_biased", "q_squared", "q_summed"))
        q_var, q_rstd, q_scaled = sem("q_var"), sem("q_rstd"), sem("q_scaled")
        qT_done, qT_ready = sem("qT_done"), sem("qT_ready")
        k_done, k_ready, v_done, v_ready = (sem(n) for n in ("k_done", "k_ready", "v_done", "v_ready"))
        kl_ready, ql_ready = sem("kl_ready"), sem("ql_ready")
        ksum_done, kvar_ready, krstd_ready = sem("ksum_done"), sem("kvar_ready"), sem("krstd_ready")
        s_done, s_ready, max_step = sem("s_done"), sem("s_ready"), sem("max_step")
        maxT_done, max_ready, mb_done = sem("maxT_done"), sem("max_ready"), sem("mb_done")
        sub_done, exp_done, psum_step = sem("sub_done"), sem("exp_done"), sem("psum_step")
        pv_done, den_done, rden_ready, o_ready = (sem(n) for n in ("pv_done", "den_done", "rden_ready", "o_ready"))
        o_scaled = sem("o_scaled")
        exp_dec = sem("exp_dec")
        dve_step = Steps("dve_step")
        pool_step = Steps("pool_step")
        csum_ready = sem("csum_ready")
        in_w2, in_wsw, in_lin, in_e0, in_w5, in_kv5, in_sh, in_rows = (
            sem(n) for n in ("in_w2", "in_wsw", "in_lin", "in_e0", "in_w5", "in_kv5", "in_sh", "in_rows"))
        in_gu = [sem(f"in_gu{c}") for c in range(NCH)]
        in_dn = [sem(f"in_dn{c}") for c in range(NCH)]
        qkv_done, qk_squared, nrstd_ready, w_ready, eq_ready, wv_ready, cum_done = (
            sem(n) for n in ("qkv_done", "qk_squared", "nrstd_ready", "w_ready", "eq_ready", "wv_ready", "cum_done"))
        sw_done, sw_silu, sw_ready = sem("sw_done"), sem("sw_silu"), sem("sw_ready")
        lin_done, lin_ready = sem("lin_done"), sem("lin_ready")
        max0_ready, tanh0_ready = sem("max0_ready"), sem("tanh0_ready")
        r0_done, sel0_ready, gu0_done, silu0_done, h0_ready, t0_done, hT0_ready = (
            sem(n) for n in ("r0_done", "sel0_ready", "gu0_done", "silu0_done", "h0_ready", "t0_done", "hT0_ready"))
        p5_done, rope_mul, rope_ready, v5_ready, t5_done, t5_ready, s5_done = (
            sem(n) for n in ("p5_done", "rope_mul", "rope_ready", "v5_ready", "t5_done", "t5_ready", "s5_done"))
        soft5, exp5, norm5, pT5_done, pT5_ready, o5_done, o5_ready = (
            sem(n) for n in ("soft5", "exp5", "norm5", "pT5_done", "pT5_ready", "o5_done", "o5_ready"))
        r1_done, exp1_done, comb_ready, gu6_done, silu6_done, h6_ready, t6_done, d6_done = (
            sem(n) for n in ("r1_done", "exp1_done", "comb_ready", "gu6_done", "silu6_done", "h6_ready", "t6_done",
                             "d6_done"))
        hT6_ready = [sem("hT6_ready0"), sem("hT6_ready1")]
        in_wo = sem("in_wo")
        proj_done = sem("proj_done")
        out_stored = sem("out_stored")
        x_ready = sem("x_ready")

        block = ctx.enter_context(nc.Block())

        @block.sync
        def _(sp):
            sp.dma_start(x[:].rearrange("p b d -> p (b d)"), a["x"]).then_inc(in_x, 16)
            sp.dma_start(consts[:].rearrange("p b d -> p (b d)"), a["consts"]).then_inc(in_consts, 16)
            sp.dma_start(wq[:].rearrange("p k n -> p (k n)"), a["wq"]).then_inc(in_wq, 16)
            for c in range(NC):
                sp.dma_start(ctxT[:, 0, :, c * GW:(c + 1) * GW],
                             a["ctxT"][:, 0, :, c * GW:(c + 1) * GW]).then_inc(in_ctx[0][c], 16)
            sp.dma_start(maskT[:].rearrange("p t n -> p (t n)"), a["maskT"]).then_inc(in_mask, 16)
            for c in range(NC):
                sp.dma_start(ctxT[:, 1, :, c * GW:(c + 1) * GW],
                             a["ctxT"][:, 1, :, c * GW:(c + 1) * GW]).then_inc(in_ctx[1][c], 16)
            with sp.Fori(0, NKV - 1) as i:
                sp.wait_ge(ksum_done, 2 * i + 2)
                sp.dma_start(wkv[:], a["wkv"][:, i + 1, :]).then_inc(in_wkv, 16)
            sp.wait_ge(ksum_done, NG)
            sp.wait_ge(csum_ready, B * KD)
            sp.dma_start(wo[:].rearrange("p h d -> p (h d)"), a["wo"]).then_inc(in_wo, 16)
            sp.dma_start(wqkv[:].rearrange("p k n -> p (k n)"), a["wqkv"]).then_inc(in_w2, 16)
            sp.dma_start(wout[:].rearrange("p k n -> p (k n)"), a["wout"]).then_inc(in_w2, 16)
            sp.dma_start(win[:].rearrange("p k n -> p (k n)"), a["win"]).then_inc(in_lin, 16)
            sp.wait_ge(s_done, NG * NT)
            sp.dma_start(wlin[:].rearrange("p k n -> p (k n)"), a["wlin"]).then_inc(in_lin, 16)
            sp.dma_start(wsw[:].rearrange("p k n -> p (k n)"), a["wsw"]).then_inc(in_wsw, 16)
            sp.wait_ge(proj_done, 2)
            sp.dma_start(w0[:].rearrange("p e k n -> p (e k n)"), a["w0"]).then_inc(in_e0, 16)
            sp.dma_start(d0[:].rearrange("p e k n -> p (e k n)"), a["d0"]).then_inc(in_e0, 16)
            sp.wait_ge(proj_done, 4)
            sp.dma_start(wkv5[:].rearrange("p k n -> p (k n)"), a["wkv5"]).then_inc(in_kv5, 16)
            sp.dma_start(wq5[:].rearrange("p k n -> p (k n)"), a["wq5"]).then_inc(in_w5, 16)
            sp.dma_start(wo5[:].rearrange("p k n -> p (k n)"), a["wo5"]).then_inc(in_w5, 16)
            sp.wait_ge(proj_done, 6)
            sp.dma_start(gush[:].rearrange("p k n -> p (k n)"), a["gush"]).then_inc(in_sh, 16)
            sp.dma_start(dnsh[:].rearrange("p k n -> p (k n)"), a["downsh"]).then_inc(in_sh, 16)

            def load_chunk(c, turn):
                lo, hi = BLOCKS[c]
                sp.dma_start(gu1[c][:].rearrange("p k n -> p (k n)"),
                             a["gu1"].rearrange("p (i c) n -> p i c n", c=NCH)[:, turn, c, :]).then_inc(in_gu[c], 16)
                return (dn1[:, lo:hi, :], a["down1"].rearrange("p (i k) n -> p i k n", k=NB)[:, turn, lo:hi, :])

            for c in range(NCH):
                sp.dma_start(*load_chunk(c, 0)).then_inc(in_dn[c], 16)
            with sp.Fori(0, E1 // IT - 1) as i:
                for c in range(NCH):
                    sp.wait_ge(gu6_done, B * NCH * i + B * (c + 2))
                    down = load_chunk(c, i + 1)
                    sp.wait_ge(d6_done, NCH * i + c + 2)
                    sp.dma_start(*down).then_inc(in_dn[c], 16)
            for b in range(B):
                sp.wait_ge(x_ready, b + 1)
                sp.dma_start(out[:, b * D:(b + 1) * D], x[:, b, :]).then_inc(out_stored, 16)
            sp.wait_ge(out_stored, 16 * B)

        @block.gpsimd
        def _(pool):
            nc.gpsimd.memset(ones[:], 1.0)
            nc.gpsimd.memset(sel0[:, :, 0:1], 1.0)
            nc.gpsimd.memset(gsc1[:], -BIG)
            for e in range(E0):
                nc.gpsimd.memset(order[:, e:e + 1], float(E0 - e))
            nc.gpsimd.memset(halfneg[:], -0.5).then_inc(consts_set, 1)
            pool.wait_ge(consts_set, 1)

            def rsqrt(dst, src, n):
                return nc.gpsimd.tensor_tensor(dst, src, halfneg[:, 0:n], ALU.pow)

            pool.wait_ge(var_ready, 1)
            rsqrt(rstd[:, 0:B], var[:, 0:B], B).then_inc(rstd_ready, 1)
            pool.wait_ge(q_var, 1)
            rsqrt(rstd[:], var[:], B * NH).then_inc(q_rstd, 1)

            def key_norms(g, b):
                pool.wait_ge(kvar_ready, g + 1)
                rsqrt(krstd[:, b, :], kvar[:, b, :], NT).then_inc(krstd_ready, 1)

            def sum_probs(g, b, tiles):
                for j in tiles:
                    pool.wait_ge(exp_done, g * NT + j + 1)
                    if j > 1:
                        pool.wait_ge(psum_step, g * (NT - 1) + j - 1)
                    nc.gpsimd.tensor_tensor(psums[b][:], S[:, 0, :] if j == 1 else psums[b][:],
                                            S[:, j, :], ALU.add).then_inc(psum_step, 1)

            def key_lows(g, b):
                for t in range(NC):
                    pool.wait_ge(k_ready, NC * g + t + 1)
                    chunk = slice(t * GW, (t + 1) * GW)
                    nc.gpsimd.tensor_tensor(KL[b][:, chunk], K[:, chunk], KH[b][:, chunk].bitcast(F32),
                                            ALU.subtract).then_inc(kl_ready, 1)

            def half(n, b, scores=True, keys=True):
                if keys:
                    key_lows(n + 2, b)
                if scores:
                    sum_probs(n + 1, 1 - b, range(1, 9))
                if keys:
                    key_norms(n + 2, b)
                if scores:
                    sum_probs(n + 1, 1 - b, range(9, NT))

            key_lows(0, 0)
            key_norms(0, 0)
            half(-1, 1)
            with pool.Fori(0, NKV - 1) as i:
                half(2 * i, 0)
                half(2 * i + 1, 1)
            half(NG - 2, 0, keys=False)

            for n, width in ((2, 2), (3, 2), (4, 4), (5, 2), (6, 2), (7, 2), (8, 2)):
                pool.wait_ge(var_ready, n)
                rsqrt(rstd[:, 0:width], var[:, 0:width], width).then_inc(rstd_ready, 1)
            for r in range(B * (NKV + 1)):
                pool.wait_ge(rope_mul, r + 1)
                if r >= 2:
                    pool.wait_ge(t5_done, r - 1)
                nc.gpsimd.tensor_tensor(rope[:, r % 2], rc[:, r % 2], rs[:, r % 2], ALU.add).then_inc(rope_ready, 1)
            pool.wait_ge(var_ready, 9)
            rsqrt(rstd[:, 0:B], var[:, 0:B], B).then_inc(rstd_ready, 1)

        @block.scalar
        def _(act):
            act.dma_start(cols[:], a["cols"]).then_inc(in_cols, 16)
            act.dma_start(wkv[:], a["wkv"][:, 0, :]).then_inc(in_wkv, 16)
            act.dma_start(bq[:], a["bq"].broadcast_to([P, NH * P])).then_inc(in_bq, 16)
            act.dma_start(bv[:], a["bv"]).then_inc(in_bv, 16)
            act.dma_start(rows[:].rearrange("p g d -> p (g d)"), a["rows"].broadcast_to([P, 3 * D])).then_inc(in_rows, 16)
            act.dma_start(router0[:].rearrange("p k d -> p (k d)"), a["router0"]).then_inc(in_rows, 16)
            act.dma_start(router1[:].rearrange("p k d -> p (k d)"), a["router1"]).then_inc(in_rows, 16)
            act.dma_start(bias1[:], a["bias1"].broadcast_to([P, E1])).then_inc(in_rows, 16)
            act.wait_ge(in_cols, 16)
            nc.scalar.activation(sig[:, 0:1], cols[:, 4:5], ACT.Exp, scale=-1.0).then_inc(exp_dec, 1)
            for u in range(B * NKV):
                act.wait_ge(q_biased, u + 1)
                if u >= 2:
                    act.wait_ge(q_summed, u - 1)
                nc.scalar.activation(qsq[:, u % 2, :], q_tok[:, u // NKV, u % NKV * GH:(u % NKV + 1) * GH, :],
                                     ACT.Square).then_inc(q_squared, 1)

            bk = wkv[:, KD * 2 * P:KD * 2 * P + 1]

            def key_chunk(g, b, t):
                act.wait_ge(k_done, NC * g + t + 1)
                if not isinstance(g, int) or g:
                    act.wait_ge(kl_ready, NC * (g - 1) + t + 1)
                nc.scalar.activation(K[:, t * GW:(t + 1) * GW], PR[t % 2][:], ACT.Identity, bias=bk)
                nc.scalar.activation(KH[b][:, t * GW:(t + 1) * GW], PR[t % 2][:], ACT.Identity, bias=bk)
                nc.scalar.activation(K2[:, t * GW:(t + 1) * GW], PR[t % 2][:], ACT.Square,
                                     bias=bk).then_inc(k_ready, 1)

            def value_chunk(g, b, t):
                act.wait_ge(v_done, NC * g + t + 1)
                nc.scalar.activation(V[b][:, 4 * t:4 * t + 4, :].rearrange("p t d -> p (t d)"), PR[t % 2][:],
                                     ACT.Copy).then_inc(v_ready, 1)

            def outputs(g, b, kvh):
                act.wait_ge(o_scaled, g + 1)
                nc.scalar.activation(OT[:, b, kvh, :], OT[:, b, kvh, :], ACT.Identity,
                                     bias=bv[:, column(kvh)]).then_inc(o_ready, 1)

            def exps(g, b, tiles):
                for j in tiles:
                    act.wait_ge(sub_done, g * NT + j + 1)
                    nc.scalar.activation(S[:, j, :], S[:, j, :], ACT.Exp).then_inc(exp_done, 1)

            def half(n, b, kvh, scores=True, pv=True, keys=True):
                after = [0, 0, 0, 0, 1, 3, 5, 7, NT]
                for t in range(2 * NC):
                    if keys:
                        (key_chunk if t < NC else value_chunk)(n + 2, b, t % NC)
                    if t == NC - 1 and pv:
                        outputs(n, b, kvh)
                    if scores:
                        exps(n + 1, 1 - b, range(after[t], after[t + 1]))

            for t in range(NC):
                key_chunk(0, 0, t)
            for t in range(NC):
                value_chunk(0, 0, t)
            for u in range(B * NKV):
                act.wait_ge(qT_done, u + 1)
                nc.scalar.activation(QH[:, u // NKV, u % NKV, :], QR[u % len(QR)][:], ACT.Identity,
                                     scale=qkn[:, 0:1]).then_inc(qT_ready, 1)
            half(-1, 1, -1, pv=False)
            act.wait_ge(in_bv, 16)
            with act.Fori(0, NKV - 1) as i:
                half(2 * i, 0, i)
                half(2 * i + 1, 1, i)
            half(NG - 2, 0, NKV - 1, keys=False)
            half(NG - 1, 1, NKV - 1, scores=False, keys=False)

            def silu_tables():
                nc.scalar.activation(warm[:], ones[:, 0:1], ACT.Silu)

            for b in range(B):
                act.wait_ge(qkv_done, 2 * b + 1)
                for i in range(2):
                    nc.scalar.activation(sq[:, 2 * b + i, :], ps[b][:, i * D:(i + 1) * D], ACT.Square,
                                         accum_out=ssq[:, 2 * b + i:2 * b + i + 1]).then_inc(qk_squared, 1)
            act.wait_ge(rstd_ready, 4)
            for b in range(B):
                nc.scalar.activation(ww[:, b, D:2 * D], ps[b][:, D:2 * D], ACT.Exp,
                                     scale=rstd[:, 2 * b + 1:2 * b + 2]).then_inc(w_ready, 1)
            act.wait_ge(nrstd_ready, 1)
            for b in range(B):
                nc.scalar.activation(eq[:, b, :], ps[b][:, 0:D], ACT.Exp,
                                     scale=nrstd[:, 2 * b:2 * b + 1]).then_inc(eq_ready, 1)
            silu_tables()
            for f in range(FB):
                act.wait_ge(sw_done, f + 1)
                if f >= 2:
                    act.wait_ge(sw_ready, f - 1)
                nc.scalar.activation(ssw[:, f % 2, :], ps[SW[f % 4]][:, D:2 * D], ACT.Silu).then_inc(sw_silu, 1)

            def silu0(e, par, batches=range(B)):
                for b in batches:
                    act.wait_ge(gu0_done, B * e + b + 1)
                    nc.scalar.activation(sg0[:, par, b, :], ps[1 + 2 * par + b][:, 0:D], ACT.Silu,
                                         scale=sel0[:, b, column(e)]).then_inc(silu0_done, 1)

            def turned0(e):
                act.wait_ge(t0_done, e + 1)
                nc.scalar.activation(hT0[:].rearrange("p k b t -> p (k b t)"), ps[5][:], ACT.Copy).then_inc(hT0_ready, 1)

            act.wait_ge(max0_ready, 1)
            nc.scalar.activation(r0s[:], r0m[:, 0], ACT.Tanh, scale=0.5).then_inc(tanh0_ready, 1)
            def step0(e, par):
                silu0(e, par, range(1))
                turned0(e - 1)
                silu0(e, par, range(1, B))

            silu0(0, 0)
            act.wait_ge(sel0_ready, 1)
            step0(1, 1)
            with act.Fori(0, 3) as i:
                step0(2 * i + 2, 0)
                step0(2 * i + 3, 1)
            step0(E0, 0)
            turned0(E0)
            nc.scalar.activation(warm[:], ones[:, 0:1], ACT.Exp)

            def turned5(r, dst):
                act.wait_ge(t5_done, r + 1)
                nc.scalar.activation(dst, ps[2][:].rearrange("p (h t) -> p h t", h=GH), ACT.Copy).then_inc(t5_ready, 1)

            for s in range(B * NKV + 2):
                b, c = divmod(s, NKV)
                if s < B * NKV and c == 0:
                    act.wait_ge(p5_done, 6 * b + 2)
                    nc.scalar.activation(V5[:, b].rearrange("p g d -> p (g d)"), ps[1][:], ACT.Copy).then_inc(v5_ready, 1)
                u = s - 1
                if 0 <= u < B * NKV:
                    if u % NKV == 0:
                        turned5(rope_at(u) - 1, KT5[:, u // NKV])
                    turned5(rope_at(u), QT5[u % 2][:])
                if 0 <= s - 2:
                    act.wait_ge(pT5_done, s - 1)
                    nc.scalar.activation(PT5[:].rearrange("p h t -> p (h t)"), ps[3][:], ACT.Copy).then_inc(pT5_ready, 1)
                    act.wait_ge(o5_done, s - 1)
                    nc.scalar.activation(OT5[:].rearrange("p h t -> p (h t)"), ps[5][:], ACT.Copy).then_inc(o5_ready, 1)
                if 0 <= u < B * NKV:
                    act.wait_ge(soft5, u + 1)
                    for h in range(GH):
                        last = nc.scalar.activation(P5[:, u % 2, h, :], P5[:, u % 2, h, :], ACT.Exp,
                                                    bias=nmax5[:, 1, u * GH + h:u * GH + h + 1],
                                                    accum_out=sum5[:, 0, u * GH + h:u * GH + h + 1])
                    last.then_inc(exp5, 1)

            act.wait_ge(r1_done, 1)
            nc.scalar.activation(sc1[:, 0].rearrange("p b e -> p (b e)"), ps[4][:, 0:B * E1], ACT.Exp,
                                 scale=-1.0).then_inc(exp1_done, 1)
            silu_tables()

            def silu6(step, width, batches=range(B)):
                for b in batches:
                    act.wait_ge(gu6_done, B * step + b + 1)
                    nc.scalar.activation(sg6[:, b, 0:width], ps[2 * b][:, 0:width], ACT.Silu).then_inc(silu6_done, 1)

            def turned6(step, n):
                act.wait_ge(t6_done, B * step + 1)
                nc.scalar.activation(hT6[:, 0, 0:n, :].rearrange("p k t -> p (k t)"), ps[4][:, 0:n * P],
                                     ACT.Copy).then_inc(hT6_ready[0], 1)

            def step6(step, n, more=True):
                if more:
                    silu6(step + 1, CW, range(1))
                turned6(step, n)
                if more:
                    silu6(step + 1, CW, range(1, B))

            silu6(0, SHW)
            step6(0, SHW // P)
            with act.Fori(0, E1 // IT - 1) as i:
                for c in range(NCH):
                    step6(NCH * i + c + 1, BLOCKS[c][1] - BLOCKS[c][0])
            for c in range(NCH):
                step6(E1 // CH - NCH + c + 1, BLOCKS[c][1] - BLOCKS[c][0], more=c < NCH - 1)

        @block.vector
        def _(dve):
            def norm_stats(src, n):
                for b in range(B):
                    c = dve_step(nc.vector.bn_stats(stats[:, b, :], src[:, b, :]))
                dve.wait_ge(dve_step.sem, c)
                for b in range(B):
                    c = dve_step(nc.vector.bn_aggr(mv[:, b, :], stats[:, b, :]))
                dve.wait_ge(dve_step.sem, c)
                nc.vector.tensor_scalar(var[:, 0:B], mv[:, :, 1], 1e-5, None, ALU.add).then_inc(var_ready, 1)
                dve.wait_ge(rstd_ready, n)

            def normalise(dst, src, sem_, n):
                norm_stats(src, n)
                for b in range(B):
                    last = nc.vector.tensor_scalar(dst[:, b, :], src[:, b, :], mv[:, b, 0:1], rstd[:, b:b + 1],
                                                   ALU.subtract, ALU.mult)
                last.then_inc(sem_, 1)

            dve.wait_ge(in_x, 16)
            normalise(xn, x, xn_ready, 1)
            dve.wait_ge(xT_done, 1)
            nc.vector.tensor_copy(xnT[:].rearrange("p k n -> p (k n)"), SC[0][:]).then_inc(xT_ready, 1)
            dve.wait_ge(exp_dec, 1)
            dve.wait_ge(consts_set, 1)
            c = dve_step(nc.vector.tensor_scalar(sig[:, 1:2], sig[:, 0:1], 1.0, None, ALU.add))
            dve_step(nc.vector.tensor_tensor(qkn[:], cols[:, 0:1], cols[:, 1:2], ALU.mult))
            dve.wait_ge(dve_step.sem, c)
            c = dve_step(nc.vector.reciprocal(sig[:, 2:3], sig[:, 1:2]))
            dve.wait_ge(dve_step.sem, c)
            dve_step(nc.vector.tensor_scalar(qkn[:], qkn[:], SCALE, None, ALU.mult))
            c = dve_step(nc.vector.tensor_tensor_scan(cdec[:, ::-1], sig[:, 2:3].broadcast_to([P, SE]),
                                                      ones[:, 0:1].broadcast_to([P, SE]), 0.0, ALU.mult, ALU.add))
            dve.wait_ge(dve_step.sem, c)
            dve_step(nc.vector.reduce_sum(sig[:, 3:4], cdec[:], AX.X))

            dve.wait_ge(in_bq, 16)
            for u in range(B * NKV + 1):
                if u < B * NKV:
                    dve.wait_ge(q_done, u + 1)
                    nc.vector.tensor_tensor(q_tok[:, u // NKV, u % NKV * GH:(u % NKV + 1) * GH, :].rearrange("p h d -> p (h d)"),
                                            SC[1 + u % 2][:], bq[:, u % NKV * GW:(u % NKV + 1) * GW],
                                            ALU.add).then_inc(q_biased, 1)
                if u:
                    dve.wait_ge(q_squared, u)
                    v = u - 1
                    nc.vector.reduce_sum(qss[:, v // NKV, v % NKV * GH:(v % NKV + 1) * GH],
                                         qsq[:, v % 2, :].rearrange("p (h d) -> p h d", h=GH), AX.X).then_inc(q_summed, 1)
            dve.wait_ge(q_summed, B * NKV)
            nc.vector.tensor_scalar(var[:], qss[:].rearrange("p b h -> p (b h)"), 1.0 / P, 1e-6,
                                    ALU.mult, ALU.add).then_inc(q_var, 1)
            def context_sum(b):
                for t in range(NC):
                    dve.wait_ge(in_ctx[b][t], 16)
                for k in range(KD):
                    if b + k:
                        dve.wait_ge(csum_ready, b * KD + k)
                    nc.vector.tensor_tensor_reduce(cprod[:], ctxT[:, b, k, :], cdec[:], 1.0, 0.0, ALU.mult, ALU.add,
                                                   csum[:, k, b:b + 1]).then_inc(csum_ready, 1)

            context_sum(0)
            dve.wait_ge(q_rstd, 1)
            for b in range(B):
                nc.vector.tensor_tensor(q_tok[:, b, :, :], q_tok[:, b, :, :],
                                        rstd[:, b * NH:(b + 1) * NH].unsqueeze(2).broadcast_to([P, NH, P]),
                                        ALU.mult).then_inc(q_scaled, 1)
            context_sum(1)
            dve.wait_ge(csum_ready, B * KD)

            def key_vars(g, b):
                dve.wait_ge(ksum_done, g + 1)
                nc.vector.tensor_scalar(kvar[:, b, :], MISC[:, 0:NT], 1.0 / P, 1e-6, ALU.mult, ALU.add).then_inc(kvar_ready, 1)

            def running_max(g, b, j):
                dve.wait_ge(s_ready, g * NT + j + 1)
                if j > 1:
                    dve.wait_ge(max_step, g * (NT - 1) + j - 1)
                nc.vector.tensor_tensor(M[b][:], S[:, 0, :] if j == 1 else M[b][:], S[:, j, :],
                                        ALU.max).then_inc(max_step, 1)

            def score_tiles(g, b, first):
                dve.wait_ge(krstd_ready, g + 1)
                for j in range(NT):
                    dve.wait_ge(s_done, g * NT + j + 1)
                    if not first:
                        dve.wait_ge(psum_step, (g - 1) * (NT - 1) + max(j, 1))
                    nc.vector.scalar_tensor_tensor(
                        out=S[:, j, :].rearrange("p (h q) -> p h q", h=GH),
                        in0=SC[j % 3][:].rearrange("p (h q) -> p h q", h=GH), scalar=krstd[:, b, j:j + 1],
                        in1=maskT[:, j, :].unsqueeze(1).broadcast_to([P, GH, P]),
                        op0=ALU.mult, op1=ALU.add).then_inc(s_ready, 1)
                    if j >= 2:
                        running_max(g, b, j - 1)
                running_max(g, b, NT - 1)

            def reduce_maxima(g):
                dve.wait_ge(maxT_done, g + 1)
                nc.vector.reduce_max(mq[:], MISC[:].rearrange("p (h k) -> p h k", h=GH), AX.X).then_inc(max_ready, 1)

            def reciprocals(g):
                dve.wait_ge(den_done, g + 1)
                nc.vector.reciprocal(rden[:], MB[:]).then_inc(rden_ready, 1)

            def outputs(g, b, kvh):
                dve.wait_ge(rden_ready, g + 1)
                nc.vector.tensor_tensor(OT[:, b, kvh, :], PO[:], rden[:], ALU.mult).then_inc(o_scaled, 1)

            def subtract_maxima(g, b, tiles):
                dve.wait_ge(mb_done, g + 1)
                for j in tiles:
                    nc.vector.tensor_tensor(S[:, j, :], S[:, j, :], MB[:], ALU.subtract).then_inc(sub_done, 1)

            def half(n, b, kvh, scores=True, pv=True, keys=True):
                if scores:
                    score_tiles(n + 1, 1 - b, not pv)
                if pv:
                    reciprocals(n)
                if scores:
                    reduce_maxima(n + 1)
                if pv:
                    outputs(n, b, kvh)
                if scores:
                    subtract_maxima(n + 1, 1 - b, range(NT))
                if keys:
                    key_vars(n + 2, b)

            key_vars(0, 0)
            for u in range(B * NKV):
                dve.wait_ge(qT_ready, u + 1)
                nc.vector.scalar_tensor_tensor(out=QL[:, u // NKV, u % NKV, :], in0=QR[u % len(QR)][:], scalar=qkn[:, 0:1],
                                               in1=QH[:, u // NKV, u % NKV, :].bitcast(F32),
                                               op0=ALU.mult, op1=ALU.subtract).then_inc(ql_ready, 1)
            dve.wait_ge(in_mask, 16)
            half(-1, 1, -1, pv=False)
            with dve.Fori(0, NKV - 1) as i:
                half(2 * i, 0, i)
                half(2 * i + 1, 1, i)
            half(NG - 2, 0, NKV - 1, keys=False)
            half(NG - 1, 1, NKV - 1, scores=False, keys=False)

            def add_to_x(n, bank=6):
                for b in range(B):
                    dve.wait_ge(proj_done, n + b)
                    last = nc.vector.tensor_tensor(x[:, b, :], x[:, b, :], ps[bank + b][:, 0:D], ALU.add)
                    if n == 9:
                        last.then_inc(x_ready, 1)
                if n < 9:
                    dve.wait_ge(dve_step.sem, dve_step(last))

            def copy_turned(n):
                dve.wait_ge(xT_done, n)
                nc.vector.tensor_copy(xnT[:].rearrange("p k n -> p (k n)"), ps[2][:]).then_inc(xT_ready, 1)

            def then(ins):
                dve.wait_ge(dve_step.sem, dve_step(ins))

            add_to_x(1, 0)
            norm_stats(x, 2)
            for b in range(B):
                c = dve_step(nc.vector.tensor_scalar(xn[:, b, :], x[:, b, :], mv[:, b, 0:1], rstd[:, b:b + 1],
                                                     ALU.subtract, ALU.mult))
            for b in range(B):
                dve.wait_ge(dve_step.sem, c - 1 + b)
                last = nc.vector.tensor_tensor_reduce(sq[:, b, :], xn[:, b, :], xn[:, b, :], 1.0 / D, 1.1920929e-07,
                                                      ALU.mult, ALU.add, var[:, b:b + 1])
            last.then_inc(var_ready, 1)
            then(nc.vector.tensor_tensor(x[:], x[:], xn[:], ALU.add))
            dve.wait_ge(rstd_ready, 3)
            for b in range(B):
                last = nc.vector.tensor_scalar(hx[:, b, :], xn[:, b, :], rstd[:, b:b + 1], None, ALU.mult)
            last.then_inc(xn_ready, 1)
            copy_turned(2)
            c = dve_step(nc.vector.tensor_scalar(lin[:, 0, :, 0], cols[:, 2:4], sig[:, 3:4], None, ALU.mult))
            dve.wait_ge(dve_step.sem, c)
            dve.wait_ge(lin_done, 1)
            then(nc.vector.tensor_tensor(lin[:, 1], ps[7][:, 0:KD * B].rearrange("p (k b) -> p k b", b=B),
                                         lin[:, 0, :, 0:1].broadcast_to([P, KD, B]), ALU.add))
            nc.vector.tensor_scalar(lin[:, 2], lin[:, 1], 1.0 / SE, None, ALU.mult).then_inc(lin_ready, 1)
            dve.wait_ge(qk_squared, 2 * B)
            nc.vector.tensor_scalar(var[:, 0:4], ssq[:], 1.0 / D, 1.1920929e-07, ALU.mult, ALU.add).then_inc(var_ready, 1)
            dve.wait_ge(rstd_ready, 4)
            nc.vector.tensor_scalar(nrstd[:], rstd[:, 0:4], -1.0, None, ALU.mult).then_inc(nrstd_ready, 1)
            for b in range(B):
                dve.wait_ge(w_ready, b + 1)
                dve.wait_ge(qkv_done, 2 * b + 2)
                nc.vector.tensor_tensor(ww[:, b, 0:D], ww[:, b, D:2 * D], ps[3 + b][:, 0:D], ALU.mult).then_inc(wv_ready, 1)
            for b in range(B):
                dve.wait_ge(cum_done, b + 1)
                c = dve_step(nc.vector.tensor_scalar(yden[:, b, :], ps[5 + b][:, D:2 * D], 1e-6, None, ALU.add))
            dve.wait_ge(eq_ready, B)
            for b in range(B):
                dve.wait_ge(dve_step.sem, c - 1 + b)
                d = dve_step(nc.vector.scalar_tensor_tensor(out=yden[:, b, :], in0=eq[:, b, :], scalar=1.0,
                                                            in1=yden[:, b, :], op0=ALU.add, op1=ALU.mult))
            for b in range(B):
                dve.wait_ge(dve_step.sem, d - 1 + b)
                c = dve_step(nc.vector.reciprocal(yden[:, b, :], yden[:, b, :]))
            for b in range(B):
                dve.wait_ge(dve_step.sem, c - 1 + b)
                last = nc.vector.tensor_tensor(yt[:, b, :], ps[5 + b][:, 0:D], yden[:, b, :], ALU.mult)
            last.then_inc(xn_ready, 1)
            copy_turned(3)
            for f in range(FB):
                dve.wait_ge(sw_silu, f + 1)
                nc.vector.tensor_tensor(hsw[:, f, :], ps[SW[f % 4]][:, 0:D], ssw[:, f % 2, :], ALU.mult).then_inc(sw_ready, 1)
            dve.wait_ge(in_rows, 64)
            dve.wait_ge(lin_done, 2)
            nc.vector.tensor_tensor(summ[:], ps[7][:].rearrange("p (b d) -> p b d", b=B),
                                    rows[:, 0:1, :].broadcast_to([P, B, D]), ALU.add).then_inc(lin_ready, 1)
            add_to_x(3, 5)

            def normalise_x(n, nx):
                norm_stats(x, n)
                for b in range(B):
                    last = nc.vector.tensor_scalar(xn[:, b, :], x[:, b, :], mv[:, b, 0:1], rstd[:, b:b + 1],
                                                   ALU.subtract, ALU.mult)
                last.then_inc(xn_ready, 1)
                copy_turned(nx)

            normalise_x(5, 4)
            dve.wait_ge(r0_done, 1)
            lg = ps[0][:, 0:B * E0].rearrange("p (b e) -> p b e", b=B)
            nc.vector.reduce_max(r0m[:, 0], lg, AX.X).then_inc(max0_ready, 1)
            dve.wait_ge(max0_ready, 1)
            then(nc.vector.tensor_tensor(r0[:, 0], lg, r0m[:, 0].unsqueeze(2).broadcast_to([P, B, E0]), ALU.is_equal))
            then(nc.vector.tensor_tensor(r0[:, 1], r0[:, 0], order[:].unsqueeze(1).broadcast_to([P, B, E0]), ALU.mult))
            then(nc.vector.reduce_max(r0m[:, 2], r0[:, 1], AX.X))
            then(nc.vector.tensor_tensor(r0[:, 2], r0[:, 1], r0m[:, 2].unsqueeze(2).broadcast_to([P, B, E0]), ALU.is_equal))
            dve.wait_ge(tanh0_ready, 1)
            then(nc.vector.tensor_scalar(r0m[:, 3], r0s[:], 0.5, 0.5, ALU.mult, ALU.add))
            nc.vector.tensor_tensor(sel0[:, :, 1:E0 + 1], r0[:, 2], r0m[:, 3].unsqueeze(2).broadcast_to([P, B, E0]),
                                    ALU.mult).then_inc(sel0_ready, 1)
            dve.wait_ge(sel0_ready, 1)

            def products0(e, par):
                for b in range(B):
                    dve.wait_ge(silu0_done, B * e + b + 1)
                    nc.vector.scalar_tensor_tensor(out=h0[:, par, b, :], in0=ps[1 + 2 * par + b][:, D:2 * D],
                                                   scalar=sel0[:, b, column(e)], in1=sg0[:, par, b, :],
                                                   op0=ALU.mult, op1=ALU.mult).then_inc(h0_ready, 1)

            products0(0, 0)
            with dve.Fori(0, E0 // 2) as i:
                products0(2 * i + 1, 1)
                products0(2 * i + 2, 0)
            add_to_x(5)

            norm_stats(x, 6)
            for b in range(B):
                c = dve_step(nc.vector.tensor_scalar(xn[:, b, :], x[:, b, :], mv[:, b, 0:1], rstd[:, b:b + 1],
                                                     ALU.subtract, ALU.mult))
            dve.wait_ge(dve_step.sem, c)
            then(nc.vector.tensor_tensor(yt[:], xn[:], summ[:], ALU.add))
            norm_stats(yt, 7)
            for b in range(B):
                c = dve_step(nc.vector.tensor_scalar(xn[:, b, :], yt[:, b, :], mv[:, b, 0:1], rstd[:, b:b + 1],
                                                     ALU.subtract, ALU.mult))
            dve.wait_ge(dve_step.sem, c)
            then(nc.vector.tensor_tensor(yt[:], xn[:], rows[:, 1:2, :].broadcast_to([P, B, D]), ALU.mult))
            then(nc.vector.tensor_tensor(xn[:], yt[:], rows[:, 2:3, :].broadcast_to([P, B, D]), ALU.add))
            then(nc.vector.tensor_tensor(x[:], x[:], xn[:], ALU.add))

            normalise_x(8, 5)

            def rotate(r, m):
                dve.wait_ge(p5_done, m + 1)
                if r >= 2:
                    dve.wait_ge(rope_ready, r - 1)
                src = ps[m % 2][:].rearrange("p (h d) -> p h d", h=GH)
                nc.vector.tensor_tensor(rc[:, r % 2], src, cosT.unsqueeze(1).broadcast_to([P, GH, P]), ALU.mult)
                for lo, hi in ((0, P // 2), (P // 2, P)):
                    last = nc.vector.tensor_tensor(rs[:, r % 2, :, lo:hi], src[:, :, P // 2 - lo:P - lo],
                                                   sinT[:, lo:hi].unsqueeze(1).broadcast_to([P, GH, P // 2]), ALU.mult)
                last.then_inc(rope_mul, 1)

            for s in range(B * NKV + 2):
                b, c = divmod(s, NKV)
                if s - 2 >= 0:
                    u = s - 2
                    dve.wait_ge(exp5, u + 1)
                    then(nc.vector.reciprocal(sum5[:, 1, u * GH:(u + 1) * GH], sum5[:, 0, u * GH:(u + 1) * GH]))
                    nc.vector.tensor_tensor(P5[:, u % 2], P5[:, u % 2],
                                            sum5[:, 1, u * GH:(u + 1) * GH].unsqueeze(2).broadcast_to([P, GH, P]),
                                            ALU.mult).then_inc(norm5, 1)
                if s < B * NKV:
                    if c == 0:
                        rotate(rope_at(s) - 1, 6 * b)
                    rotate(rope_at(s), 6 * b + 2 + c)
                if 1 <= s <= B * NKV:
                    u = s - 1
                    dve.wait_ge(s5_done, u + 1)
                    then(nc.vector.scalar_tensor_tensor(
                        out=P5[:, u % 2], in0=ps[4][:].rearrange("p (h k) -> p h k", h=GH), scalar=SCALE,
                        in1=causal.unsqueeze(1).broadcast_to([P, GH, P]), op0=ALU.mult, op1=ALU.add))
                    then(nc.vector.reduce_max(nmax5[:, 0, u * GH:(u + 1) * GH], P5[:, u % 2], AX.X))
                    nc.vector.tensor_scalar(nmax5[:, 1, u * GH:(u + 1) * GH], nmax5[:, 0, u * GH:(u + 1) * GH], -1.0, None,
                                            ALU.mult).then_inc(soft5, 1)
            add_to_x(7)

            normalise_x(9, 6)
            dve.wait_ge(exp1_done, 1)
            then(nc.vector.tensor_scalar(sc1[:, 0], sc1[:, 0], 1.0, None, ALU.add))
            then(nc.vector.reciprocal(sc1[:, 1], sc1[:, 0]))
            then(nc.vector.tensor_tensor(sc1[:, 2], sc1[:, 1], bias1[:].unsqueeze(1).broadcast_to([P, B, E1]), ALU.add))
            four = sc1[:, 2].rearrange("p b (g f) -> p (b g) f", f=4)
            nc.vector.tensor_tensor(pair1[:, 0], four[:, :, 0:2], four[:, :, 2:4], ALU.max)
            then(nc.vector.tensor_tensor(pair1[:, 1], four[:, :, 0:2], four[:, :, 2:4], ALU.min))
            nc.vector.tensor_tensor(grp1[:, 0], pair1[:, 0, :, 0], pair1[:, 0, :, 1], ALU.max)
            nc.vector.tensor_tensor(grp1[:, 1], pair1[:, 0, :, 0], pair1[:, 0, :, 1], ALU.min)
            then(nc.vector.tensor_tensor(grp1[:, 2], pair1[:, 1, :, 0], pair1[:, 1, :, 1], ALU.max))
            then(nc.vector.tensor_tensor(grp1[:, 1], grp1[:, 1], grp1[:, 2], ALU.max))
            then(nc.vector.tensor_tensor(gsc1[:, :, 0:E1 // 4], grp1[:, 0].rearrange("p (b g) -> p b g", b=B),
                                         grp1[:, 1].rearrange("p (b g) -> p b g", b=B), ALU.add))
            for b in range(B):
                then(nc.vector.max(top1[:, b, :], gsc1[:, b, :]))
                then(nc.vector.memset(top1[:, b, 4:8], -BIG))
                c = dve_step(nc.vector.match_replace(gre1[:, b, :], top1[:, b, :], gsc1[:, b, :], -BIG))
            dve.wait_ge(dve_step.sem, c)
            then(nc.vector.tensor_tensor(gsel1[:], gsc1[:, :, 0:E1 // 4], gre1[:, :, 0:E1 // 4], ALU.not_equal))
            then(nc.vector.tensor_scalar(gsel1[:], gsel1[:], BIG, -BIG, ALU.mult, ALU.add))
            then(nc.vector.tensor_tensor(msk1[:, 0].rearrange("p b (g f) -> p (b g) f", f=4), four,
                                         gsel1[:].rearrange("p b g -> p (b g)").unsqueeze(2).broadcast_to([P, B * E1 // 4, 4]),
                                         ALU.add))
            for b in range(B):
                then(nc.vector.max(top1[:, 2 + b, :], msk1[:, 0, b, :]))
                then(nc.vector.memset(top1[:, 2 + b, 6:8], -BIG))
                c = dve_step(nc.vector.match_replace(msk1[:, 1, b, :], top1[:, 2 + b, :], msk1[:, 0, b, :], -BIG))
            dve.wait_ge(dve_step.sem, c)
            then(nc.vector.tensor_tensor(msk1[:, 1], msk1[:, 0], msk1[:, 1], ALU.not_equal))
            nc.vector.tensor_tensor(comb[:], msk1[:, 1], sc1[:, 1], ALU.mult).then_inc(comb_ready, 1)

            def products6(step, e, batches=range(B)):
                for b in batches:
                    dve.wait_ge(silu6_done, B * step + b + 1)
                    if e is None:
                        last = nc.vector.tensor_tensor(h6[:, b, IT * M1 - SHW:IT * M1], ps[2 * b + 1][:, 0:SHW],
                                                       sg6[:, b, :], ALU.mult)
                    else:
                        chunk, first = e
                        for j in range(CH):
                            last = nc.vector.scalar_tensor_tensor(
                                out=h6[:, b, chunk * CW + j * M1:chunk * CW + (j + 1) * M1],
                                in0=ps[2 * b + 1][:, j * M1:(j + 1) * M1], scalar=comb[:, b, column(first + j)],
                                in1=sg6[:, b, j * M1:(j + 1) * M1], op0=ALU.mult, op1=ALU.mult)
                    last.then_inc(h6_ready, 1)

            def turned6(step, n):
                dve.wait_ge(t6_done, B * step + 2)
                nc.vector.tensor_copy(hT6[:, 1, 0:n, :].rearrange("p k t -> p (k t)"), ps[5][:, 0:n * P])\
                    .then_inc(hT6_ready[1], 1)

            def step6(step, n, e):
                if e:
                    products6(step + 1, e, range(1))
                turned6(step, n)
                if e:
                    products6(step + 1, e, range(1, B))

            products6(0, None)
            dve.wait_ge(comb_ready, 1)
            step6(0, SHW // P, (0, 0))
            with dve.Fori(0, E1 // IT - 1) as i:
                for c in range(NCH):
                    step6(NCH * i + c + 1, BLOCKS[c][1] - BLOCKS[c][0], ((c + 1) % NCH, IT * i + CH * (c + 1)))
            for c in range(NCH):
                step6(E1 // CH - NCH + c + 1, BLOCKS[c][1] - BLOCKS[c][0],
                      (c + 1, E1 - IT + CH * (c + 1)) if c < NCH - 1 else None)
            add_to_x(9)

        @block.tensor
        def _(pe):
            mm, tr = nc.tensor.matmul, nc.tensor.transpose

            def transpose_tokens(dst):
                for k in range(KD):
                    for b in range(B):
                        last = tr(dst[:, (k * B + b) * P:(k * B + b + 1) * P], xn[:, b, k * P:(k + 1) * P], ident)
                last.then_inc(xT_done, 1)

            pe.wait_ge(in_consts, 16)
            pe.wait_ge(xn_ready, 1)
            transpose_tokens(SC[0])
            pe.wait_ge(xT_ready, 1)
            pe.wait_ge(in_wq, 16)
            for u in range(B * NKV):
                if u >= 2:
                    pe.wait_ge(q_biased, u - 1)
                for k in range(KD):
                    last = mm(SC[1 + u % 2][:], xnT[:, k, u // NKV * P:(u // NKV + 1) * P],
                              wq[:, k, u % NKV * GW:(u % NKV + 1) * GW], start=(k == 0), stop=(k == KD - 1))
                last.then_inc(q_done, 1)

            def key_chunks(g, b, kvh, chunks, first=False):
                pe.wait_ge(in_wkv, 16 * (kvh + 1))
                for t in chunks:
                    if isinstance(g, int) and g < B:
                        pe.wait_ge(in_ctx[b][t], 16)
                    if t >= 2:
                        pe.wait_ge(k_ready, NC * g + t - 1)
                    elif not first:
                        pe.wait_ge(v_ready, NC * (g - 1) + t + 3)
                    for k in range(KD):
                        last = mm(PR[t % 2][:], wkv[:, k * 2 * P:k * 2 * P + P], ctxT[:, b, k, t * GW:(t + 1) * GW],
                                  start=(k == 0), stop=(k == KD - 1))
                    last.then_inc(k_done, 1)

            def value_chunks(g, b, first=False):
                for t in range(NC):
                    if t < 2:
                        pe.wait_ge(k_ready, NC * g + t + 3)
                    else:
                        pe.wait_ge(v_ready, NC * g + t - 1)
                    for j in range(4):
                        for k in range(KD):
                            last = mm(PR[t % 2][:, j * P:(j + 1) * P], ctxT[:, b, k, (4 * t + j) * P:(4 * t + j + 1) * P],
                                      wkv[:, k * 2 * P + P:(k + 1) * 2 * P], start=(k == 0), stop=(k == KD - 1))
                    last.then_inc(v_done, 1)
                if not first:
                    pe.wait_ge(max_ready, g)
                for j in range(NT):
                    last = mm(MISC[:, j:j + 1], K2[:, j * P:(j + 1) * P], ones[:, 0:1], start=True, stop=True)
                last.then_inc(ksum_done, 1)

            def score_tile(g, b, kvh, j):
                if j == 0:
                    pe.wait_ge(kl_ready, NC * (g + 1))
                if j >= 3:
                    pe.wait_ge(s_ready, g * NT + j - 2)
                keys = slice(j * P, (j + 1) * P)
                mm(SC[j % 3][:], KH[b][:, keys], QH[:, b, kvh, :], start=True, stop=False)
                mm(SC[j % 3][:], KH[b][:, keys], QL[:, b, kvh, :], start=False, stop=False)
                mm(SC[j % 3][:], KL[b][:, keys], QH[:, b, kvh, :], start=False, stop=True).then_inc(s_done, 1)

            def value_tile(g, b, j):
                pe.wait_ge(exp_done, g * NT + j + 1)
                if j == 0 and (not isinstance(g, int) or g):
                    pe.wait_ge(o_scaled, g)
                mm(PO[:], V[b][:, j, :], S[:, j, :], start=(j == 0), stop=(j == NT - 1))

            def transpose_maxima(g, b):
                pe.wait_ge(max_step, (g + 1) * (NT - 1))
                for h in range(GH):
                    last = tr(MISC[:, h * P:(h + 1) * P], M[b][:, h * P:(h + 1) * P], ident)
                last.then_inc(maxT_done, 1)

            def spread_maxima(g):
                pe.wait_ge(max_ready, g + 1)
                if not isinstance(g, int) or g:
                    pe.wait_ge(rden_ready, g)
                for h in range(GH):
                    last = mm(MB[:, h * P:(h + 1) * P], mq[:, h:h + 1].broadcast_to([P, P]), ident, start=True, stop=True)
                last.then_inc(mb_done, 1)

            def denominators(g, b):
                pe.wait_ge(psum_step, (g + 1) * (NT - 1))
                mm(MB[:], ones[:], psums[b][:], start=True, stop=True).then_inc(den_done, 1)

            def half(n, b, kvh, scores=True, pv=True, keys=True):
                for j in range(NT):
                    if pv:
                        value_tile(n, b, j)
                    if scores:
                        score_tile(n + 1, 1 - b, kvh + b, j)
                    if keys and not pv and j % 4 == 3:
                        key_chunks(n + 2, b, kvh + 1, [j // 4])
                if pv:
                    denominators(n, b)
                if keys and pv:
                    key_chunks(n + 2, b, kvh + 1, range(0, 1))
                if scores:
                    transpose_maxima(n + 1, 1 - b)
                if keys and pv:
                    key_chunks(n + 2, b, kvh + 1, range(1, 3))
                if scores:
                    spread_maxima(n + 1)
                if keys and pv:
                    key_chunks(n + 2, b, kvh + 1, range(3, NC))
                if keys:
                    value_chunks(n + 2, b)

            key_chunks(0, 0, 0, range(NC), first=True)
            value_chunks(0, 0, first=True)
            for u in range(B * NKV):
                if u == 0:
                    pe.wait_ge(v_ready, NC)
                if u % NKV == 0:
                    pe.wait_ge(q_scaled, u // NKV + 1)
                if u >= len(QR):
                    pe.wait_ge(qT_ready, u - len(QR) + 1)
                    pe.wait_ge(ql_ready, u - len(QR) + 1)
                for h in range(GH):
                    last = tr(QR[u % len(QR)][:, h * P:(h + 1) * P], q_tok[:, u // NKV, u % NKV * GH + h, :], ident)
                last.then_inc(qT_done, 1)
            pe.wait_ge(qT_ready, B * NKV)
            pe.wait_ge(ql_ready, B * NKV)
            half(-1, 1, -1, pv=False)
            with pe.Fori(0, NKV - 1) as i:
                half(2 * i, 0, i)
                half(2 * i + 1, 1, i)
            half(NG - 2, 0, NKV - 1, keys=False)
            half(NG - 1, 1, NKV - 1, scores=False, keys=False)

            pe.wait_ge(in_wo, 16)
            pe.wait_ge(o_ready, NG)
            for b in range(B):
                for h in range(NH):
                    last = mm(ps[b][:, 0:D], OT[:, b, h // GH, h % GH * P:(h % GH + 1) * P], wo[:, h, :],
                              start=(h == 0), stop=(h == NH - 1))
                last.then_inc(proj_done, 1)

            def turn(src, n):
                pe.wait_ge(xn_ready, n)
                for k in range(KD):
                    for b in range(B):
                        last = tr(ps[2][:, (k * B + b) * P:(k * B + b + 1) * P], src[:, b, k * P:(k + 1) * P], ident)
                last.then_inc(xT_done, 1)
                pe.wait_ge(xT_ready, n)

            def over_tokens(dst, b, weights):
                for k in range(KD):
                    last = mm(dst, xnT[:, k, b * P:(b + 1) * P], weights[:, k, :], start=(k == 0), stop=(k == KD - 1))
                return last

            turn(hx, 2)
            pe.wait_ge(in_w2, 32)
            for b in range(B):
                over_tokens(ps[b][:], b, wqkv[:, :, 0:2 * D]).then_inc(qkv_done, 1)
                over_tokens(ps[3 + b][:, 0:D], b, wqkv[:, :, 2 * D:3 * D]).then_inc(qkv_done, 1)
            pe.wait_ge(in_lin, 32)
            pe.wait_ge(csum_ready, B * KD)
            for m in range(KD):
                for k in range(KD):
                    last = mm(ps[7][:, m * B:(m + 1) * B], win[:, k, m * P:(m + 1) * P], csum[:, k, :],
                              start=(k == 0), stop=(k == KD - 1))
            last.then_inc(lin_done, 1)
            for b in range(B):
                pe.wait_ge(wv_ready, b + 1)
                mm(ps[5 + b][:], tri, ww[:, b, :], start=True, stop=True).then_inc(cum_done, 1)
            pe.wait_ge(lin_ready, 1)
            for b in range(B):
                for k in range(KD):
                    last = mm(ps[7][:, b * D:(b + 1) * D], lin[:, 2, k, b:b + 1].broadcast_to([P, P]), wlin[:, k, :],
                              start=(k == 0), stop=(k == KD - 1))
            last.then_inc(lin_done, 1)
            turn(yt, 3)
            pe.wait_ge(in_wsw, 16)

            def swiglu_out(f):
                pe.wait_ge(sw_ready, f + 1)
                for b in range(B):
                    last = mm(ps[5 + b][:, 0:D], hsw[:, f, b * P:(b + 1) * P], wout[:, f, :],
                              start=(f == 0), stop=(f == FB - 1))
                    if f == FB - 1:
                        last.then_inc(proj_done, 1)

            for f in range(FB):
                if f >= 4:
                    pe.wait_ge(sw_ready, f - 3)
                for i in range(2):
                    for k in range(KD):
                        last = mm(ps[SW[f % 4]][:, i * D:(i + 1) * D], wsw[:, k, i * FF + f * P:i * FF + (f + 1) * P],
                                  xnT[:, k, :], start=(k == 0), stop=(k == KD - 1))
                last.then_inc(sw_done, 1)
                if f >= 2:
                    swiglu_out(f - 2)
            swiglu_out(FB - 2)
            swiglu_out(FB - 1)

            turn(xn, 4)
            pe.wait_ge(in_rows, 64)
            for b in range(B):
                last = over_tokens(ps[0][:, b * E0:(b + 1) * E0], b, router0)
            last.then_inc(r0_done, 1)
            pe.wait_ge(in_e0, 32)

            def gate_up0(e, par, b):
                over_tokens(ps[1 + 2 * par + b][:], b, w0[:, e]).then_inc(gu0_done, 1)

            def step0(e, par, first=False, more=True):
                if more:
                    if not first:
                        pe.wait_ge(h0_ready, B * e)
                    gate_up0(e + 1, 1 - par, 0)
                pe.wait_ge(h0_ready, B * (e + 1))
                if not first:
                    pe.wait_ge(hT0_ready, e)
                for k in range(KD):
                    for b in range(B):
                        last = tr(ps[5][:, (k * B + b) * P:(k * B + b + 1) * P], h0[:, par, b, k * P:(k + 1) * P], ident)
                last.then_inc(t0_done, 1)
                if more:
                    gate_up0(e + 1, 1 - par, 1)
                pe.wait_ge(hT0_ready, e + 1)
                for b in range(B):
                    for k in range(KD):
                        last = mm(ps[6 + b][:, 0:D], hT0[:, k, b, :], d0[:, e, k, :], start=(first and k == 0),
                                  stop=(not more and k == KD - 1), skip_group_check=True)
                    if not more:
                        last.then_inc(proj_done, 1)

            for b in range(B):
                gate_up0(0, 0, b)
            step0(0, 0, first=True)
            with pe.Fori(0, 3) as i:
                step0(2 * i + 1, 1)
                step0(2 * i + 2, 0)
            step0(E0 - 1, 1)
            step0(E0, 0, more=False)

            turn(xn, 5)
            pe.wait_ge(in_kv5, 16)

            def project5(m, weights):
                if m >= 2:
                    b, c = divmod(m - 2, 6)
                    if c == 1:
                        pe.wait_ge(v5_ready, b + 1)
                    else:
                        pe.wait_ge(rope_mul, b * (NKV + 1) + (c if c == 0 else c - 1) + 1)
                over_tokens(ps[m % 2][:], m // 6, weights).then_inc(p5_done, 1)

            def turn5(r):
                pe.wait_ge(rope_ready, r + 1)
                if r:
                    pe.wait_ge(t5_ready, r)
                for h in range(GH):
                    last = tr(ps[2][:, h * P:(h + 1) * P], rope[:, r % 2, h, :], ident)
                last.then_inc(t5_done, 1)

            for s in range(B * NKV + 3):
                b, c = divmod(s, NKV)
                if s < B * NKV:
                    if c == 0:
                        project5(6 * b, wkv5[:, :, 0:GW])
                        project5(6 * b + 1, wkv5[:, :, GW:2 * GW])
                    if s == 0:
                        pe.wait_ge(in_w5, 32)
                    project5(6 * b + 2 + c, wq5[:, :, c * GW:(c + 1) * GW])
                u = s - 1
                if 0 <= u < B * NKV:
                    if u % NKV == 0:
                        turn5(rope_at(u) - 1)
                    turn5(rope_at(u))
                u = s - 3
                if 0 <= u:
                    pe.wait_ge(o5_ready, u + 1)
                    for h in range(GH):
                        last = mm(ps[6 + u // NKV][:, 0:D], OT5[:, h, :], wo5[:, u % NKV * GH + h, :],
                                  start=(u % NKV == 0 and h == 0), stop=(u % NKV == NKV - 1 and h == GH - 1))
                    if u % NKV == NKV - 1:
                        last.then_inc(proj_done, 1)
                u = s - 2
                if 0 <= u < B * NKV:
                    pe.wait_ge(norm5, u + 1)
                    if u:
                        pe.wait_ge(pT5_ready, u)
                    for h in range(GH):
                        last = tr(ps[3][:, h * P:(h + 1) * P], P5[:, u % 2, h, :], ident)
                    last.then_inc(pT5_done, 1)
                u = s - 1
                if 0 <= u < B * NKV:
                    pe.wait_ge(t5_ready, rope_at(u) + 1)
                    if u:
                        pe.wait_ge(soft5, u)
                    for h in range(GH):
                        last = mm(ps[4][:, h * P:(h + 1) * P], QT5[u % 2][:, h, :], KT5[:, u // NKV, u % NKV, :],
                                  start=True, stop=True)
                    last.then_inc(s5_done, 1)
                u = s - 2
                if 0 <= u < B * NKV:
                    pe.wait_ge(pT5_ready, u + 1)
                    pe.wait_ge(v5_ready, u // NKV + 1)
                    if u:
                        pe.wait_ge(o5_ready, u)
                    mm(ps[5][:], V5[:, u // NKV, u % NKV, :], PT5[:].rearrange("p h t -> p (h t)"), start=True,
                       stop=True).then_inc(o5_done, 1)

            turn(xn, 6)
            for b in range(B):
                last = over_tokens(ps[4][:, b * E1:(b + 1) * E1], b, router1)
            last.then_inc(r1_done, 1)

            def gate_up6(step, b, weights, width, first=False):
                if not first:
                    pe.wait_ge(h6_ready, B * (step - 1) + b + 1)
                for i in range(2):
                    last = over_tokens(ps[2 * b + i][:, 0:width], b, weights[:, :, i * width:(i + 1) * width])
                last.then_inc(gu6_done, 1)

            def step6(step, blocks, down, ready, following=None, first=False, last_=False):
                if following:
                    c, turn_ = following
                    pe.wait_ge(in_gu[c], 16 * (turn_ + 1))
                    gate_up6(step + 1, 0, gu1[c], CW)
                pe.wait_ge(h6_ready, B * (step + 1))
                n = len(blocks)
                for b in range(B):
                    for k, blk in enumerate(blocks):
                        last = tr(ps[4 + b][:, k * P:(k + 1) * P], h6[:, b, blk * P:(blk + 1) * P], ident)
                    last.then_inc(t6_done, 1)
                if following:
                    gate_up6(step + 1, 1, gu1[c], CW)
                ready()
                for b in range(B):
                    pe.wait_ge(hT6_ready[b], step + 1)
                    for k in range(n):
                        last = mm(ps[6 + b][:, 0:D], hT6[:, b, k, :], down[:, k, :], start=(first and k == 0),
                                  stop=(last_ and k == n - 1), skip_group_check=True)
                    if last_:
                        last.then_inc(proj_done, 1)
                if not last_:
                    last.then_inc(d6_done, 1)

            def routed_step(step, c, turn_, following, last_=False):
                lo, hi = BLOCKS[c]
                step6(step, range(lo, hi), dn1[:, lo:hi], lambda: pe.wait_ge(in_dn[c], 16 * (turn_ + 1)), following,
                      last_=last_)

            pe.wait_ge(in_sh, 32)
            for b in range(B):
                gate_up6(0, b, gush, SHW, first=True)
            pe.wait_ge(exp1_done, 1)
            step6(0, range(NB - SHW // P, NB), dnsh, lambda: None, (0, 0), first=True)
            with pe.Fori(0, E1 // IT - 1) as i:
                for c in range(NCH):
                    routed_step(NCH * i + c + 1, c, i, (c + 1, i) if c < NCH - 1 else (0, i + 1))
            for c in range(NCH):
                routed_step(E1 // CH - NCH + c + 1, c, E1 // IT - 1, (c + 1, E1 // IT - 1) if c < NCH - 1 else None,
                            last_=(c == NCH - 1))


def _blocks(w):
    k, n = w.shape
    return w.reshape(k // P, P, n).transpose(1, 0, 2)


def _constants():
    import numpy as np
    i = np.arange(P)
    ident = np.eye(P, dtype=np.float32)
    tri = (i[:, None] <= i[None, :]).astype(np.float32)
    causal = np.where(i[None, :] <= i[:, None], 0.0, -1e30).astype(np.float32)
    fraction = np.arange(0, P, 2, dtype=np.float32) / np.float32(P)
    angle = i[:, None].astype(np.float32) / (np.float32(10000.0) ** fraction)[None, :]
    cos, sin = np.cos(angle), np.sin(angle)
    return np.stack([ident, tri, causal, np.concatenate([cos, cos], 1), np.concatenate([-sin, sin], 1)], 1)


def _layout(i):
    import numpy as np
    c = lambda v, *s: np.ascontiguousarray(v).reshape(*s)
    wk = _blocks(i["L0_xattn_Wk"]).reshape(P, KD, NKV, P)
    wv = _blocks(i["L0_xattn_Wv"]).reshape(P, KD, NKV, P)
    wkv = np.stack([wk, wv], 3).transpose(0, 2, 1, 3, 4).reshape(P, NKV, KD * 2 * P)
    bk = i["L0_xattn_bk"].reshape(NKV, P).T[:, :, None]
    zeros = np.zeros((P, 2), np.float32)
    decay = np.broadcast_to(i["L1_xattn_decay"].reshape(1, 1), (P, 1))
    b_in = i["L1_xattn_b_in"].reshape(KD, P).T
    experts0 = [(i["L0_ffn_shared_gate_w"], i["L0_ffn_shared_up_w"], i["L0_ffn_shared_down_w"])]
    experts0 += [(i["L0_ffn_gate_w"][e], i["L0_ffn_up_w"][e], i["L0_ffn_down_w"][e]) for e in range(E0)]
    gu1 = [np.concatenate([_blocks(np.concatenate(list(i[n][CH * c:CH * c + CH]), 1))
                           for n in ("L1_ffn_gate_w", "L1_ffn_up_w")], 2).reshape(P, -1) for c in range(E1 // CH)]
    pad = lambda w: np.pad(w, ((0, 0), (0, SHW - w.shape[1])))
    return {
        "x": c(i["x"].transpose(1, 0, 2), P, B * D),
        "consts": c(_constants(), P, 5 * P),
        "ctxT": c(i["ctx_2048"].transpose(2, 0, 1).reshape(KD, P, B, SE).transpose(1, 2, 0, 3), P, B, KD, SE),
        "maskT": c(i["mask_1xSxS2_ff0"][0].T.reshape(NT, P, P).transpose(1, 0, 2), P, NT * P),
        "wq": c(_blocks(i["L0_xattn_Wq"]), P, KD * NH * P),
        "bq": c(i["L0_xattn_bq"], 1, NH * P),
        "wkv": c(np.concatenate([wkv, bk], 2), P, NKV, KD * 2 * P + 1),
        "bv": c(i["L0_xattn_bv"].reshape(NKV, P).T, P, NKV),
        "wo": c(_blocks(i["L0_xattn_Wo"]), P, NH * D),
        "cols": c(np.concatenate([i["L0_xattn_qn_w"][:, None], i["L0_xattn_kn_w"][:, None], b_in, decay, zeros,
                                  zeros[:, :1]], 1), P, 8),
        "wqkv": c(_blocks(i["L0_attn_w_qkv"].T), P, KD * 3 * D),
        "wsw": c(_blocks(i["L0_attn_w_swiglu"].T), P, KD * 2 * FF),
        "wout": c(_blocks(i["L0_attn_w_out"].T), P, FB * D),
        "w0": c(np.stack([_blocks(np.concatenate([g, u], 1)) for g, u, _ in experts0], 1), P, (E0 + 1) * KD * 2 * D),
        "d0": c(np.stack([_blocks(d) for _, _, d in experts0], 1), P, (E0 + 1) * KD * D),
        "router0": c(_blocks(i["L0_ffn_router_w"]), P, KD * E0),
        "win": c(_blocks(i["L1_xattn_W_in"].T), P, KD * D),
        "wlin": c(_blocks(i["L1_xattn_W_out"].T), P, KD * D),
        "rows": c(np.concatenate([i["L1_xattn_b_out"], i["L1_xattn_gamma"], i["L1_xattn_beta"]]), 1, 3 * D),
        "wq5": c(_blocks(i["L1_attn_q_kernel"]), P, KD * NH * P),
        "wkv5": c(_blocks(np.concatenate([i["L1_attn_k_kernel"], i["L1_attn_v_kernel"]], 1)), P, KD * 2 * NKV * P),
        "wo5": c(_blocks(i["L1_attn_out_kernel"]), P, NH * D),
        "router1": c(_blocks(i["L1_ffn_w_router"]), P, KD * E1),
        "bias1": c(i["L1_ffn_corr_bias"], 1, E1),
        "gu1": c(np.stack(gu1, 1), P, E1 // CH, KD * 2 * CW),
        "down1": c(_blocks(i["L1_ffn_down_w"].reshape(E1 * M1, D)), P, E1 * M1 // P, D),
        "gush": c(np.concatenate([_blocks(pad(i["L1_ffn_sh_gate_w"])), _blocks(pad(i["L1_ffn_sh_up_w"]))], 2),
                  P, KD * 2 * SHW),
        "downsh": c(_blocks(np.pad(i["L1_ffn_sh_down_w"], ((0, SHW - 352), (0, 0)))), P, SHW // P * D),
    }


def kernel(**inputs):
    import numpy as np
    import concourse.bacc as bacc
    from concourse.bass_utils import run_bass_kernel_spmd

    arrays = {f"in_{n}": v for n, v in _layout({k: np.asarray(v) for k, v in inputs.items()}).items()}
    nc = bacc.Bacc("TRN2", target_bir_lowering=False, num_devices=1)
    aps = {n[3:]: nc.dram_tensor(n, v.shape, mybir.dt.from_np(v.dtype), kind="ExternalInput").ap()
           for n, v in arrays.items()}
    out = nc.dram_tensor("out_x", (P, B * D), F32, kind="ExternalOutput").ap()
    perceiver(nc, aps, out)
    r = run_bass_kernel_spmd(nc, [arrays], core_ids=[0])
    return r.results[0]["out_x"].reshape(P, B, D).transpose(1, 0, 2)
```

```python
from contextlib import ExitStack

import concourse.bass as bass
from concourse import mybir
from concourse.alu_op_type import AluOpType as ALU

F32 = mybir.dt.float32
F32R = mybir.dt.float32r
ACT = mybir.ActivationFunctionType
AX = mybir.AxisListType

P = 128
B = 2
D = 256
KD = D // P
NH, NKV = 16, 4
GH = NH // NKV
GW = GH * P
SE = 2048
NT = SE // P
NG = NKV * B
NC = SE // GW
FF = 1024
FB = FF // P
E0 = 8
E1, M1 = 32, 176
CH = 2
CW = CH * M1
IT = 8
NCH = IT // CH
BLOCKS = [(0, 2), (2, 5), (5, 8), (8, 11)]
SHW = 384
NB = IT * M1 // P
BIG = 3.0e38
SCALE = float(P) ** -0.5

KB = 1024
AT_CTX = 0
AT_S0 = 32 * KB
AT_S1 = 64 * KB
AT_V = 96 * KB
AT_QH = 128 * KB
AT_QL = 144 * KB
AT_MASK = 160 * KB
AT_K2 = 168 * KB
AT_M = 176 * KB
AT_SMALL = 186 * KB



PAUSES = (22, 8, 9, 12, 38, 12)
SW = (0, 1, 3, 4)


def rope_at(u):
    return u + u // NKV + 1


def column(e):
    return bass.ds(e, 1) if not isinstance(e, int) else slice(e, e + 1)


def perceiver(nc, a, out):
    ctx = ExitStack()
    base = (nc.sbuf_base + 31) // 32 * 32
    small = [AT_SMALL]

    def at(name, shape, offset, dtype=F32):
        n = 4
        for s in shape[1:]:
            n *= s
        assert base + offset + n <= nc.sbuf_usable_end, name
        return nc.alloc_sbuf_tensor_at(name, shape, dtype, offset=base + offset)

    def sb(name, *shape):
        t = at(name, [P, *shape], small[0])
        n = 4
        for s in shape:
            n *= s
        small[0] += (n + 31) // 32 * 32
        return t

    def sem(name):
        return ctx.enter_context(nc.semaphore(name))

    class Steps:

        def __init__(self, name):
            self.sem, self.n = sem(name), 0

        def __call__(self, ins):
            ins.then_inc(self.sem, 1)
            self.n += 1
            return self.n

    with ctx:
        ctxT = at("ctxT", [P, B, KD, SE], AT_CTX)
        S = at("S", [P, NT, GW], AT_S0)
        q_tok = at("q_tok", [P, B, NH, P], AT_S0)
        cdec = at("cdec", [P, SE], AT_S0 + 16 * KB)
        cprod = at("cprod", [P, SE], AT_S0 + 24 * KB)
        KH, KL = ([at(f"{n}{i}", [P, SE], AT_S1 + (2 * i + j) * 8 * KB, F32R) for i in range(2)]
                  for j, n in enumerate(("KH", "KL")))
        wq = at("wq", [P, KD, NH * P], AT_S1 + 16 * KB)
        V = [at(f"V{i}", [P, NT, P], AT_V + 2 * i * 8 * KB) for i in range(2)]
        K = at("K", [P, SE], AT_V + 8 * KB)
        bq = at("bq", [P, NH * P], AT_V + 16 * KB)
        qsq = at("qsq", [P, 2, GW], AT_V + 24 * KB)
        K2 = at("K2", [P, SE], AT_K2)
        QH = at("QH", [P, B, NKV, GW], AT_QH, F32R)
        QL = at("QL", [P, B, NKV, GW], AT_QL, F32R)
        OT = at("OT", [P, B, NKV, GW], AT_QH)
        maskT = at("maskT", [P, NT, P], AT_MASK)
        M = at("M", [P, GW], AT_M)
        psumsH = at("psumsH", [P, GW], AT_M + 2 * KB, F32R)
        psumsL = [at(f"psumsL{i}", [P, GW], AT_M + (2 + i) * 2 * KB, F32R) for i in range(2)]
        psums = [at(f"psums{i}", [P, GW], AT_M + (2 + i) * 2 * KB) for i in range(2)]
        cscratch = at("cscratch", [P, SE], AT_M)
        rden = at("rden", [P, GW], AT_M + 8 * KB)
        wo = at("wo", [P, NH, D], AT_CTX)
        wqkv = at("wqkv", [P, KD, 3 * D], AT_CTX + 16 * KB)
        wout = at("wout", [P, FB, D], AT_CTX + 22 * KB)
        wsw = at("wsw", [P, KD, 2 * FF], AT_S1)
        hsw = at("hsw", [P, FB, D], AT_S1 + 16 * KB)
        ww = at("ww", [P, B, 2 * D], AT_S1 + 24 * KB)
        w0 = at("w0", [P, E0 + 1, KD, 2 * D], AT_V)
        d0 = at("d0", [P, E0 + 1, KD, D], AT_S0)
        wq5 = at("wq5", [P, KD, NH * P], AT_CTX)
        wo5 = at("wo5", [P, NH, D], AT_CTX + 16 * KB)
        wkv5 = at("wkv5", [P, KD, 2 * NKV * P], AT_QL)

        hx = at("hx", [P, B, D], AT_MASK)
        yt = at("yt", [P, B, D], AT_MASK + 2 * KB)
        eq = at("eq", [P, B, D], AT_MASK + 4 * KB)
        yden = at("yden", [P, B, D], AT_MASK + 6 * KB)
        sq = at("sq", [P, 4, D], AT_MASK + 8 * KB)
        win = at("win", [P, KD, D], AT_CTX + 30 * KB)
        wlin = at("wlin", [P, KD, D], AT_S1 + 28 * KB)
        ssw = at("ssw", [P, 2, D], AT_QL + 8 * KB)
        sg0 = at("sg0", [P, 2, B, D], AT_QL + 10 * KB)
        hT0H = at("hT0H", [P, KD, B, P], AT_QL + 14 * KB, F32R)
        hT0L = at("hT0L", [P, KD, B, P], AT_QL + 8 * KB, F32R)
        w0H, w0L, d0H, d0L = (
            [at(f"{n}{i}", [P, KD, w], base_at + offset * KB, F32R)
             for i, base_at in enumerate((AT_S0 + 18 * KB, AT_QH + 4 * KB))]
            for n, w, offset in (("w0H", 2 * D, 0), ("w0L", 2 * D, 4), ("d0H", D, 8), ("d0L", D, 10)))
        x0H = at("x0H", [P, KD, B * P], AT_S1 + 24 * KB, F32R)
        x0L = at("x0L", [P, KD, B * P], AT_S1 + 26 * KB, F32R)
        h0 = at("h0", [P, 2, B, D], AT_M)
        rc = at("rc", [P, 2, GH, P], AT_S0)
        rs = at("rs", [P, 2, GH, P], AT_S0 + 4 * KB)
        rope = at("rope", [P, 2, GH, P], AT_S0 + 8 * KB)
        KT5 = at("KT5", [P, B, NKV, P], AT_S0 + 12 * KB)
        V5 = at("V5", [P, B, NKV, P], AT_S0 + 16 * KB)
        QT5 = [at(f"QT5{i}", [P, GH, P], AT_S0 + (20 + 2 * i) * KB) for i in range(2)]
        P5 = at("P5", [P, 2, GH, P], AT_S0 + 24 * KB)
        PT5 = at("PT5", [P, GH, P], AT_S0 + 28 * KB)
        OT5 = at("OT5", [P, GH, P], AT_S0 + 30 * KB)
        gu1 = [at(f"gu1{c}", [P, KD, 2 * CW], AT_S1 + c * 5632) for c in range(NCH)]
        dn1 = at("dn1", [P, NB, D], AT_S1 + 22 * KB)
        gush = at("gush", [P, KD, 2 * SHW], AT_S1 + 33 * KB)
        dnsh = at("dnsh", [P, SHW // P, D], AT_S1 + 39 * KB)
        h6 = at("h6", [P, B, IT * M1], AT_S1 + 42 * KB)
        sg6 = at("sg6", [P, B, SHW], AT_S1 + 53 * KB)
        guH, guL = ([at(f"{n}{i}", [P, KD, 2 * SHW], AT_QH + (2 * i + j) * 6 * KB, F32R) for i in range(2)]
                    for j, n in enumerate(("guH", "guL")))
        dnH, dnL = ([at(f"{n}{i}", [P, SHW // P, D], AT_MASK + (2 * i + j) * 3 * KB, F32R) for i in range(2)]
                    for j, n in enumerate(("dnH", "dnL")))
        xH = at("xH", [P, KD, B * P], AT_MASK + 12 * KB, F32R)
        xL = at("xL", [P, KD, B * P], AT_MASK + 14 * KB, F32R)
        hTH = at("hTH", [P, B, 3, P], AT_QH + 24 * KB, F32R)
        hTL = at("hTL", [P, B, 3, P], AT_QH + 27 * KB, F32R)

        late_at = [AT_M + 4 * KB]

        def late(name, *shape):
            t = at(name, [P, *shape], late_at[0])
            n = 4
            for s in shape:
                n *= s
            late_at[0] += (n + 31) // 32 * 32
            assert late_at[0] <= AT_SMALL
            return t

        nmax5 = late("nmax5", 2, GH * B * NKV)
        sum5 = late("sum5", 2, GH * B * NKV)
        sc1 = late("sc1", 3, B, E1)
        pair1 = late("pair1", 2, B * E1 // 4, 2)
        grp1 = late("grp1", 3, B * E1 // 4)
        gre1 = late("gre1", B, 16)
        top1 = late("top1", 4, 8)
        gsel1 = late("gsel1", B, E1 // 4)
        msk1 = late("msk1", 2, B, E1)
        comb = late("comb", B, E1)
        summ = late("summ", B, D)
        lin = late("lin", 3, KD, B)
        ssq = late("ssq", 4)
        nrstd = late("nrstd", 4)
        r0m = late("r0m", 4, B)
        r0s = late("r0s", B)

        x = sb("xres", B, D)
        xn = sb("xn", B, D)
        xnT = sb("xnT", KD, B * P)
        consts = sb("consts", 5, P)
        ident, tri, causal, cosT, sinT = (consts[:, i, :] for i in range(5))
        ones = sb("ones", P)
        onesR = at("onesR", [P, P], small[0], F32R)
        small[0] += P * 4
        wkv = sb("wkv", KD * 2 * P + 1)
        bv = sb("bv", NKV)
        cols = sb("cols", 8)
        stats = sb("stats", B, 6)
        mv = sb("mv", B, 2)
        var = sb("var", 32)
        rstd = sb("rstd", 32)
        kvar = sb("kvar", 2, NT)
        krstd = sb("krstd", 2, NT)
        halfneg = sb("halfneg", 32)
        qkn = sb("qkn", 1)
        qss = sb("qss", B, NH)
        mq = sb("mq", GH)
        sig = sb("sig", 4)
        csum = sb("csum", KD, B)
        rows = sb("rows", 3, D)
        warm = sb("warm", 1)
        router0 = sb("router0", KD, E0)
        router1 = sb("router1", KD, E1)
        r0 = sb("r0", 4, B, E0)
        sel0 = sb("sel0", B, E0 + 1)
        order = sb("order", E0)
        bias1 = sb("bias1", E1)
        gsc1 = sb("gsc1", B, 16)

        ps = [ctx.enter_context(nc.psum_tensor(f"ps{i}", [P, GW], F32)) for i in range(8)]
        SC = ps[0:3]
        PR = ps[3:5]
        QR = [ps[i] for i in (6, 7, 0, 1, 2, 3, 4, 6)]
        MISC, MB, PO = ps[5], ps[6], ps[7]

        in_x, in_consts, in_cols, in_bq, in_mask, in_bv = (
            sem(n) for n in ("in_x", "in_consts", "in_cols", "in_bq", "in_mask", "in_bv"))
        in_wq = [sem(f"in_wq{c}") for c in range(NKV)]
        in_wkv = sem("in_wkv")
        in_ctx = [[sem(f"in_ctx{b}{c}") for c in range(NC)] for b in range(B)]
        consts_set = sem("consts_set")
        var_ready, rstd_ready = sem("var_ready"), sem("rstd_ready")
        xn_ready, xT_done, xT_ready = sem("xn_ready"), sem("xT_done"), sem("xT_ready")
        q_done, q_biased, q_squared, q_summed = (sem(n) for n in ("q_done", "q_biased", "q_squared", "q_summed"))
        q_var, q_rstd, q_scaled = sem("q_var"), sem("q_rstd"), [sem("q_scaled0"), sem("q_scaled1")]
        qT_done, qT_ready = sem("qT_done"), sem("qT_ready")
        k_done, k_ready, v_done, v_ready = (sem(n) for n in ("k_done", "k_ready", "v_done", "v_ready"))
        kl_ready, ql_ready = sem("kl_ready"), sem("ql_ready")
        ksum_done, kvar_ready, krstd_ready = sem("ksum_done"), sem("kvar_ready"), sem("krstd_ready")
        s_done, s_ready, max_step = sem("s_done"), sem("s_ready"), sem("max_step")
        maxT_done, max_ready, mb_done = sem("maxT_done"), sem("max_ready"), sem("mb_done")
        sub_done, exp_done, psum_step = sem("sub_done"), sem("exp_done"), sem("psum_step")
        den_done, rden_ready, o_ready = (sem(n) for n in ("den_done", "rden_ready", "o_ready"))
        o_scaled, pv_done, last_sum = sem("o_scaled"), sem("pv_done"), sem("last_sum")
        onesR_set, psumsH_ready, psumsL_ready = sem("onesR_set"), sem("psumsH_ready"), sem("psumsL_ready")
        exp_dec, cdec_ready, cdec_summed = sem("exp_dec"), sem("cdec_ready"), sem("cdec_summed")
        dve_step = Steps("dve_step")
        csum_ready = sem("csum_ready")
        in_w2, in_wsw, in_lin, in_e0, in_w5, in_kv5, in_sh, in_rows = (
            sem(n) for n in ("in_w2", "in_wsw", "in_lin", "in_e0", "in_w5", "in_kv5", "in_sh", "in_rows"))
        in_gu = [sem(f"in_gu{c}") for c in range(NCH)]
        in_dn = [sem(f"in_dn{c}") for c in range(NCH)]
        qkv_done, qk_squared, nrstd_ready, w_ready, eq_ready, wv_ready, cum_done = (
            sem(n) for n in ("qkv_done", "qk_squared", "nrstd_ready", "w_ready", "eq_ready", "wv_ready", "cum_done"))
        sw_done, sw_silu, sw_ready = sem("sw_done"), sem("sw_silu"), sem("sw_ready")
        lin_done, lin_ready = sem("lin_done"), sem("lin_ready")
        max0_ready, tanh0_ready = sem("max0_ready"), sem("tanh0_ready")
        r0_done, sel0_ready, gu0_done, silu0_done, h0_ready, t0_done, hT0_ready = (
            sem(n) for n in ("r0_done", "sel0_ready", "gu0_done", "silu0_done", "h0_ready", "t0_done", "hT0_ready"))
        p5_done, rope_mul, rope_ready, v5_ready, t5_done, t5_ready, s5_done = (
            sem(n) for n in ("p5_done", "rope_mul", "rope_ready", "v5_ready", "t5_done", "t5_ready", "s5_done"))
        soft5, exp5, norm5, pT5_done, pT5_ready, o5_done, o5_ready = (
            sem(n) for n in ("soft5", "exp5", "norm5", "pT5_done", "pT5_ready", "o5_done", "o5_ready"))
        r1_done, exp1_done, comb_ready, gu6_done, silu6_done, h6_ready, t6_done, d6_done = (
            sem(n) for n in ("r1_done", "exp1_done", "comb_ready", "gu6_done", "silu6_done", "h6_ready", "t6_done",
                             "d6_done"))
        w0H_ready, w0L_ready, d0H_ready, d0L_ready, hT0L_ready, down0_done = (
            sem(n) for n in ("w0H_ready", "w0L_ready", "d0H_ready", "d0L_ready", "hT0L_ready", "down0_done"))
        hTH_ready, hTL_ready = sem("hTH_ready"), sem("hTL_ready")
        guH_ready, guL_ready, dnH_ready, dnL_ready, xH_ready, xL_ready = (
            sem(n) for n in ("guH_ready", "guL_ready", "dnH_ready", "dnL_ready", "xH_ready", "xL_ready"))
        in_wo = sem("in_wo")
        proj_done = sem("proj_done")
        out_stored = sem("out_stored")
        x_ready = sem("x_ready")

        block = ctx.enter_context(nc.Block())

        @block.sync
        def _(sp):
            sp.dma_start(x[:].rearrange("p b d -> p (b d)"), a["x"]).then_inc(in_x, 16)
            sp.dma_start(consts[:].rearrange("p b d -> p (b d)"), a["consts"]).then_inc(in_consts, 16)
            for c in range(NKV):
                sp.dma_start(wq[:, :, c * GW:(c + 1) * GW], a["wq"][:, :, c * GW:(c + 1) * GW]).then_inc(in_wq[c], 16)
            for c in range(NC):
                sp.dma_start(ctxT[:, 0, :, c * GW:(c + 1) * GW],
                             a["ctxT"][:, 0, :, c * GW:(c + 1) * GW]).then_inc(in_ctx[0][c], 16)
            sp.dma_start(maskT[:].rearrange("p t n -> p (t n)"), a["maskT"]).then_inc(in_mask, 16)
            for c in range(NC):
                sp.dma_start(ctxT[:, 1, :, c * GW:(c + 1) * GW],
                             a["ctxT"][:, 1, :, c * GW:(c + 1) * GW]).then_inc(in_ctx[1][c], 16)
            with sp.Fori(0, NKV - 1) as i:
                sp.wait_ge(ksum_done, 2 * i + 2)
                sp.dma_start(wkv[:], a["wkv"][:, i + 1, :]).then_inc(in_wkv, 16)
            sp.wait_ge(ksum_done, NG)
            sp.wait_ge(csum_ready, B * KD)
            sp.dma_start(wo[:].rearrange("p h d -> p (h d)"), a["wo"]).then_inc(in_wo, 16)
            sp.dma_start(wqkv[:].rearrange("p k n -> p (k n)"), a["wqkv"]).then_inc(in_w2, 16)
            sp.dma_start(wout[:].rearrange("p k n -> p (k n)"), a["wout"]).then_inc(in_w2, 16)
            sp.dma_start(win[:].rearrange("p k n -> p (k n)"), a["win"]).then_inc(in_lin, 16)
            sp.wait_ge(s_done, NG * NT)
            sp.dma_start(wlin[:].rearrange("p k n -> p (k n)"), a["wlin"]).then_inc(in_lin, 16)
            sp.dma_start(wsw[:].rearrange("p k n -> p (k n)"), a["wsw"]).then_inc(in_wsw, 16)
            sp.wait_ge(proj_done, 2)
            sp.dma_start(w0[:].rearrange("p e k n -> p (e k n)"), a["w0"]).then_inc(in_e0, 16)
            sp.dma_start(d0[:].rearrange("p e k n -> p (e k n)"), a["d0"]).then_inc(in_e0, 16)
            sp.wait_ge(proj_done, 4)
            sp.dma_start(wkv5[:].rearrange("p k n -> p (k n)"), a["wkv5"]).then_inc(in_kv5, 16)
            sp.dma_start(wq5[:].rearrange("p k n -> p (k n)"), a["wq5"]).then_inc(in_w5, 16)
            sp.dma_start(wo5[:].rearrange("p k n -> p (k n)"), a["wo5"]).then_inc(in_w5, 16)
            sp.wait_ge(proj_done, 6)
            sp.dma_start(gush[:].rearrange("p k n -> p (k n)"), a["gush"]).then_inc(in_sh, 16)
            sp.dma_start(dnsh[:].rearrange("p k n -> p (k n)"), a["downsh"]).then_inc(in_sh, 16)

            def load_chunk(c, turn):
                lo, hi = BLOCKS[c]
                sp.dma_start(gu1[c][:].rearrange("p k n -> p (k n)"),
                             a["gu1"].rearrange("p (i c) n -> p i c n", c=NCH)[:, turn, c, :]).then_inc(in_gu[c], 16)
                return (dn1[:, lo:hi, :], a["down1"].rearrange("p (i k) n -> p i k n", k=NB)[:, turn, lo:hi, :])

            for c in range(NCH):
                sp.dma_start(*load_chunk(c, 0)).then_inc(in_dn[c], 16)
            with sp.Fori(0, E1 // IT - 1) as i:
                for c in range(NCH):
                    sp.wait_ge(guL_ready, NCH * i + c + 2)
                    down = load_chunk(c, i + 1)
                    sp.wait_ge(dnL_ready, NCH * i + c + 2)
                    sp.dma_start(*down).then_inc(in_dn[c], 16)
            for b in range(B):
                sp.wait_ge(x_ready, b + 1)
                sp.dma_start(out[:, b * D:(b + 1) * D], x[:, b, :]).then_inc(out_stored, 16)
            sp.wait_ge(out_stored, 16 * B)

        @block.gpsimd
        def _(pool):
            nc.gpsimd.memset(ones[:], 1.0)
            nc.gpsimd.memset(sel0[:, :, 0:1], 1.0)
            nc.gpsimd.memset(gsc1[:], -BIG)
            for e in range(E0):
                nc.gpsimd.memset(order[:, e:e + 1], float(E0 - e))
            nc.gpsimd.memset(halfneg[:], -0.5).then_inc(consts_set, 1)
            pool.wait_ge(consts_set, 1)

            def rsqrt(dst, src, n):
                return nc.gpsimd.tensor_tensor(dst, src, halfneg[:, 0:n], ALU.pow)

            pool.wait_ge(var_ready, 1)
            rsqrt(rstd[:, 0:B], var[:, 0:B], B).then_inc(rstd_ready, 1)
            pool.wait_ge(q_var, 1)
            rsqrt(rstd[:], var[:], B * NH).then_inc(q_rstd, 1)
            pool.wait_ge(q_rstd, 1)
            nc.gpsimd.tensor_tensor(q_tok[:, 1], q_tok[:, 1], rstd[:, NH:2 * NH].unsqueeze(2).broadcast_to([P, NH, P]),
                                    ALU.mult).then_inc(q_scaled[1], 1)

            def key_norms(g, b):
                pool.wait_ge(kvar_ready, g + 1)
                rsqrt(krstd[:, b, :], kvar[:, b, :], NT).then_inc(krstd_ready, 1)

            def sum_probs(g, b, tiles):
                for j in tiles:
                    pool.wait_ge(exp_done, g * NT + j + 1)
                    if j > 1:
                        pool.wait_ge(psum_step, g * (NT - 1) + j - 1)
                    nc.gpsimd.tensor_tensor(psums[b][:], S[:, 0, :] if j == 1 else psums[b][:],
                                            S[:, j, :], ALU.add).then_inc(psum_step, 1)

            def key_lows(g, b):
                for t in range(NC):
                    pool.wait_ge(k_ready, NC * g + t + 1)
                    chunk = slice(t * GW, (t + 1) * GW)
                    nc.gpsimd.tensor_tensor(KL[b][:, chunk], K[:, chunk], KH[b][:, chunk].bitcast(F32),
                                            ALU.subtract).then_inc(kl_ready, 1)

            def half(n, b, scores=True, pv=True, keys=True):
                if pv:
                    pool.wait_ge(psumsH_ready, n + 1)
                    nc.gpsimd.tensor_tensor(psumsL[b][:], psums[b][:], psumsH[:].bitcast(F32),
                                            ALU.subtract).then_inc(psumsL_ready, 1)
                if keys:
                    key_lows(n + 2, b)
                if scores:
                    sum_probs(n + 1, 1 - b, range(1, 7))
                if keys:
                    key_norms(n + 2, b)
                if scores:
                    sum_probs(n + 1, 1 - b, range(7, NT // 2 if isinstance(n, int) and n == NG - 2 else NT))

            key_lows(0, 0)
            key_norms(0, 0)
            half(-1, 1, pv=False)
            with pool.Fori(0, NKV - 1) as i:
                half(2 * i, 0)
                half(2 * i + 1, 1)
            half(NG - 2, 0, keys=False)

            def norms(requests):
                for n, width in requests:
                    pool.wait_ge(var_ready, n)
                    rsqrt(rstd[:, 0:width], var[:, 0:width], width).then_inc(rstd_ready, 1)

            def expert_low(e, par):
                pool.wait_ge(w0H_ready, e + 1)
                nc.gpsimd.tensor_tensor(w0L[par][:], w0[:, e], w0H[par][:].bitcast(F32),
                                        ALU.subtract).then_inc(w0L_ready, 1)

            norms(((2, 4), (3, 4)))
            expert_low(0, 0)
            expert_low(1, 1)
            norms(((4, 2),))
            expert_low(2, 0)
            with pool.Fori(0, 3) as i:
                expert_low(2 * i + 3, 1)
                expert_low(2 * i + 4, 0)
            norms(((5, 2), (6, 2), (7, 2)))
            def gate_up_low(step, par, src, width):
                pool.wait_ge(guH_ready, step + 1)
                nc.gpsimd.tensor_tensor(guL[par][:, :, 0:width], src[:], guH[par][:, :, 0:width].bitcast(F32),
                                        ALU.subtract).then_inc(guL_ready, 1)

            gate_up_low(0, 0, gush, 2 * SHW)
            gate_up_low(1, 1, gu1[0], 2 * CW)
            pool.wait_ge(var_ready, 8)
            rsqrt(rstd[:, 0:B], var[:, 0:B], B).then_inc(rstd_ready, 1)
            for c in range(1, NCH):
                gate_up_low(c + 1, (c + 1) % 2, gu1[c], 2 * CW)
            with pool.Fori(1, E1 // IT) as i:
                for c in range(NCH):
                    gate_up_low(NCH * i + c + 1, (c + 1) % 2, gu1[c], 2 * CW)

        @block.scalar
        def _(act):
            act.dma_start(cols[:], a["cols"]).then_inc(in_cols, 16)
            act.dma_start(bq[:], a["bq"].broadcast_to([P, NH * P])).then_inc(in_bq, 16)
            act.dma_start(wkv[:], a["wkv"][:, 0, :]).then_inc(in_wkv, 16)
            act.dma_start(bv[:], a["bv"]).then_inc(in_bv, 16)
            act.dma_start(rows[:].rearrange("p g d -> p (g d)"), a["rows"].broadcast_to([P, 3 * D])).then_inc(in_rows, 16)
            act.dma_start(router0[:].rearrange("p k d -> p (k d)"), a["router0"]).then_inc(in_rows, 16)
            act.dma_start(router1[:].rearrange("p k d -> p (k d)"), a["router1"]).then_inc(in_rows, 16)
            act.dma_start(bias1[:], a["bias1"].broadcast_to([P, E1])).then_inc(in_rows, 16)
            act.wait_ge(in_cols, 16)
            act.wait_ge(consts_set, 1)
            nc.scalar.activation(onesR[:], ones[:], ACT.Copy).then_inc(onesR_set, 1)
            nc.scalar.activation(sig[:, 0:1], cols[:, 4:5], ACT.Exp, scale=-1.0).then_inc(exp_dec, 1)
            for u in range(B * NKV):
                act.wait_ge(q_biased, u + 1)
                if u >= 2:
                    act.wait_ge(q_summed, u - 1)
                nc.scalar.activation(qsq[:, u % 2, :], q_tok[:, u % B, u // B * GH:(u // B + 1) * GH, :],
                                     ACT.Square).then_inc(q_squared, 1)

            bk = wkv[:, KD * 2 * P:KD * 2 * P + 1]

            def key_chunk(g, b, t):
                act.wait_ge(k_done, NC * g + t + 1)
                if not isinstance(g, int) or g:
                    act.wait_ge(kl_ready, NC * (g - 1) + t + 1)
                nc.scalar.activation(K[:, t * GW:(t + 1) * GW], PR[t % 2][:], ACT.Identity, bias=bk)
                nc.scalar.activation(KH[b][:, t * GW:(t + 1) * GW], PR[t % 2][:], ACT.Identity, bias=bk)
                nc.scalar.activation(K2[:, t * GW:(t + 1) * GW], PR[t % 2][:], ACT.Square,
                                     bias=bk).then_inc(k_ready, 1)

            def value_chunk(g, b, t):
                act.wait_ge(v_done, NC * g + t + 1)
                nc.scalar.activation(V[b][:, 4 * t:4 * t + 4, :].rearrange("p t d -> p (t d)"), PR[t % 2][:],
                                     ACT.Copy).then_inc(v_ready, 1)

            def outputs(g, b, kvh):
                act.wait_ge(o_scaled, g + 1)
                nc.scalar.activation(OT[:, b, kvh, :], OT[:, b, kvh, :], ACT.Identity,
                                     bias=bv[:, column(kvh)]).then_inc(o_ready, 1)

            def exps(g, b, tiles):
                for j in tiles:
                    act.wait_ge(sub_done, g * NT + j + 1)
                    nc.scalar.activation(S[:, j, :], S[:, j, :], ACT.Exp).then_inc(exp_done, 1)

            def half(n, b, kvh, scores=True, pv=True, keys=True):
                if pv and scores:
                    act.wait_ge(psum_step, (n + 1) * (NT - 1))
                    nc.scalar.activation(psumsH[:], psums[b][:], ACT.Copy).then_inc(psumsH_ready, 1)
                after = [0, 0, 0, 0, 1, 3, 5, 7, NT]
                for t in range(2 * NC):
                    if keys:
                        (key_chunk if t < NC else value_chunk)(n + 2, b, t % NC)
                    if t == NC - 1 and pv:
                        outputs(n, b, kvh)
                    if scores:
                        exps(n + 1, 1 - b, range(after[t], after[t + 1]))

            for t in range(NC):
                key_chunk(0, 0, t)
            def query_high(units):
                for u in units:
                    act.wait_ge(qT_done, u + 1)
                    nc.scalar.activation(QH[:, u // NKV, u % NKV, :], QR[u][:], ACT.Identity,
                                         scale=qkn[:, 0:1]).then_inc(qT_ready, 1)

            act.wait_ge(cdec_ready, 1)
            nc.scalar.activation(cscratch[:], cdec[:], ACT.Copy, accum_out=sig[:, 3:4]).then_inc(cdec_summed, 1)
            value_chunk(0, 0, 0)
            value_chunk(0, 0, 1)
            query_high(range(5))
            value_chunk(0, 0, 2)
            value_chunk(0, 0, 3)
            query_high(range(5, B * NKV))
            half(-1, 1, -1, pv=False)
            act.wait_ge(in_bv, 16)
            with act.Fori(0, NKV - 1) as i:
                half(2 * i, 0, i)
                half(2 * i + 1, 1, i)
            half(NG - 2, 0, NKV - 1, keys=False)
            half(NG - 1, 1, NKV - 1, scores=False, keys=False)

            def silu_tables():
                nc.scalar.activation(warm[:], ones[:, 0:1], ACT.Silu)

            for b in range(B):
                act.wait_ge(qkv_done, 2 * b + 1)
                for i in range(2):
                    nc.scalar.activation(sq[:, 2 * b + i, :], ps[b][:, i * D:(i + 1) * D], ACT.Square,
                                         accum_out=ssq[:, 2 * b + i:2 * b + i + 1]).then_inc(qk_squared, 1)
            act.wait_ge(rstd_ready, 3)
            for b in range(B):
                nc.scalar.activation(ww[:, b, D:2 * D], ps[b][:, D:2 * D], ACT.Exp,
                                     scale=rstd[:, 2 * b + 1:2 * b + 2]).then_inc(w_ready, 1)
            act.wait_ge(nrstd_ready, 1)
            for b in range(B):
                nc.scalar.activation(eq[:, b, :], ps[b][:, 0:D], ACT.Exp,
                                     scale=nrstd[:, 2 * b:2 * b + 1]).then_inc(eq_ready, 1)
            silu_tables()
            act.wait_ge(in_e0, 32)
            for e in range(2):
                nc.scalar.activation(w0H[e][:], w0[:, e], ACT.Copy).then_inc(w0H_ready, 1)
                nc.scalar.activation(d0H[e][:], d0[:, e], ACT.Copy).then_inc(d0H_ready, 1)
            for f in range(FB):
                act.wait_ge(sw_done, f + 1)
                if f >= 2:
                    act.wait_ge(sw_ready, f - 1)
                nc.scalar.activation(ssw[:, f % 2, :], ps[SW[f % 4]][:, D:2 * D], ACT.Silu).then_inc(sw_silu, 1)

            def silu0(e, par, batches=range(B)):
                for b in batches:
                    act.wait_ge(gu0_done, B * e + b + 1)
                    nc.scalar.activation(sg0[:, par, b, :], ps[1 + 2 * par + b][:, 0:D], ACT.Silu,
                                         scale=sel0[:, b, column(e)]).then_inc(silu0_done, 1)

            def turned0(e):
                act.wait_ge(t0_done, e + 1)
                nc.scalar.activation(hT0H[:].rearrange("p k b t -> p (k b t)"), ps[5][:], ACT.Copy).then_inc(hT0_ready, 1)

            def gates_high(e, par):
                nc.scalar.activation(w0H[par][:], w0[:, e], ACT.Copy).then_inc(w0H_ready, 1)

            def down_high0(e, par):
                act.wait_ge(down0_done, e - 1)
                nc.scalar.activation(d0H[par][:], d0[:, e], ACT.Copy).then_inc(d0H_ready, 1)

            def step0(e, par, more=True, gates=True, downs=True):
                turned0(e)
                if more:
                    silu0(e + 1, 1 - par)
                if gates:
                    gates_high(e + 3, 1 - par)
                if downs:
                    down_high0(e + 2, par)

            act.wait_ge(max0_ready, 1)
            nc.scalar.activation(r0s[:], r0m[:, 0], ACT.Tanh, scale=0.5).then_inc(tanh0_ready, 1)
            silu0(0, 0)
            gates_high(2, 0)
            act.wait_ge(sel0_ready, 1)
            step0(0, 0)
            with act.Fori(0, 2) as i:
                step0(2 * i + 1, 1)
                step0(2 * i + 2, 0)
            step0(E0 - 3, 1)
            step0(E0 - 2, 0, gates=False)
            step0(E0 - 1, 1, gates=False, downs=False)
            step0(E0, 0, more=False, gates=False, downs=False)
            nc.scalar.activation(warm[:], ones[:, 0:1], ACT.Exp)

            def turned5(r, dst):
                act.wait_ge(t5_done, r + 1)
                nc.scalar.activation(dst, ps[2][:].rearrange("p (h t) -> p h t", h=GH), ACT.Copy).then_inc(t5_ready, 1)

            def gate_up_high(step, par, src, width):
                nc.scalar.activation(guH[par][:, :, 0:width], src[:], ACT.Copy).then_inc(guH_ready, 1)

            def split_gate_up(step, c, turn):
                act.wait_ge(in_gu[c], 16 * (turn + 1))
                gate_up_high(step, (c + 1) % 2, gu1[c], 2 * CW)

            for s in range(B * NKV + 2):
                b, c = divmod(s, NKV)
                if s < B * NKV and c == 0:
                    act.wait_ge(p5_done, 6 * b + 2)
                    nc.scalar.activation(V5[:, b].rearrange("p g d -> p (g d)"), ps[1][:], ACT.Copy).then_inc(v5_ready, 1)
                u = s - 1
                if 0 <= u < B * NKV:
                    if u % NKV == 0:
                        turned5(rope_at(u) - 1, KT5[:, u // NKV])
                    turned5(rope_at(u), QT5[u % 2][:])
                if 0 <= s - 2:
                    act.wait_ge(pT5_done, s - 1)
                    nc.scalar.activation(PT5[:].rearrange("p h t -> p (h t)"), ps[3][:], ACT.Copy).then_inc(pT5_ready, 1)
                    act.wait_ge(o5_done, s - 1)
                    nc.scalar.activation(OT5[:].rearrange("p h t -> p (h t)"), ps[5][:], ACT.Copy).then_inc(o5_ready, 1)
                if 0 <= u < B * NKV:
                    act.wait_ge(soft5, u + 1)
                    for h in range(GH):
                        last = nc.scalar.activation(P5[:, u % 2, h, :], P5[:, u % 2, h, :], ACT.Exp,
                                                    bias=nmax5[:, 1, u * GH + h:u * GH + h + 1],
                                                    accum_out=sum5[:, 0, u * GH + h:u * GH + h + 1])
                    last.then_inc(exp5, 1)
                if s == B * NKV - 3:
                    act.wait_ge(in_sh, 32)
                    gate_up_high(0, 0, gush, 2 * SHW)
                if s == B * NKV - 2:
                    split_gate_up(1, 0, 0)

            def silu6(step, width, batches=range(B)):
                for b in batches:
                    act.wait_ge(gu6_done, B * step + b + 1)
                    nc.scalar.activation(sg6[:, b, 0:width], ps[2 * b][:, 0:width], ACT.Silu).then_inc(silu6_done, 1)

            def turned6(step, n):
                for b in range(B):
                    act.wait_ge(t6_done, B * step + b + 1)
                    nc.scalar.activation(hTH[:, b, 0:n, :].rearrange("p k t -> p (k t)"), ps[4 + b][:, 0:n * P],
                                         ACT.Copy).then_inc(hTH_ready, 1)

            def down_high(step, par, src, n):
                nc.scalar.activation(dnH[par][:, 0:n], src, ACT.Copy).then_inc(dnH_ready, 1)

            def split_down(step, c, turn, first=False):
                lo, hi = BLOCKS[c]
                act.wait_ge(in_dn[c], 16 * (turn + 1))
                if not first:
                    act.wait_ge(d6_done, step - 1)
                down_high(step, (c + 1) % 2, dn1[:, lo:hi], hi - lo)

            def step6(step, n, more=True, gu_next=None, dn_next=None):
                if more:
                    silu6(step + 1, CW, range(1))
                turned6(step, n)
                if more:
                    silu6(step + 1, CW, range(1, B))
                if gu_next:
                    split_gate_up(step + 3, *gu_next)
                if dn_next:
                    split_down(step + 2, *dn_next)

            def after(c, n, turn):
                return (c + n) % NCH, turn + (c + n) // NCH

            down_high(0, 0, dnsh[:], SHW // P)
            split_down(1, 0, 0, first=True)
            act.wait_ge(r1_done, 1)
            nc.scalar.activation(sc1[:, 0].rearrange("p b e -> p (b e)"), ps[4][:, 0:B * E1], ACT.Exp,
                                 scale=-1.0).then_inc(exp1_done, 1)
            silu_tables()
            silu6(0, SHW)
            split_gate_up(2, 1, 0)
            step6(0, SHW // P, gu_next=(2, 0), dn_next=(1, 0))
            with act.Fori(0, E1 // IT - 1) as i:
                for c in range(NCH):
                    step6(NCH * i + c + 1, BLOCKS[c][1] - BLOCKS[c][0], gu_next=after(c, 3, i), dn_next=after(c, 2, i))
            for c in range(NCH):
                step6(E1 // CH - NCH + c + 1, BLOCKS[c][1] - BLOCKS[c][0], more=c < NCH - 1,
                      gu_next=after(c, 3, E1 // IT - 1) if c + 3 < NCH else None,
                      dn_next=after(c, 2, E1 // IT - 1) if c + 2 < NCH else None)

        @block.vector
        def _(dve):
            def row_stats(src):
                for b in range(B):
                    c = dve_step(nc.vector.bn_stats(stats[:, b, :], src[:, b, :]))
                dve.wait_ge(dve_step.sem, c)
                for b in range(B):
                    c = dve_step(nc.vector.bn_aggr(mv[:, b, :], stats[:, b, :]))
                dve.wait_ge(dve_step.sem, c)

            def row_stats_eps(src):
                row_stats(src)
                nc.vector.tensor_scalar(var[:, 0:B], mv[:, :, 1], 1e-5, None, ALU.add).then_inc(var_ready, 1)

            def norm_stats(src, n):
                row_stats_eps(src)
                dve.wait_ge(rstd_ready, n)

            def normalise(dst, src, sem_, n):
                norm_stats(src, n)
                for b in range(B):
                    last = nc.vector.tensor_scalar(dst[:, b, :], src[:, b, :], mv[:, b, 0:1], rstd[:, b:b + 1],
                                                   ALU.subtract, ALU.mult)
                last.then_inc(sem_, 1)

            dve.wait_ge(in_x, 16)
            normalise(xn, x, xn_ready, 1)
            dve.wait_ge(xT_done, 1)
            nc.vector.tensor_copy(xnT[:].rearrange("p k n -> p (k n)"), SC[0][:]).then_inc(xT_ready, 1)
            dve.wait_ge(in_bq, 16)
            for u in range(B * NKV + 1):
                if u < B * NKV:
                    dve.wait_ge(q_done, u + 1)
                    nc.vector.tensor_tensor(q_tok[:, u % B, u // B * GH:(u // B + 1) * GH, :].rearrange("p h d -> p (h d)"),
                                            SC[1 + u % 2][:], bq[:, u // B * GW:(u // B + 1) * GW],
                                            ALU.add).then_inc(q_biased, 1)
                if u:
                    dve.wait_ge(q_squared, u)
                    v = u - 1
                    nc.vector.reduce_sum(qss[:, v % B, v // B * GH:(v // B + 1) * GH],
                                         qsq[:, v % 2, :].rearrange("p (h d) -> p h d", h=GH), AX.X).then_inc(q_summed, 1)
            dve.wait_ge(q_summed, B * NKV)
            nc.vector.tensor_scalar(var[:], qss[:].rearrange("p b h -> p (b h)"), 1.0 / P, 1e-6,
                                    ALU.mult, ALU.add).then_inc(q_var, 1)
            def context_sum(b):
                for t in range(NC):
                    dve.wait_ge(in_ctx[b][t], 16)
                for k in range(KD):
                    if b + k:
                        dve.wait_ge(csum_ready, b * KD + k)
                    nc.vector.tensor_tensor_reduce(cprod[:], ctxT[:, b, k, :], cdec[:], 1.0, 0.0, ALU.mult, ALU.add,
                                                   csum[:, k, b:b + 1]).then_inc(csum_ready, 1)

            dve.wait_ge(exp_dec, 1)
            dve.wait_ge(consts_set, 1)
            c = dve_step(nc.vector.tensor_scalar(sig[:, 1:2], sig[:, 0:1], 1.0, None, ALU.add))
            dve_step(nc.vector.tensor_tensor(qkn[:], cols[:, 0:1], cols[:, 1:2], ALU.mult))
            dve.wait_ge(dve_step.sem, c)
            c = dve_step(nc.vector.reciprocal(sig[:, 2:3], sig[:, 1:2]))
            dve.wait_ge(dve_step.sem, c)
            dve_step(nc.vector.tensor_scalar(qkn[:], qkn[:], SCALE, None, ALU.mult))
            nc.vector.tensor_tensor_scan(cdec[:, ::-1], sig[:, 2:3].broadcast_to([P, SE]),
                                         ones[:, 0:1].broadcast_to([P, SE]), 0.0, ALU.mult, ALU.add).then_inc(cdec_ready, 1)
            dve.wait_ge(cdec_ready, 1)
            context_sum(0)
            dve.wait_ge(q_rstd, 1)
            nc.vector.tensor_tensor(q_tok[:, 0], q_tok[:, 0], rstd[:, 0:NH].unsqueeze(2).broadcast_to([P, NH, P]),
                                    ALU.mult).then_inc(q_scaled[0], 1)
            context_sum(1)
            dve.wait_ge(csum_ready, B * KD)

            def key_vars(g, b):
                dve.wait_ge(ksum_done, g + 1)
                nc.vector.tensor_scalar(kvar[:, b, :], MISC[:, 0:NT], 1.0 / P, 1e-6, ALU.mult, ALU.add).then_inc(kvar_ready, 1)

            def running_max(g, b, j):
                dve.wait_ge(s_ready, g * NT + j + 1)
                if j > 1:
                    dve.wait_ge(max_step, g * (NT - 1) + j - 1)
                nc.vector.tensor_tensor(M[:], S[:, 0, :] if j == 1 else M[:], S[:, j, :],
                                        ALU.max).then_inc(max_step, 1)

            def score_tiles(g, b, first):
                dve.wait_ge(krstd_ready, g + 1)
                for j in range(NT):
                    dve.wait_ge(s_done, g * NT + j + 1)
                    if not first:
                        dve.wait_ge(psum_step, (g - 1) * (NT - 1) + max(j, 1))
                    nc.vector.scalar_tensor_tensor(
                        out=S[:, j, :].rearrange("p (h q) -> p h q", h=GH),
                        in0=SC[j % 3][:].rearrange("p (h q) -> p h q", h=GH), scalar=krstd[:, b, j:j + 1],
                        in1=maskT[:, j, :].unsqueeze(1).broadcast_to([P, GH, P]),
                        op0=ALU.mult, op1=ALU.add).then_inc(s_ready, 1)
                    if j >= 2:
                        running_max(g, b, j - 1)
                running_max(g, b, NT - 1)

            def reduce_maxima(g):
                dve.wait_ge(maxT_done, g + 1)
                nc.vector.reduce_max(mq[:], SC[2][:].rearrange("p (h k) -> p h k", h=GH), AX.X).then_inc(max_ready, 1)

            def reciprocals(g):
                dve.wait_ge(den_done, g + 1)
                nc.vector.reciprocal(rden[:], MISC[:]).then_inc(rden_ready, 1)

            def outputs(g, b, kvh):
                dve.wait_ge(pv_done, g + 1)
                dve.wait_ge(rden_ready, g + 1)
                nc.vector.tensor_tensor(OT[:, b, kvh, :], PO[:], rden[:], ALU.mult).then_inc(o_scaled, 1)

            def subtract_maxima(g, b, tiles):
                dve.wait_ge(mb_done, g + 1)
                for j in tiles:
                    nc.vector.tensor_tensor(S[:, j, :], S[:, j, :], MB[:], ALU.subtract).then_inc(sub_done, 1)

            def half(n, b, kvh, scores=True, pv=True, keys=True):
                if scores:
                    score_tiles(n + 1, 1 - b, not pv)
                if pv:
                    reciprocals(n)
                if scores:
                    reduce_maxima(n + 1)
                if pv:
                    outputs(n, b, kvh)
                if scores:
                    subtract_maxima(n + 1, 1 - b, range(NT))
                if keys:
                    key_vars(n + 2, b)

            for u in range(B * NKV):
                dve.wait_ge(qT_ready, u + 1)
                nc.vector.scalar_tensor_tensor(out=QL[:, u // NKV, u % NKV, :], in0=QR[u][:], scalar=qkn[:, 0:1],
                                               in1=QH[:, u // NKV, u % NKV, :].bitcast(F32),
                                               op0=ALU.mult, op1=ALU.subtract).then_inc(ql_ready, 1)
                if u == 4:
                    key_vars(0, 0)
            dve.wait_ge(in_mask, 16)
            dve.wait_ge(cdec_summed, 1)
            half(-1, 1, -1, pv=False)
            with dve.Fori(0, NKV - 1) as i:
                half(2 * i, 0, i)
                half(2 * i + 1, 1, i)
            half(NG - 2, 0, NKV - 1, keys=False)
            g, b = NG - 1, 1
            for j in range(NT // 2 + 1, NT):
                dve.wait_ge(exp_done, g * NT + j + 1)
                c = dve_step(nc.vector.tensor_tensor(M[:], S[:, j - 1, :] if j == NT // 2 + 1 else M[:], S[:, j, :], ALU.add))
                dve.wait_ge(dve_step.sem, c)
            dve.wait_ge(psum_step, g * (NT - 1) + NT // 2 - 1)
            nc.vector.tensor_tensor(psums[b][:], psums[b][:], M[:], ALU.add).then_inc(last_sum, 1)
            half(NG - 1, 1, NKV - 1, scores=False, keys=False)

            def add_to_x(n, bank=6):
                for b in range(B):
                    dve.wait_ge(proj_done, n + b)
                    last = nc.vector.tensor_tensor(x[:, b, :], x[:, b, :], ps[bank + b][:, 0:D], ALU.add)
                    if n == 9:
                        last.then_inc(x_ready, 1)
                if n < 9:
                    dve.wait_ge(dve_step.sem, dve_step(last))

            def copy_turned(n):
                dve.wait_ge(xT_done, n)
                nc.vector.tensor_copy(xnT[:].rearrange("p k n -> p (k n)"), ps[2][:]).then_inc(xT_ready, 1)

            def then(ins):
                dve.wait_ge(dve_step.sem, dve_step(ins))

            add_to_x(1, 0)
            row_stats(x)
            then(nc.vector.tensor_scalar(var[:, 0:B], mv[:, :, 1], 1e-5, None, ALU.add))
            then(nc.vector.reciprocal(ssq[:, 0:B], var[:, 0:B]))
            then(nc.vector.tensor_tensor(ssq[:, B:2 * B], ssq[:, 0:B], mv[:, :, 1], ALU.mult))
            nc.vector.tensor_scalar(var[:, B:2 * B], ssq[:, B:2 * B], 1.1920929e-07, None, ALU.add).then_inc(var_ready, 1)
            dve.wait_ge(rstd_ready, 2)
            for b in range(B):
                c = dve_step(nc.vector.tensor_scalar(xn[:, b, :], x[:, b, :], mv[:, b, 0:1], rstd[:, b:b + 1],
                                                     ALU.subtract, ALU.mult))
            for b in range(B):
                dve.wait_ge(dve_step.sem, c - 1 + b)
                last = nc.vector.tensor_scalar(hx[:, b, :], xn[:, b, :], rstd[:, B + b:B + b + 1], None, ALU.mult)
            last.then_inc(xn_ready, 1)
            then(nc.vector.tensor_tensor(x[:], x[:], xn[:], ALU.add))
            copy_turned(2)
            dve.wait_ge(cdec_summed, 1)
            c = dve_step(nc.vector.tensor_scalar(lin[:, 0, :, 0], cols[:, 2:4], sig[:, 3:4], None, ALU.mult))
            dve.wait_ge(dve_step.sem, c)
            dve.wait_ge(lin_done, 1)
            then(nc.vector.tensor_tensor(lin[:, 1], ps[7][:, 0:KD * B].rearrange("p (k b) -> p k b", b=B),
                                         lin[:, 0, :, 0:1].broadcast_to([P, KD, B]), ALU.add))
            nc.vector.tensor_scalar(lin[:, 2], lin[:, 1], 1.0 / SE, None, ALU.mult).then_inc(lin_ready, 1)
            dve.wait_ge(qk_squared, 2 * B)
            nc.vector.tensor_scalar(var[:, 0:4], ssq[:], 1.0 / D, 1.1920929e-07, ALU.mult, ALU.add).then_inc(var_ready, 1)
            dve.wait_ge(rstd_ready, 3)
            nc.vector.tensor_scalar(nrstd[:], rstd[:, 0:4], -1.0, None, ALU.mult).then_inc(nrstd_ready, 1)
            for b in range(B):
                dve.wait_ge(w_ready, b + 1)
                dve.wait_ge(qkv_done, 2 * b + 2)
                nc.vector.tensor_tensor(ww[:, b, 0:D], ww[:, b, D:2 * D], ps[3 + b][:, 0:D], ALU.mult).then_inc(wv_ready, 1)
            dve.wait_ge(eq_ready, B)
            then(nc.vector.tensor_scalar(eq[:], eq[:], 1.0, None, ALU.add))
            for b in range(B):
                dve.wait_ge(cum_done, b + 1)
                d = dve_step(nc.vector.scalar_tensor_tensor(out=yden[:, b, :], in0=ps[5 + b][:, D:2 * D], scalar=1e-6,
                                                            in1=eq[:, b, :], op0=ALU.add, op1=ALU.mult))
            for b in range(B):
                dve.wait_ge(dve_step.sem, d - 1 + b)
                c = dve_step(nc.vector.reciprocal(yden[:, b, :], yden[:, b, :]))
            for b in range(B):
                dve.wait_ge(dve_step.sem, c - 1 + b)
                last = nc.vector.tensor_tensor(yt[:, b, :], ps[5 + b][:, 0:D], yden[:, b, :], ALU.mult)
            last.then_inc(xn_ready, 1)
            copy_turned(3)

            def down_low0(e, par):
                dve.wait_ge(d0H_ready, e + 1)
                nc.vector.tensor_tensor(d0L[par][:], d0[:, e], d0H[par][:].bitcast(F32),
                                        ALU.subtract).then_inc(d0L_ready, 1)

            down_low0(0, 0)
            down_low0(1, 1)
            for f in range(FB):
                dve.wait_ge(sw_silu, f + 1)
                nc.vector.tensor_tensor(hsw[:, f, :], ps[SW[f % 4]][:, 0:D], ssw[:, f % 2, :], ALU.mult).then_inc(sw_ready, 1)
            dve.wait_ge(in_rows, 64)
            dve.wait_ge(lin_done, 2)
            nc.vector.tensor_tensor(summ[:], ps[7][:].rearrange("p (b d) -> p b d", b=B),
                                    rows[:, 0:1, :].broadcast_to([P, B, D]), ALU.add).then_inc(lin_ready, 1)
            add_to_x(3, 5)

            def normalise_x(n, nx):
                norm_stats(x, n)
                for b in range(B):
                    last = nc.vector.tensor_scalar(xn[:, b, :], x[:, b, :], mv[:, b, 0:1], rstd[:, b:b + 1],
                                                   ALU.subtract, ALU.mult)
                last.then_inc(xn_ready, 1)
                copy_turned(nx)

            def split_tokens(high, low, n):
                flat = lambda t: t[:].rearrange("p k n -> p (k n)")
                nc.vector.tensor_copy(flat(high), ps[2][:]).then_inc(xH_ready, 1)
                dve.wait_ge(xH_ready, n)
                nc.vector.tensor_tensor(flat(low), ps[2][:], flat(high).bitcast(F32), ALU.subtract).then_inc(xL_ready, 1)

            normalise_x(4, 4)
            split_tokens(x0H, x0L, 1)
            dve.wait_ge(r0_done, 1)
            lg = ps[0][:, 0:B * E0].rearrange("p (b e) -> p b e", b=B)
            nc.vector.reduce_max(r0m[:, 0], lg, AX.X).then_inc(max0_ready, 1)
            dve.wait_ge(max0_ready, 1)
            then(nc.vector.tensor_tensor(r0[:, 0], lg, r0m[:, 0].unsqueeze(2).broadcast_to([P, B, E0]), ALU.is_equal))
            then(nc.vector.tensor_tensor(r0[:, 1], r0[:, 0], order[:].unsqueeze(1).broadcast_to([P, B, E0]), ALU.mult))
            then(nc.vector.reduce_max(r0m[:, 2], r0[:, 1], AX.X))
            then(nc.vector.tensor_tensor(r0[:, 2], r0[:, 1], r0m[:, 2].unsqueeze(2).broadcast_to([P, B, E0]), ALU.is_equal))
            dve.wait_ge(tanh0_ready, 1)
            then(nc.vector.tensor_scalar(r0m[:, 3], r0s[:], 0.5, 0.5, ALU.mult, ALU.add))
            nc.vector.tensor_tensor(sel0[:, :, 1:E0 + 1], r0[:, 2], r0m[:, 3].unsqueeze(2).broadcast_to([P, B, E0]),
                                    ALU.mult).then_inc(sel0_ready, 1)
            dve.wait_ge(sel0_ready, 1)

            def products0(e, par):
                for b in range(B):
                    dve.wait_ge(silu0_done, B * e + b + 1)
                    nc.vector.scalar_tensor_tensor(out=h0[:, par, b, :], in0=ps[1 + 2 * par + b][:, D:2 * D],
                                                   scalar=sel0[:, b, column(e)], in1=sg0[:, par, b, :],
                                                   op0=ALU.mult, op1=ALU.mult).then_inc(h0_ready, 1)

            def turned0(e):
                dve.wait_ge(hT0_ready, e + 1)
                nc.vector.tensor_tensor(hT0L[:].rearrange("p k b t -> p (k b t)"), ps[5][:],
                                        hT0H[:].rearrange("p k b t -> p (k b t)").bitcast(F32),
                                        ALU.subtract).then_inc(hT0L_ready, 1)

            def step0(e, par, downs=True):
                turned0(e)
                products0(e + 1, 1 - par)
                if downs:
                    down_low0(e + 2, par)

            products0(0, 0)
            step0(0, 0)
            with dve.Fori(0, E0 // 2 - 1) as i:
                step0(2 * i + 1, 1)
                step0(2 * i + 2, 0)
            step0(E0 - 1, 1, downs=False)
            turned0(E0)
            add_to_x(5)

            row_stats_eps(x)
            nc.vector.tensor_tensor(xn[:], x[:], rows[:, 2:3, :].broadcast_to([P, B, D]), ALU.add)
            dve.wait_ge(rstd_ready, 5)
            for b in range(B):
                c = dve_step(nc.vector.scalar_tensor_tensor(out=yt[:, b, :], in0=x[:, b, :], scalar=rstd[:, b:b + 1],
                                                            in1=summ[:, b, :], op0=ALU.mult, op1=ALU.add))
            dve.wait_ge(dve_step.sem, c)
            row_stats_eps(yt)
            for b in range(B):
                c = dve_step(nc.vector.scalar_tensor_tensor(out=hx[:, b, :], in0=yt[:, b, :], scalar=mv[:, b, 0:1],
                                                            in1=rows[:, 1, :], op0=ALU.subtract, op1=ALU.mult))
            dve.wait_ge(dve_step.sem, c)
            dve.wait_ge(rstd_ready, 6)
            for b in range(B):
                c = dve_step(nc.vector.scalar_tensor_tensor(out=x[:, b, :], in0=hx[:, b, :], scalar=rstd[:, b:b + 1],
                                                            in1=xn[:, b, :], op0=ALU.mult, op1=ALU.add))
            dve.wait_ge(dve_step.sem, c)

            normalise_x(7, 5)

            def rotate(r, m):
                dve.wait_ge(p5_done, m + 1)
                src = ps[m % 2][:].rearrange("p (h d) -> p h d", h=GH)
                nc.vector.tensor_tensor(rc[:, r % 2], src, cosT.unsqueeze(1).broadcast_to([P, GH, P]), ALU.mult)
                for lo, hi in ((0, P // 2), (P // 2, P)):
                    last = nc.vector.tensor_tensor(rs[:, r % 2, :, lo:hi], src[:, :, P // 2 - lo:P - lo],
                                                   sinT[:, lo:hi].unsqueeze(1).broadcast_to([P, GH, P // 2]), ALU.mult)
                last.then_inc(rope_mul, 1)
                dve.wait_ge(rope_mul, r + 1)
                if r >= 2:
                    dve.wait_ge(t5_done, r - 1)
                nc.vector.tensor_tensor(rope[:, r % 2], rc[:, r % 2], rs[:, r % 2], ALU.add).then_inc(rope_ready, 1)

            for s in range(B * NKV + 2):
                b, c = divmod(s, NKV)
                if s - 2 >= 0:
                    u = s - 2
                    dve.wait_ge(exp5, u + 1)
                    then(nc.vector.reciprocal(sum5[:, 1, u * GH:(u + 1) * GH], sum5[:, 0, u * GH:(u + 1) * GH]))
                    nc.vector.tensor_tensor(P5[:, u % 2], P5[:, u % 2],
                                            sum5[:, 1, u * GH:(u + 1) * GH].unsqueeze(2).broadcast_to([P, GH, P]),
                                            ALU.mult).then_inc(norm5, 1)
                if s < B * NKV:
                    if c == 0:
                        rotate(rope_at(s) - 1, 6 * b)
                    rotate(rope_at(s), 6 * b + 2 + c)
                if 1 <= s <= B * NKV:
                    u = s - 1
                    dve.wait_ge(s5_done, u + 1)
                    then(nc.vector.scalar_tensor_tensor(
                        out=P5[:, u % 2], in0=ps[4][:].rearrange("p (h k) -> p h k", h=GH), scalar=SCALE,
                        in1=causal.unsqueeze(1).broadcast_to([P, GH, P]), op0=ALU.mult, op1=ALU.add))
                    then(nc.vector.reduce_max(nmax5[:, 0, u * GH:(u + 1) * GH], P5[:, u % 2], AX.X))
                    nc.vector.tensor_scalar(nmax5[:, 1, u * GH:(u + 1) * GH], nmax5[:, 0, u * GH:(u + 1) * GH], -1.0, None,
                                            ALU.mult).then_inc(soft5, 1)
            add_to_x(7)

            def down_low(step, par, src, n):
                dve.wait_ge(dnH_ready, step + 1)
                nc.vector.tensor_tensor(dnL[par][:, 0:n], src, dnH[par][:, 0:n].bitcast(F32),
                                        ALU.subtract).then_inc(dnL_ready, 1)

            def split_down(step, c):
                lo, hi = BLOCKS[c]
                down_low(step, (c + 1) % 2, dn1[:, lo:hi], hi - lo)

            normalise_x(8, 6)
            split_tokens(xH, xL, 2)
            down_low(0, 0, dnsh[:], SHW // P)
            split_down(1, 0)
            dve.wait_ge(exp1_done, 1)
            then(nc.vector.tensor_scalar(sc1[:, 0], sc1[:, 0], 1.0, None, ALU.add))
            then(nc.vector.reciprocal(sc1[:, 1], sc1[:, 0]))
            then(nc.vector.tensor_tensor(sc1[:, 2], sc1[:, 1], bias1[:].unsqueeze(1).broadcast_to([P, B, E1]), ALU.add))
            four = sc1[:, 2].rearrange("p b (g f) -> p (b g) f", f=4)
            nc.vector.tensor_tensor(pair1[:, 0], four[:, :, 0:2], four[:, :, 2:4], ALU.max)
            then(nc.vector.tensor_tensor(pair1[:, 1], four[:, :, 0:2], four[:, :, 2:4], ALU.min))
            nc.vector.tensor_tensor(grp1[:, 0], pair1[:, 0, :, 0], pair1[:, 0, :, 1], ALU.max)
            nc.vector.tensor_tensor(grp1[:, 1], pair1[:, 0, :, 0], pair1[:, 0, :, 1], ALU.min)
            then(nc.vector.tensor_tensor(grp1[:, 2], pair1[:, 1, :, 0], pair1[:, 1, :, 1], ALU.max))
            then(nc.vector.tensor_tensor(grp1[:, 1], grp1[:, 1], grp1[:, 2], ALU.max))
            then(nc.vector.tensor_tensor(gsc1[:, :, 0:E1 // 4], grp1[:, 0].rearrange("p (b g) -> p b g", b=B),
                                         grp1[:, 1].rearrange("p (b g) -> p b g", b=B), ALU.add))
            for b in range(B):
                then(nc.vector.max(top1[:, b, :], gsc1[:, b, :]))
                then(nc.vector.memset(top1[:, b, 4:8], -BIG))
                c = dve_step(nc.vector.match_replace(gre1[:, b, :], top1[:, b, :], gsc1[:, b, :], -BIG))
            dve.wait_ge(dve_step.sem, c)
            then(nc.vector.tensor_tensor(gsel1[:], gsc1[:, :, 0:E1 // 4], gre1[:, :, 0:E1 // 4], ALU.not_equal))
            then(nc.vector.tensor_scalar(gsel1[:], gsel1[:], BIG, -BIG, ALU.mult, ALU.add))
            then(nc.vector.tensor_tensor(msk1[:, 0].rearrange("p b (g f) -> p (b g) f", f=4), four,
                                         gsel1[:].rearrange("p b g -> p (b g)").unsqueeze(2).broadcast_to([P, B * E1 // 4, 4]),
                                         ALU.add))
            for b in range(B):
                then(nc.vector.max(top1[:, 2 + b, :], msk1[:, 0, b, :]))
                then(nc.vector.memset(top1[:, 2 + b, 6:8], -BIG))
                c = dve_step(nc.vector.match_replace(msk1[:, 1, b, :], top1[:, 2 + b, :], msk1[:, 0, b, :], -BIG))
            dve.wait_ge(dve_step.sem, c)
            then(nc.vector.tensor_tensor(msk1[:, 1], msk1[:, 0], msk1[:, 1], ALU.not_equal))
            nc.vector.tensor_tensor(comb[:], msk1[:, 1], sc1[:, 1], ALU.mult).then_inc(comb_ready, 1)

            def products6(step, e, batches=range(B)):
                for b in batches:
                    dve.wait_ge(silu6_done, B * step + b + 1)
                    if e is None:
                        last = nc.vector.tensor_tensor(h6[:, b, IT * M1 - SHW:IT * M1], ps[2 * b + 1][:, 0:SHW],
                                                       sg6[:, b, :], ALU.mult)
                    else:
                        chunk, first = e
                        for j in range(CH):
                            last = nc.vector.scalar_tensor_tensor(
                                out=h6[:, b, chunk * CW + j * M1:chunk * CW + (j + 1) * M1],
                                in0=ps[2 * b + 1][:, j * M1:(j + 1) * M1], scalar=comb[:, b, column(first + j)],
                                in1=sg6[:, b, j * M1:(j + 1) * M1], op0=ALU.mult, op1=ALU.mult)
                    last.then_inc(h6_ready, 1)

            def turned6(step, n):
                for b in range(B):
                    dve.wait_ge(hTH_ready, B * step + b + 1)
                    nc.vector.tensor_tensor(hTL[:, b, 0:n, :].rearrange("p k t -> p (k t)"), ps[4 + b][:, 0:n * P],
                                            hTH[:, b, 0:n, :].rearrange("p k t -> p (k t)").bitcast(F32),
                                            ALU.subtract).then_inc(hTL_ready, 1)

            def step6(step, n, e, dn_next=None):
                if e:
                    products6(step + 1, e, range(1))
                turned6(step, n)
                if e:
                    products6(step + 1, e, range(1, B))
                if dn_next is not None:
                    split_down(step + 2, dn_next)

            products6(0, None)
            dve.wait_ge(comb_ready, 1)
            step6(0, SHW // P, (0, 0), 1)
            with dve.Fori(0, E1 // IT - 1) as i:
                for c in range(NCH):
                    step6(NCH * i + c + 1, BLOCKS[c][1] - BLOCKS[c][0], ((c + 1) % NCH, IT * i + CH * (c + 1)),
                          (c + 2) % NCH)
            for c in range(NCH):
                step6(E1 // CH - NCH + c + 1, BLOCKS[c][1] - BLOCKS[c][0],
                      (c + 1, E1 - IT + CH * (c + 1)) if c < NCH - 1 else None, c + 2 if c + 2 < NCH else None)
            add_to_x(9)

        @block.tensor
        def _(pe):
            mm, tr = nc.tensor.matmul, nc.tensor.transpose

            def hold_clock(bank, count):
                for _ in range(count):
                    mm(ps[bank][:, 0:P], ones[:], ones[:], start=True, stop=True)

            pe.wait_ge(consts_set, 1)
            hold_clock(7, 12)
            def transpose_tokens(dst):
                for k in range(KD):
                    for b in range(B):
                        last = tr(dst[:, (k * B + b) * P:(k * B + b + 1) * P], xn[:, b, k * P:(k + 1) * P], ident)
                last.then_inc(xT_done, 1)

            pe.wait_ge(in_consts, 16)
            pe.wait_ge(xn_ready, 1)
            transpose_tokens(SC[0])
            pe.wait_ge(xT_ready, 1)
            for u in range(B * NKV):
                pe.wait_ge(in_wq[u // B], 16)
                if u >= 2:
                    pe.wait_ge(q_biased, u - 1)
                for k in range(KD):
                    last = mm(SC[1 + u % 2][:], xnT[:, k, u % B * P:(u % B + 1) * P],
                              wq[:, k, u // B * GW:(u // B + 1) * GW], start=(k == 0), stop=(k == KD - 1))
                last.then_inc(q_done, 1)

            def key_chunks(g, b, kvh, chunks, first=False):
                pe.wait_ge(in_wkv, 16 * (kvh + 1))
                for t in chunks:
                    if isinstance(g, int) and g < B:
                        pe.wait_ge(in_ctx[b][t], 16)
                    if t >= 2:
                        pe.wait_ge(k_ready, NC * g + t - 1)
                    elif not first:
                        pe.wait_ge(v_ready, NC * (g - 1) + t + 3)
                    for k in range(KD):
                        last = mm(PR[t % 2][:], wkv[:, k * 2 * P:k * 2 * P + P], ctxT[:, b, k, t * GW:(t + 1) * GW],
                                  start=(k == 0), stop=(k == KD - 1))
                    last.then_inc(k_done, 1)

            def value_chunks(g, b, first=False, between=None):
                if not (isinstance(g, int) and g < B):
                    pe.wait_ge(rden_ready, g - 1)
                for t in range(NC):
                    if between and t in between:
                        between[t]()
                    if t < 2:
                        pe.wait_ge(k_ready, NC * g + t + 3)
                    else:
                        pe.wait_ge(v_ready, NC * g + t - 1)
                    for j in range(4 * t, 4 * t + 4):
                        for k in range(KD):
                            last = mm(PR[t % 2][:, (j - 4 * t) * P:(j - 4 * t + 1) * P], ctxT[:, b, k, j * P:(j + 1) * P],
                                      wkv[:, k * 2 * P + P:(k + 1) * 2 * P], start=(k == 0), stop=(k == KD - 1))
                        if j == 4 * t + 3:
                            last.then_inc(v_done, 1)
                        last = mm(MISC[:, j:j + 1], K2[:, j * P:(j + 1) * P], ones[:, 0:1], start=True, stop=True)
                last.then_inc(ksum_done, 1)

            def score_tile(g, b, kvh, j):
                if j == 0:
                    pe.wait_ge(kl_ready, NC * (g + 1))
                if j >= 3:
                    pe.wait_ge(s_ready, g * NT + j - 2)
                keys = slice(j * P, (j + 1) * P)
                mm(SC[j % 3][:], KH[b][:, keys], QH[:, b, kvh, :], start=True, stop=False)
                mm(SC[j % 3][:], KH[b][:, keys], QL[:, b, kvh, :], start=False, stop=False)
                mm(SC[j % 3][:], KL[b][:, keys], QH[:, b, kvh, :], start=False, stop=True).then_inc(s_done, 1)

            def value_tile(g, b, j):
                pe.wait_ge(exp_done, g * NT + j + 1)
                if j == 0 and (not isinstance(g, int) or g):
                    pe.wait_ge(o_scaled, g)
                last = mm(PO[:], V[b][:, j, :], S[:, j, :], start=(j == 0), stop=(j == NT - 1))
                if j == NT - 1:
                    last.then_inc(pv_done, 1)

            def transpose_maxima(g, b):
                pe.wait_ge(max_step, (g + 1) * (NT - 1))
                for h in range(GH):
                    last = tr(SC[2][:, h * P:(h + 1) * P], M[:, h * P:(h + 1) * P], ident)
                last.then_inc(maxT_done, 1)

            def spread_maxima(g):
                pe.wait_ge(max_ready, g + 1)
                for h in range(GH):
                    last = mm(MB[:, h * P:(h + 1) * P], mq[:, h:h + 1].broadcast_to([P, P]), ident, start=True, stop=True)
                last.then_inc(mb_done, 1)

            def denominators(g, b):
                pe.wait_ge(onesR_set, 1)
                pe.wait_ge(kvar_ready, min(g + 2, NG) if isinstance(g, int) else g + 2)
                pe.wait_ge(psumsL_ready, g + 1)
                mm(MISC[:], onesR[:], psumsH[:], start=True, stop=False)
                mm(MISC[:], onesR[:], psumsL[b][:], start=False, stop=True).then_inc(den_done, 1)

            def half(n, b, kvh, scores=True, pv=True, keys=True, fill=None):
                for j in range(NT):
                    if pv and scores and j == NT - 2:
                        denominators(n, b)
                    if pv:
                        value_tile(n, b, j)
                    if scores:
                        score_tile(n + 1, 1 - b, kvh + b, j)
                    if keys and not pv and j == 3:
                        pe.wait_ge(ql_ready, B * NKV)
                    if keys and not pv and j % 4 == 3:
                        key_chunks(n + 2, b, kvh + 1, [j // 4])
                if keys and pv:
                    key_chunks(n + 2, b, kvh + 1, range(0, 2))
                if fill:
                    fill(1)
                if not pv:
                    value_chunks(n + 2, b, between={1: lambda: (transpose_maxima(n + 1, 1 - b), spread_maxima(n + 1))})
                    return
                if scores:
                    transpose_maxima(n + 1, 1 - b)
                if keys:
                    key_chunks(n + 2, b, kvh + 1, range(2, NC))
                if fill:
                    fill(0)
                if scores:
                    spread_maxima(n + 1)
                if keys:
                    value_chunks(n + 2, b)

            key_chunks(0, 0, 0, range(NC), first=True)
            def turn_queries(units):
                for u in units:
                    if u == 5:
                        pe.wait_ge(v_ready, NC)
                    pe.wait_ge(q_scaled[u // NKV], 1)
                    if u == len(QR) - 1:
                        pe.wait_ge(ql_ready, 1)
                    for h in range(GH):
                        last = tr(QR[u][:, h * P:(h + 1) * P], q_tok[:, u // NKV, u % NKV * GH + h, :], ident)
                    last.then_inc(qT_done, 1)

            value_chunks(0, 0, first=True, between={2: lambda: turn_queries(range(5))})
            turn_queries(range(5, B * NKV))
            pe.wait_ge(ql_ready, 5)
            half(-1, 1, -1, pv=False)
            with pe.Fori(0, NKV - 1) as i:
                half(2 * i, 0, i)
                half(2 * i + 1, 1, i)
            def project_heads(b, heads):
                for h in heads:
                    last = mm(ps[b][:, 0:D], OT[:, b, h // GH, h % GH * P:(h % GH + 1) * P], wo[:, h, :],
                              start=(h == 0), stop=(h == NH - 1), skip_group_check=True)
                return last

            def first_heads(b):
                pe.wait_ge(in_wo, 16)
                pe.wait_ge(o_ready, NG - 2)
                pe.wait_ge(s_ready, NG * NT - 2 + 2 * (1 - b))
                project_heads(b, range(0, NH // 2))

            half(NG - 2, 0, NKV - 1, keys=False, fill=first_heads)
            half(NG - 1, 1, NKV - 1, scores=False, keys=False)
            pe.wait_ge(last_sum, 1)
            mm(MISC[:], ones[:], psums[1][:], start=True, stop=True).then_inc(den_done, 1)
            for b in range(B):
                project_heads(b, range(NH // 2, NH - GH))
            pe.wait_ge(o_ready, NG - 1)
            project_heads(0, range(NH - GH, NH)).then_inc(proj_done, 1)
            pe.wait_ge(o_ready, NG)
            project_heads(1, range(NH - GH, NH)).then_inc(proj_done, 1)

            def turn(src, n, pause=0):
                hold_clock(3, pause)
                pe.wait_ge(xn_ready, n)
                for k in range(KD):
                    for b in range(B):
                        last = tr(ps[2][:, (k * B + b) * P:(k * B + b + 1) * P], src[:, b, k * P:(k + 1) * P], ident)
                last.then_inc(xT_done, 1)
                pe.wait_ge(xT_ready, n)

            def over_tokens(dst, b, weights):
                for k in range(KD):
                    last = mm(dst, xnT[:, k, b * P:(b + 1) * P], weights[:, k, :], start=(k == 0), stop=(k == KD - 1))
                return last

            turn(hx, 2, PAUSES[0])
            pe.wait_ge(in_w2, 32)
            for b in range(B):
                over_tokens(ps[b][:], b, wqkv[:, :, 0:2 * D]).then_inc(qkv_done, 1)
                over_tokens(ps[3 + b][:, 0:D], b, wqkv[:, :, 2 * D:3 * D]).then_inc(qkv_done, 1)
            pe.wait_ge(in_lin, 32)
            pe.wait_ge(csum_ready, B * KD)
            for m in range(KD):
                for k in range(KD):
                    last = mm(ps[7][:, m * B:(m + 1) * B], win[:, k, m * P:(m + 1) * P], csum[:, k, :],
                              start=(k == 0), stop=(k == KD - 1))
            last.then_inc(lin_done, 1)
            hold_clock(5, PAUSES[1])
            for b in range(B):
                pe.wait_ge(wv_ready, b + 1)
                mm(ps[5 + b][:], tri, ww[:, b, :], start=True, stop=True).then_inc(cum_done, 1)
            pe.wait_ge(lin_ready, 1)
            for b in range(B):
                for k in range(KD):
                    last = mm(ps[7][:, b * D:(b + 1) * D], lin[:, 2, k, b:b + 1].broadcast_to([P, P]), wlin[:, k, :],
                              start=(k == 0), stop=(k == KD - 1))
            last.then_inc(lin_done, 1)
            turn(yt, 3, PAUSES[2])
            pe.wait_ge(in_wsw, 16)

            def swiglu_out(f):
                pe.wait_ge(sw_ready, f + 1)
                for b in range(B):
                    last = mm(ps[5 + b][:, 0:D], hsw[:, f, b * P:(b + 1) * P], wout[:, f, :],
                              start=(f == 0), stop=(f == FB - 1))
                    if f == FB - 1:
                        last.then_inc(proj_done, 1)

            for f in range(FB):
                if f >= 4:
                    pe.wait_ge(sw_ready, f - 3)
                for i in range(2):
                    for k in range(KD):
                        last = mm(ps[SW[f % 4]][:, i * D:(i + 1) * D], wsw[:, k, i * FF + f * P:i * FF + (f + 1) * P],
                                  xnT[:, k, :], start=(k == 0), stop=(k == KD - 1))
                last.then_inc(sw_done, 1)
                if f >= 2:
                    swiglu_out(f - 2)
            swiglu_out(FB - 2)
            swiglu_out(FB - 1)

            turn(xn, 4, PAUSES[3])
            pe.wait_ge(in_rows, 64)
            for b in range(B):
                last = over_tokens(ps[0][:, b * E0:(b + 1) * E0], b, router0)
            last.then_inc(r0_done, 1)
            def product3(dst, pairs, start, stop):
                for k, (lH, lL, rH, rL) in enumerate(pairs):
                    mm(dst, lH, rH, start=(start and k == 0), stop=False, skip_group_check=True)
                    mm(dst, lH, rL, start=False, stop=False, skip_group_check=True)
                    last = mm(dst, lL, rH, start=False, stop=(stop and k == len(pairs) - 1), skip_group_check=True)
                return last

            def gate_up0(e, par):
                pe.wait_ge(w0L_ready, e + 1)
                for b in range(B):
                    tokens = slice(b * P, (b + 1) * P)
                    product3(ps[1 + 2 * par + b][:],
                             [(x0H[:, k, tokens], x0L[:, k, tokens], w0H[par][:, k], w0L[par][:, k])
                              for k in range(KD)], True, True).then_inc(gu0_done, 1)

            def step0(e, par, first=False, more=True):
                pe.wait_ge(h0_ready, B * (e + 1))
                for k in range(KD):
                    for b in range(B):
                        last = tr(ps[5][:, (k * B + b) * P:(k * B + b + 1) * P], h0[:, par, b, k * P:(k + 1) * P], ident)
                last.then_inc(t0_done, 1)
                if more:
                    gate_up0(e + 1, 1 - par)
                pe.wait_ge(hT0L_ready, e + 1)
                pe.wait_ge(d0L_ready, e + 1)
                for b in range(B):
                    last = product3(ps[6 + b][:, 0:D], [(hT0H[:, k, b], hT0L[:, k, b], d0H[par][:, k], d0L[par][:, k])
                                                        for k in range(KD)], first, not more)
                    if not more:
                        last.then_inc(proj_done, 1)
                if more:
                    last.then_inc(down0_done, 1)

            pe.wait_ge(xL_ready, 1)
            gate_up0(0, 0)
            step0(0, 0, first=True)
            with pe.Fori(0, 3) as i:
                step0(2 * i + 1, 1)
                step0(2 * i + 2, 0)
            step0(E0 - 1, 1)
            step0(E0, 0, more=False)

            turn(xn, 5, PAUSES[4])
            pe.wait_ge(in_kv5, 16)

            def project5(m, weights):
                if m >= 2:
                    b, c = divmod(m - 2, 6)
                    if c == 1:
                        pe.wait_ge(v5_ready, b + 1)
                    else:
                        pe.wait_ge(rope_mul, b * (NKV + 1) + (c if c == 0 else c - 1) + 1)
                over_tokens(ps[m % 2][:], m // 6, weights).then_inc(p5_done, 1)

            def turn5(r):
                pe.wait_ge(rope_ready, r + 1)
                if r:
                    pe.wait_ge(t5_ready, r)
                for h in range(GH):
                    last = tr(ps[2][:, h * P:(h + 1) * P], rope[:, r % 2, h, :], ident)
                last.then_inc(t5_done, 1)

            for s in range(B * NKV + 3):
                b, c = divmod(s, NKV)
                if s < B * NKV:
                    if c == 0:
                        project5(6 * b, wkv5[:, :, 0:GW])
                        project5(6 * b + 1, wkv5[:, :, GW:2 * GW])
                    if s == 0:
                        pe.wait_ge(in_w5, 32)
                    project5(6 * b + 2 + c, wq5[:, :, c * GW:(c + 1) * GW])
                u = s - 1
                if 0 <= u < B * NKV:
                    if u % NKV == 0:
                        turn5(rope_at(u) - 1)
                    turn5(rope_at(u))
                u = s - 3
                if 0 <= u:
                    pe.wait_ge(o5_ready, u + 1)
                    for h in range(GH):
                        last = mm(ps[6 + u // NKV][:, 0:D], OT5[:, h, :], wo5[:, u % NKV * GH + h, :],
                                  start=(u % NKV == 0 and h == 0), stop=(u % NKV == NKV - 1 and h == GH - 1))
                    if u % NKV == NKV - 1:
                        last.then_inc(proj_done, 1)
                u = s - 2
                if 0 <= u < B * NKV:
                    pe.wait_ge(norm5, u + 1)
                    if u:
                        pe.wait_ge(pT5_ready, u)
                    for h in range(GH):
                        last = tr(ps[3][:, h * P:(h + 1) * P], P5[:, u % 2, h, :], ident)
                    last.then_inc(pT5_done, 1)
                u = s - 1
                if 0 <= u < B * NKV:
                    pe.wait_ge(t5_ready, rope_at(u) + 1)
                    if u:
                        pe.wait_ge(soft5, u)
                    for h in range(GH):
                        last = mm(ps[4][:, h * P:(h + 1) * P], QT5[u % 2][:, h, :], KT5[:, u // NKV, u % NKV, :],
                                  start=True, stop=True)
                    last.then_inc(s5_done, 1)
                u = s - 2
                if 0 <= u < B * NKV:
                    pe.wait_ge(pT5_ready, u + 1)
                    pe.wait_ge(v5_ready, u // NKV + 1)
                    if u:
                        pe.wait_ge(o5_ready, u)
                    mm(ps[5][:], V5[:, u // NKV, u % NKV, :], PT5[:].rearrange("p h t -> p (h t)"), start=True,
                       stop=True).then_inc(o5_done, 1)

            turn(xn, 6, PAUSES[5])
            for b in range(B):
                last = over_tokens(ps[4][:, b * E1:(b + 1) * E1], b, router1)
            last.then_inc(r1_done, 1)

            def gate_up6(step, b, par, width, first=False):
                if b == 0:
                    pe.wait_ge(guL_ready, step + 1)
                if not first:
                    pe.wait_ge(h6_ready, B * (step - 1) + b + 1)
                tokens = slice(b * P, (b + 1) * P)
                for i in range(2):
                    part = slice(i * width, (i + 1) * width)
                    last = product3(ps[2 * b + i][:, 0:width],
                                    [(xH[:, k, tokens], xL[:, k, tokens], guH[par][:, k, part], guL[par][:, k, part])
                                     for k in range(KD)], True, True)
                last.then_inc(gu6_done, 1)

            def step6(step, par, blocks, more=True, first=False):
                if more:
                    gate_up6(step + 1, 0, 1 - par, CW)
                pe.wait_ge(h6_ready, B * (step + 1))
                n = len(blocks)
                for b in range(B):
                    for k, blk in enumerate(blocks):
                        last = tr(ps[4 + b][:, k * P:(k + 1) * P], h6[:, b, blk * P:(blk + 1) * P], ident)
                    last.then_inc(t6_done, 1)
                if more:
                    gate_up6(step + 1, 1, 1 - par, CW)
                pe.wait_ge(dnL_ready, step + 1)
                for b in range(B):
                    pe.wait_ge(hTL_ready, B * step + b + 1)
                    last = product3(ps[6 + b][:, 0:D], [(hTH[:, b, k], hTL[:, b, k], dnH[par][:, k], dnL[par][:, k])
                                                        for k in range(n)], first, not more)
                    if not more:
                        last.then_inc(proj_done, 1)
                if more:
                    last.then_inc(d6_done, 1)

            pe.wait_ge(xL_ready, 2)
            for b in range(B):
                gate_up6(0, b, 0, SHW, first=True)
            pe.wait_ge(exp1_done, 1)
            step6(0, 0, range(NB - SHW // P, NB), first=True)
            with pe.Fori(0, E1 // IT - 1) as i:
                for c in range(NCH):
                    step6(NCH * i + c + 1, (c + 1) % 2, range(*BLOCKS[c]))
            for c in range(NCH):
                step6(E1 // CH - NCH + c + 1, (c + 1) % 2, range(*BLOCKS[c]), more=c < NCH - 1)


def _blocks(w):
    k, n = w.shape
    return w.reshape(k // P, P, n).transpose(1, 0, 2)


def _constants():
    import numpy as np
    i = np.arange(P)
    ident = np.eye(P, dtype=np.float32)
    tri = (i[:, None] <= i[None, :]).astype(np.float32)
    causal = np.where(i[None, :] <= i[:, None], 0.0, -1e30).astype(np.float32)
    fraction = np.arange(0, P, 2, dtype=np.float32) / np.float32(P)
    angle = i[:, None].astype(np.float32) / (np.float32(10000.0) ** fraction)[None, :]
    cos, sin = np.cos(angle), np.sin(angle)
    return np.stack([ident, tri, causal, np.concatenate([cos, cos], 1), np.concatenate([-sin, sin], 1)], 1)


def _layout(i):
    import numpy as np
    c = lambda v, *s: np.ascontiguousarray(v).reshape(*s)
    wk = _blocks(i["L0_xattn_Wk"]).reshape(P, KD, NKV, P)
    wv = _blocks(i["L0_xattn_Wv"]).reshape(P, KD, NKV, P)
    wkv = np.stack([wk, wv], 3).transpose(0, 2, 1, 3, 4).reshape(P, NKV, KD * 2 * P)
    bk = i["L0_xattn_bk"].reshape(NKV, P).T[:, :, None]
    zeros = np.zeros((P, 2), np.float32)
    decay = np.broadcast_to(i["L1_xattn_decay"].reshape(1, 1), (P, 1))
    b_in = i["L1_xattn_b_in"].reshape(KD, P).T
    experts0 = [(i["L0_ffn_shared_gate_w"], i["L0_ffn_shared_up_w"], i["L0_ffn_shared_down_w"])]
    experts0 += [(i["L0_ffn_gate_w"][e], i["L0_ffn_up_w"][e], i["L0_ffn_down_w"][e]) for e in range(E0)]
    gu1 = [np.concatenate([_blocks(np.concatenate(list(i[n][CH * c:CH * c + CH]), 1))
                           for n in ("L1_ffn_gate_w", "L1_ffn_up_w")], 2).reshape(P, -1) for c in range(E1 // CH)]
    pad = lambda w: np.pad(w, ((0, 0), (0, SHW - w.shape[1])))
    return {
        "x": c(i["x"].transpose(1, 0, 2), P, B * D),
        "consts": c(_constants(), P, 5 * P),
        "ctxT": c(i["ctx_2048"].transpose(2, 0, 1).reshape(KD, P, B, SE).transpose(1, 2, 0, 3), P, B, KD, SE),
        "maskT": c(i["mask_1xSxS2_ff0"][0].T.reshape(NT, P, P).transpose(1, 0, 2), P, NT * P),
        "wq": c(_blocks(i["L0_xattn_Wq"]), P, KD, NH * P),
        "bq": c(i["L0_xattn_bq"], 1, NH * P),
        "wkv": c(np.concatenate([wkv, bk], 2), P, NKV, KD * 2 * P + 1),
        "bv": c(i["L0_xattn_bv"].reshape(NKV, P).T, P, NKV),
        "wo": c(_blocks(i["L0_xattn_Wo"]), P, NH * D),
        "cols": c(np.concatenate([i["L0_xattn_qn_w"][:, None], i["L0_xattn_kn_w"][:, None], b_in, decay, zeros,
                                  zeros[:, :1]], 1), P, 8),
        "wqkv": c(_blocks(i["L0_attn_w_qkv"].T), P, KD * 3 * D),
        "wsw": c(_blocks(i["L0_attn_w_swiglu"].T), P, KD * 2 * FF),
        "wout": c(_blocks(i["L0_attn_w_out"].T), P, FB * D),
        "w0": c(np.stack([_blocks(np.concatenate([g, u], 1)) for g, u, _ in experts0], 1), P, (E0 + 1) * KD * 2 * D),
        "d0": c(np.stack([_blocks(d) for _, _, d in experts0], 1), P, (E0 + 1) * KD * D),
        "router0": c(_blocks(i["L0_ffn_router_w"]), P, KD * E0),
        "win": c(_blocks(i["L1_xattn_W_in"].T), P, KD * D),
        "wlin": c(_blocks(i["L1_xattn_W_out"].T), P, KD * D),
        "rows": c(np.concatenate([i["L1_xattn_b_out"], i["L1_xattn_gamma"], i["L1_xattn_beta"]]), 1, 3 * D),
        "wq5": c(_blocks(i["L1_attn_q_kernel"]), P, KD * NH * P),
        "wkv5": c(_blocks(np.concatenate([i["L1_attn_k_kernel"], i["L1_attn_v_kernel"]], 1)), P, KD * 2 * NKV * P),
        "wo5": c(_blocks(i["L1_attn_out_kernel"]), P, NH * D),
        "router1": c(_blocks(i["L1_ffn_w_router"]), P, KD * E1),
        "bias1": c(i["L1_ffn_corr_bias"], 1, E1),
        "gu1": c(np.stack(gu1, 1), P, E1 // CH, KD * 2 * CW),
        "down1": c(_blocks(i["L1_ffn_down_w"].reshape(E1 * M1, D)), P, E1 * M1 // P, D),
        "gush": c(np.concatenate([_blocks(pad(i["L1_ffn_sh_gate_w"])), _blocks(pad(i["L1_ffn_sh_up_w"]))], 2),
                  P, KD * 2 * SHW),
        "downsh": c(_blocks(np.pad(i["L1_ffn_sh_down_w"], ((0, SHW - 352), (0, 0)))), P, SHW // P * D),
    }


def kernel(**inputs):
    import numpy as np
    import concourse.bacc as bacc
    from concourse.bass_utils import run_bass_kernel_spmd

    arrays = {f"in_{n}": v for n, v in _layout({k: np.asarray(v) for k, v in inputs.items()}).items()}
    nc = bacc.Bacc("TRN2", target_bir_lowering=False, num_devices=1)
    aps = {n[3:]: nc.dram_tensor(n, v.shape, mybir.dt.from_np(v.dtype), kind="ExternalInput").ap()
           for n, v in arrays.items()}
    out = nc.dram_tensor("out_x", (P, B * D), F32, kind="ExternalOutput").ap()
    perceiver(nc, aps, out)
    r = run_bass_kernel_spmd(nc, [arrays], core_ids=[0])
    return r.results[0]["out_x"].reshape(P, B, D).transpose(1, 0, 2)
```
